# Optimizing a Trainium2 kernel written in Bass

```python
import numpy as np
import jax
import jax.numpy as jnp

def _softmax(x, axis=-1):
    return jax.nn.softmax(x, axis=axis)

def _gelu(x):
    return jax.nn.gelu(x, approximate=True)

def _silu(x):
    return jax.nn.silu(x)

def _sigmoid(x):
    return jax.nn.sigmoid(x)

def _layernorm(x, axis=-1, eps=1e-05):
    m = jnp.mean(x, axis=axis, keepdims=True)
    v = jnp.var(x, axis=axis, keepdims=True)
    return (x - m) / jnp.sqrt(v + eps)

def _scatter_add(tgt, idx, src, axis=0):
    return tgt.at[idx].add(src)

def _segment_sum(src, seg, n):
    return jax.ops.segment_sum(src, seg, n)
kernel_name = 'mk_adj_preln_d4_adj_r2_1d2a18'

def setup_inputs(seed: int=0):
    np.random.seed(seed)
    _w = jnp.asarray

    def _rec_inputs():
        import jax
        import jax.numpy as jnp
        _gk = jax.random.key(seed)
        x = 7.22e-05 + 1 * jax.random.normal(jax.random.fold_in(_gk, 1), (16, 512, 128), jnp.float32)
        _a = jax.random.bernoulli(jax.random.fold_in(_gk, 2), 0.015625, (512, 512))
        _a = jnp.logical_or(_a, jnp.swapaxes(_a, -1, -2))
        _a = jnp.logical_or(_a, jnp.eye(512, dtype=bool))
        _af = _a.astype(jnp.float32)
        _af = _af * jax.random.uniform(jax.random.fold_in(_gk, 3), (512, 512), jnp.float32, 0.05, 0.000976562)
        adj = _af
        return (x, adj)
    x, adj = _rec_inputs()

    def _L0_gnn_setup():
        import jax, jax.numpy as jnp
        import numpy as np
        N_STEPS = 8
        SPATIAL_SCALE = 1.0
        key = jax.random.key(seed)
        ks = jax.random.split(key, 6)
        B, N, D = (32, 512, 128)
        x = jax.random.normal(ks[0], (B, N, D), dtype=jnp.float32)
        adj_mx = jax.random.uniform(ks[1], (N, N), dtype=jnp.float32) / N
        alpha_train = jnp.ones((N,), dtype=jnp.float32)
        w = jnp.eye(D, dtype=jnp.float32) + 0.01 * jax.random.normal(ks[2], (D, D), dtype=jnp.float32)
        d = jax.random.uniform(ks[3], (D,), dtype=jnp.float32)
        fc_in_w = jax.random.normal(ks[4], (D, D), dtype=jnp.float32) * (1.0 / np.sqrt(D))
        fc_in_b = jnp.zeros((D,), dtype=jnp.float32)
        return {'x': x, 'adj_mx': adj_mx, 'alpha_train': alpha_train, 'w': w, 'd': d, 'fc_in_w': fc_in_w, 'fc_in_b': fc_in_b, 'vt': 0}
    _L0_gnn_all = _L0_gnn_setup()
    _L0_gnn_in = {k: v for k, v in _L0_gnn_all.items() if k in ('alpha_train', 'w', 'd', 'fc_in_w', 'fc_in_b')}
    del _L0_gnn_all

    def _L1_gnn_setup():
        import jax, jax.numpy as jnp
        import numpy as np
        ALPHA = 0.2
        key = jax.random.key(seed)
        k1, k2, k3, k4 = jax.random.split(key, 4)
        B, N, Fin, Fout = (8, 1024, 128, 128)
        h = jax.random.normal(k1, (B, N, Fin), dtype=jnp.float32)
        adj = jax.random.randint(k2, (N, N), 0, 2).astype(jnp.float32)
        adj = jnp.maximum(adj, jnp.eye(N, dtype=jnp.float32))

        def xavier(k, shape, gain=1.414):
            fan_in, fan_out = (shape[0], shape[1])
            a = gain * np.sqrt(6.0 / (fan_in + fan_out))
            return jax.random.uniform(k, shape, dtype=jnp.float32, minval=-a, maxval=a)
        W = xavier(k3, (Fin, Fout))
        a = xavier(k4, (2 * Fout, 1))
        return {'h': h, 'adj_matrix': adj, 'W': W, 'a': a}
    _L1_gnn_all = _L1_gnn_setup()
    _L1_gnn_in = {k: v for k, v in _L1_gnn_all.items() if k in ('W', 'a')}
    del _L1_gnn_all

    def _L2_gnn_setup():
        import jax, jax.numpy as jnp
        import numpy as np
        BT, N, D, HEADS, E = (512, 64, 128, 4, 256)
        LRELU_SLOPE = 0.2
        EPS = 1e-08
        key = jax.random.key(seed)
        ks = jax.random.split(key, 8)
        d = D
        return {'H': jax.random.normal(ks[0], (BT, N, d), jnp.float32), 'W_lin': jax.random.normal(ks[1], (d, d), jnp.float32) / np.sqrt(d).astype(np.float32), 'W_val': jax.random.normal(ks[2], (d, d), jnp.float32) / np.sqrt(d).astype(np.float32), 'a': jax.random.normal(ks[3], (HEADS, d // HEADS), jnp.float32), 'W_out': jax.random.normal(ks[4], (d, d), jnp.float32) / np.sqrt(d).astype(np.float32), 'A0': jax.random.uniform(ks[5], (N, N), jnp.float32), 'src': jax.random.randint(ks[6], (E,), 0, N, jnp.int32), 'dst': jax.random.randint(ks[7], (E,), 0, N, jnp.int32)}
    _L2_gnn_all = _L2_gnn_setup()
    _L2_gnn_in = {k: v for k, v in _L2_gnn_all.items() if k in ('W_lin', 'W_val', 'a', 'W_out', 'src', 'dst')}
    del _L2_gnn_all

    def _L3_gnn_setup():
        import jax, jax.numpy as jnp
        import numpy as np
        EPS_LN = 1e-05

        def _layernorm(x, g, b):
            mu = x.mean(-1, keepdims=True)
            var = ((x - mu) ** 2).mean(-1, keepdims=True)
            return (x - mu) / jnp.sqrt(var + EPS_LN) * g + b
        key = jax.random.key(seed)
        B, N, D, H = (4, 1024, 128, 4)
        hid = int(D * 2.0)
        ks = jax.random.split(key, 12)
        x = jax.random.normal(ks[0], (B, N, D), jnp.float32)
        Au = jax.random.uniform(ks[1], (N, N)) < 0.004
        A = jnp.logical_or(Au, Au.T)
        A = A.at[jnp.arange(N), jnp.arange(N)].set(False)
        Af = A.astype(jnp.float32)
        deg = Af.sum(axis=1)
        L = jnp.diag(deg) - Af
        adjacency = Af + jnp.eye(N, dtype=jnp.float32)
        s = lambda k, sh, f: jax.random.normal(k, sh, jnp.float32) * f
        sc = 1.0 / np.sqrt(D)
        Wc = s(ks[2], (D, D), sc)
        bc = jnp.zeros((D,), jnp.float32)
        Wq = s(ks[3], (D, D), sc)
        Wk = s(ks[4], (D, D), sc)
        Wv = s(ks[5], (D, D), sc)
        Wo = s(ks[6], (D, D), sc)
        bo = jnp.zeros((D,), jnp.float32)
        W1 = s(ks[7], (D, hid), sc)
        b1 = jnp.zeros((hid,), jnp.float32)
        W2 = s(ks[8], (hid, D), 1.0 / np.sqrt(hid))
        b2 = jnp.zeros((D,), jnp.float32)
        g1 = jnp.ones((D,), jnp.float32)
        be1 = jnp.zeros((D,), jnp.float32)
        g2 = jnp.ones((D,), jnp.float32)
        be2 = jnp.zeros((D,), jnp.float32)
        g3 = jnp.ones((D,), jnp.float32)
        be3 = jnp.zeros((D,), jnp.float32)
        return dict(x=x, L=L, adjacency=adjacency, Wc=Wc, bc=bc, g1=g1, be1=be1, Wq=Wq, Wk=Wk, Wv=Wv, Wo=Wo, bo=bo, g2=g2, be2=be2, W1=W1, b1=b1, W2=W2, b2=b2, g3=g3, be3=be3)
    _L3_gnn_all = _L3_gnn_setup()
    _L3_gnn_in = {k: v for k, v in _L3_gnn_all.items() if k in ('Wc', 'bc', 'g1', 'be1', 'Wq', 'Wk', 'Wv', 'Wo', 'bo', 'g2', 'be2', 'W1', 'b1', 'W2', 'b2', 'g3', 'be3')}
    del _L3_gnn_all
    return {'x': x, 'adj': adj, 'L0_gnn_alpha_train': _L0_gnn_in['alpha_train'], 'L0_gnn_w': _L0_gnn_in['w'], 'L0_gnn_d': _L0_gnn_in['d'], 'L0_gnn_fc_in_w': _L0_gnn_in['fc_in_w'], 'L0_gnn_fc_in_b': _L0_gnn_in['fc_in_b'], 'L1_gnn_W': _L1_gnn_in['W'], 'L1_gnn_a': _L1_gnn_in['a'], 'L2_gnn_W_lin': _L2_gnn_in['W_lin'], 'L2_gnn_W_val': _L2_gnn_in['W_val'], 'L2_gnn_a': _L2_gnn_in['a'], 'L2_gnn_W_out': _L2_gnn_in['W_out'], 'L2_gnn_src': _L2_gnn_in['src'], 'L2_gnn_dst': _L2_gnn_in['dst'], 'L3_gnn_Wc': _L3_gnn_in['Wc'], 'L3_gnn_bc': _L3_gnn_in['bc'], 'L3_gnn_g1': _L3_gnn_in['g1'], 'L3_gnn_be1': _L3_gnn_in['be1'], 'L3_gnn_Wq': _L3_gnn_in['Wq'], 'L3_gnn_Wk': _L3_gnn_in['Wk'], 'L3_gnn_Wv': _L3_gnn_in['Wv'], 'L3_gnn_Wo': _L3_gnn_in['Wo'], 'L3_gnn_bo': _L3_gnn_in['bo'], 'L3_gnn_g2': _L3_gnn_in['g2'], 'L3_gnn_be2': _L3_gnn_in['be2'], 'L3_gnn_W1': _L3_gnn_in['W1'], 'L3_gnn_b1': _L3_gnn_in['b1'], 'L3_gnn_W2': _L3_gnn_in['W2'], 'L3_gnn_b2': _L3_gnn_in['b2'], 'L3_gnn_g3': _L3_gnn_in['g3'], 'L3_gnn_be3': _L3_gnn_in['be3']}

def reference(x, adj, L0_gnn_alpha_train, L0_gnn_w, L0_gnn_d, L0_gnn_fc_in_w, L0_gnn_fc_in_b, L1_gnn_W, L1_gnn_a, L2_gnn_W_lin, L2_gnn_W_val, L2_gnn_a, L2_gnn_W_out, L2_gnn_src, L2_gnn_dst, L3_gnn_Wc, L3_gnn_bc, L3_gnn_g1, L3_gnn_be1, L3_gnn_Wq, L3_gnn_Wk, L3_gnn_Wv, L3_gnn_Wo, L3_gnn_bo, L3_gnn_g2, L3_gnn_be2, L3_gnn_W1, L3_gnn_b1, L3_gnn_W2, L3_gnn_b2, L3_gnn_g3, L3_gnn_be3):
    import jax
    import jax.numpy as jnp

    def _L0_gnn_ref(x, adj_mx, alpha_train, w, d, fc_in_w, fc_in_b, vt):
        import jax, jax.numpy as jnp
        import numpy as np
        N_STEPS = 8
        SPATIAL_SCALE = 1.0
        x0 = jax.lax.stop_gradient(x)
        h = jnp.einsum('bnd,ed->bne', x, fc_in_w) + fc_in_b
        alph = jax.nn.sigmoid(alpha_train)[:, None]
        d_clamped = jnp.clip(d, 0.0, 1.0)
        w_eff = w * d_clamped @ w.T
        dt = jnp.float32(SPATIAL_SCALE / N_STEPS)

        def euler_step(h, _):
            ax = jnp.einsum('nm,bmd->bnd', adj_mx, h)
            f = alph * 0.5 * (ax - h) + h @ w_eff - h + x0
            return (h + dt * f, None)
        h, _ = jax.lax.scan(euler_step, h, None, length=N_STEPS)
        return h

    def _L1_gnn_ref(h, adj_matrix, W, a):
        import jax, jax.numpy as jnp
        import numpy as np
        ALPHA = 0.2
        Fout = W.shape[1]
        Wh = jnp.einsum('bnf,fo->bno', h, W)
        a1, a2 = (a[:Fout, 0], a[Fout:, 0])
        s1 = Wh @ a1
        s2 = Wh @ a2
        e = s1[:, :, None] + s2[:, None, :]
        e = jnp.where(e >= 0, e, ALPHA * e)
        e = jnp.where(adj_matrix[None] == 0, -jnp.inf, e)
        attention = jax.nn.softmax(e, axis=-1)
        h_prime = jnp.einsum('bij,bjo->bio', attention, Wh)
        return h_prime

    def _L2_gnn_ref(H, W_lin, W_val, a, W_out, A0, src, dst):
        import jax, jax.numpy as jnp
        import numpy as np
        BT, N, D, HEADS, E = (512, 64, 128, 4, 256)
        LRELU_SLOPE = 0.2
        EPS = 1e-08
        bt, n, d = H.shape
        h, dh = a.shape
        Xq = (H @ W_lin.T).reshape(bt, n, h, dh)
        Xv = (H @ W_val.T).reshape(bt, n, h, dh)
        Qs = Xq[:, src]
        Kt = Xq[:, dst]
        e = jnp.einsum('behd,hd->beh', jax.nn.leaky_relu(Qs + Kt, LRELU_SLOPE), a)
        e = e + jnp.log(A0[src, dst] + EPS)[None, :, None]
        e_t = e.transpose(1, 0, 2)
        m = jax.ops.segment_max(e_t, src, num_segments=n)
        ex = jnp.exp(e_t - m[src])
        denom = jax.ops.segment_sum(ex, src, num_segments=n)
        attn = ex / denom[src]
        Vt = Xv[:, dst].transpose(1, 0, 2, 3)
        Y = jax.ops.segment_sum(attn[..., None] * Vt, src, num_segments=n)
        Y = Y.transpose(1, 0, 2, 3).reshape(bt, n, d)
        return Y @ W_out.T

    def _L3_gnn_ref(x, L, adjacency, Wc, bc, g1, be1, Wq, Wk, Wv, Wo, bo, g2, be2, W1, b1, W2, b2, g3, be3):
        import jax, jax.numpy as jnp
        import numpy as np
        EPS_LN = 1e-05

        def _layernorm(x, g, b):
            mu = x.mean(-1, keepdims=True)
            var = ((x - mu) ** 2).mean(-1, keepdims=True)
            return (x - mu) / jnp.sqrt(var + EPS_LN) * g + b
        B, N, D = x.shape
        H = 4
        hd = D // H
        eig = jnp.linalg.eigvalsh(L)
        lam_max = eig[-1] + 1e-08
        L_norm = 2.0 * L / lam_max - jnp.eye(N, dtype=L.dtype)
        xp = jnp.einsum('mn,bnf->bmf', L_norm, x)
        h = xp @ Wc + bc
        h = _layernorm(h, g1, be1)
        h = jax.nn.relu(h)
        x1 = h + x
        q = (x1 @ Wq).reshape(B, N, H, hd).transpose(0, 2, 1, 3)
        k = (x1 @ Wk).reshape(B, N, H, hd).transpose(0, 2, 1, 3)
        v = (x1 @ Wv).reshape(B, N, H, hd).transpose(0, 2, 1, 3)
        scores = jnp.einsum('bhnd,bhmd->bhnm', q, k) / np.sqrt(hd).astype(np.float32)
        scores = jnp.where(adjacency[None, None] > 0, scores, jnp.float32(-1000000000.0))
        attn = jax.nn.softmax(scores, axis=-1)
        o = jnp.einsum('bhnm,bhmd->bhnd', attn, v)
        o = o.transpose(0, 2, 1, 3).reshape(B, N, D)
        o = o @ Wo + bo
        x2 = _layernorm(x1 + o, g2, be2)
        m = jax.nn.gelu(x2 @ W1 + b1, approximate=False) @ W2 + b2
        return _layernorm(x2 + m, g3, be3)
    h = jnp.maximum(_layernorm(x, axis=-1), 0.0)
    x = x + _L0_gnn_ref(h, adj, L0_gnn_alpha_train, L0_gnn_w, L0_gnn_d, L0_gnn_fc_in_w, L0_gnn_fc_in_b, 0)
    h = jnp.maximum(_layernorm(x, axis=-1), 0.0)
    x = x + _L1_gnn_ref(h, adj, L1_gnn_W, L1_gnn_a)
    h = jnp.maximum(_layernorm(x, axis=-1), 0.0)
    x = x + _L2_gnn_ref(h, L2_gnn_W_lin, L2_gnn_W_val, L2_gnn_a, L2_gnn_W_out, adj, L2_gnn_src, L2_gnn_dst)
    h = jnp.maximum(_layernorm(x, axis=-1), 0.0)
    x = x + _L3_gnn_ref(h, adj, adj, L3_gnn_Wc, L3_gnn_bc, L3_gnn_g1, L3_gnn_be1, L3_gnn_Wq, L3_gnn_Wk, L3_gnn_Wv, L3_gnn_Wo, L3_gnn_bo, L3_gnn_g2, L3_gnn_be2, L3_gnn_W1, L3_gnn_b1, L3_gnn_W2, L3_gnn_b2, L3_gnn_g3, L3_gnn_be3)
    return x

_drawn_inputs = setup_inputs


def setup_inputs(seed=0):
    import zlib

    import numpy as np

    out = dict(_drawn_inputs(seed))
    spreads = {'L0_gnn_alpha_train': (1.0, 0.6),
     'L0_gnn_fc_in_b': (0.0, 0.1),
     'L3_gnn_bc': (0.0, 0.1),
     'L3_gnn_g1': (1.0, 0.2),
     'L3_gnn_be1': (0.0, 0.1),
     'L3_gnn_bo': (0.0, 0.1),
     'L3_gnn_g2': (1.0, 0.2),
     'L3_gnn_be2': (0.0, 0.1),
     'L3_gnn_b1': (0.0, 0.356),
     'L3_gnn_b2': (0.0, 0.1),
     'L3_gnn_g3': (1.0, 0.2),
     'L3_gnn_be3': (0.0, 0.1)}
    factors = {}
    for name, (base, spread) in spreads.items():
        noise = np.random.default_rng([zlib.crc32(name.encode()), seed]).standard_normal(out[name].shape)
        drawn = base * np.exp(spread * noise) if base else spread * noise
        out[name] = jnp.asarray(drawn.astype(out[name].dtype))
    for name, factor in factors.items():
        out[name] = (out[name] * factor).astype(out[name].dtype)
    return out
```

```python
from contextlib import ExitStack
from math import comb

import concourse.bass as bass
from concourse import mybir

F32 = mybir.dt.float32
R32 = mybir.dt.float32r
I32 = mybir.dt.int32
BF16 = mybir.dt.bfloat16
ALU = mybir.AluOpType
ACT = mybir.ActivationFunctionType
AX = mybir.AxisListType.X

B, N, D = 16, 512, 128
P = 128
NT = N // P
H = 4
HD = D // H
E = 256
ET = E // P
HID = 2 * D
EPS = 1e-5
STEPS = 8
DT = 1.0 / STEPS
HB = B // 2
CB = 4
NC = HB // CB
SQUARINGS = 9
BIG = 1.0e30
HUGE = 3.0e38
QK_SCALE = float(HD) ** -0.5
MASKED = -1.0e9

NAMES = ["x", "adj", "alpha", "w", "d", "fcw", "fcb", "W1g", "ag", "Wlin", "Wval", "aL2", "Wout", "src", "dst",
         "Wc", "bc", "g1", "be1", "Wq", "Wk", "Wv", "Wo", "bo", "g2", "be2", "W1", "b1", "W2", "b2", "g3", "be3"]
ROWS = ["fcb", "bc", "g1", "be1", "bo", "g2", "be2", "b2", "g3", "be3"]


def need(eng, sem, value):
    if isinstance(value, int) and value <= 0:
        return
    eng.wait_ge(sem, value)


class Shared(dict):
    __getattr__ = dict.__getitem__


def build(nc, t_in, out):
    ctx = ExitStack()
    with ctx:
        def sb(name, shape, dt=F32, c=None):
            return (c or ctx).enter_context(nc.sbuf_tensor(name, shape, dt))

        sems, part = {}, ["start"]

        def sem(name):
            if name not in sems:
                sems[name] = nc.alloc_semaphore(f"{name}_{part[0]}")
            return sems[name]

        bank = [ctx.enter_context(nc.psum_tensor(f"bank{i}", [P, 512], F32)) for i in range(8)]
        x1_dram = nc.dram_tensor("x_after_l0", (B, N, D), F32, kind="Internal").ap()
        x3_dram = nc.dram_tensor("x_after_l2", (B, N, D), F32, kind="Internal").ap()
        res_dram = nc.dram_tensor("attn_residual", (B, N, D), F32, kind="Internal").ap()
        v_dram = nc.dram_tensor("values", (B, N, D), F32, kind="Internal").ap()

        def nodes1(ap, b):
            return ap[bass.ds(b, 1)].rearrange("o (t p) d -> p (o t) d", p=P)

        ident = sb("ident", [P, P])
        ones = sb("ones", [P, P])
        adjT_hi = sb("adjT_hi", [P, NT, N], R32)
        adjT_lo = sb("adjT_lo", [P, NT, N], R32)
        mask_gat = sb("mask_gat", [P, NT, N], BF16)
        mask_att = sb("mask_att", [P, NT, N], BF16)
        edge_pick = sb("edge_pick", [P, NT, 2 * E])
        src_rows = sb("src_rows", [P, ET, N])
        seg_bias = sb("seg_bias", [P, ET, E])
        same_src = sb("same_src", [P, ET, E])
        logA = sb("logA", [P, ET])
        W = {n: sb("w_" + n, [P, D]) for n in ["W1g", "Wc", "Wq", "Wk", "Wv", "Wo", "WlinT", "WvalT", "WoutT"]}
        W1 = sb("w_W1", [P, HID])
        W2 = sb("w_W2", [P, 2, D])
        rowv = sb("rowv", [P, len(ROWS), D])
        row = {n: rowv[:, i, :] for i, n in enumerate(ROWS)}
        b1c = sb("b1c", [P, 2])
        neg_half = sb("neg_half", [P, NT])
        gat_a = sb("gat_a", [P, 2])
        gat_a2b = sb("gat_a2b", [P, P])
        head_a = sb("head_a", [P, H, P])
        head_a4 = sb("head_a4", [P, H])
        two_lam = sb("two_lam", [P, 1])

        def row4(name, c=NT):
            return row[name].unsqueeze(1).broadcast_to([P, c, D])

        k = Shared(t_in=t_in, out=out, bank=bank, sem=sem, nodes1=nodes1, row=row, row4=row4, W=W, W1=W1, W2=W2,
                   x1_dram=x1_dram, x3_dram=x3_dram, res_dram=res_dram, v_dram=v_dram, rowv=rowv, b1c=b1c,
                   ident=ident, ones=ones, neg_half=neg_half, adjT_hi=adjT_hi, adjT_lo=adjT_lo, mask_gat=mask_gat,
                   mask_att=mask_att, edge_pick=edge_pick, src_rows=src_rows, seg_bias=seg_bias,
                   same_src=same_src, logA=logA, gat_a=gat_a, gat_a2b=gat_a2b, head_a=head_a, head_a4=head_a4,
                   two_lam=two_lam)

        one = ExitStack()
        with one:
            def s1(name, shape, dt=F32):
                return sb(name, shape, dt, one)

            adj = s1("adj", [P, NT, N])
            PT_hi = s1("PT_hi", [P, NT, N], R32)
            PT_lo = s1("PT_lo", [P, NT, N], R32)
            G_hi = s1("G_hi", [P, STEPS + 1, D], R32)
            G_lo = s1("G_lo", [P, STEPS + 1, D], R32)
            gb = s1("gb", [P, STEPS + 1, D])
            k_one = Shared(k, adj=adj, PT_hi=PT_hi, PT_lo=PT_lo, G_hi=G_hi, G_lo=G_lo, gb=gb)
            build_tables(nc, k_one)
            build_layer0(nc, k_one)

        nc.all_engine_barrier()
        nc.clear_and_free_semaphores(list(sems.values()))
        sems.clear()
        part[0] = "layers"
        nc.all_engine_barrier()

        build_layers(nc, k)


def build_tables(nc, k):
    t_in, bank, sem, W, row = k.t_in, k.bank, k.sem, k.W, k.row
    with ExitStack() as c:
        def sb(name, shape, dt=F32):
            return c.enter_context(nc.sbuf_tensor(name, shape, dt))

        asym = sb("asym", [P, NT, N])
        adjT = sb("adjT", [P, NT, N])
        P_row = sb("P_row", [P, NT, N])
        PT = sb("PT", [P, NT, N])
        S = [sb(f"S{i}", [P, NT, N], R32) for i in range(2)]
        sqr = sb("sqr", [P, NT * N])
        raw = {n: sb("raw_" + n, [P, D]) for n in ["w", "fcw", "Wlin", "Wval", "Wout"]}
        wT = sb("wT", [P, D])
        wTd = sb("wTd", [P, D])
        Rp = sb("Rp", [P, STEPS + 1, D])
        FR = sb("FR", [P, STEPS + 1, D])
        G = sb("G", [P, STEPS + 1, D])
        alpha = sb("alpha_c", [P, NT])
        sg = sb("sg", [P, 4, NT])
        dcol = sb("dcol", [P, 1])
        dclip = sb("dclip", [P, 1])
        fcb_col = sb("fcb_col", [P, 1])
        fcb_b = sb("fcb_b", [P, P])
        a_rows = sb("a_rows", [P, 2, D])
        acol = sb("acol", [P, 1])
        edge_i = sb("edge_i", [P, 2, E], I32)
        edge_f = sb("edge_f", [P, 2, E])
        edge_ci = sb("edge_ci", [P, 2, ET], I32)
        edge_c = sb("edge_c", [P, 2, ET])
        node_row = sb("node_row", [P, N])
        node_col = sb("node_col", [P, NT])
        pick_s = sb("pick_s", [P, NT, E])
        dst_rows = sb("dst_rows", [P, ET, N])
        a0e = sb("a0e", [P, ET])
        logAb = sb("logAb", [P, ET, P])
        junk = sb("junk", [P, ET, N])
        junk2 = sb("junk2", [P, 4, D])
        ssq = sb("ssq", [P, SQUARINGS])
        nrm = sb("nrm", [P, SQUARINGS])
        vec = sb("vec", [P, 3, NT])
        dots = sb("dots", [P, 2])
        lam = sb("lam", [P, 4])
        tiny = sb("tiny", [P, 1])

        loads = [
            (k.adj[:], t_in["adj"].rearrange("(t p) m -> p t m", p=P)),
            (raw["w"][:], t_in["w"]), (raw["fcw"][:], t_in["fcw"]), (raw["Wlin"][:], t_in["Wlin"]),
            (raw["Wval"][:], t_in["Wval"]), (raw["Wout"][:], t_in["Wout"]),
            (W["W1g"][:], t_in["W1g"]), (W["Wc"][:], t_in["Wc"]), (W["Wq"][:], t_in["Wq"]),
            (W["Wk"][:], t_in["Wk"]), (W["Wv"][:], t_in["Wv"]), (W["Wo"][:], t_in["Wo"]),
            (k.W1[:], t_in["W1"]), (k.W2[:], t_in["W2"].rearrange("(k p) d -> p k d", p=P)),
            (alpha[:], t_in["alpha"].rearrange("(t p) -> p t", p=P)),
            (dcol[:], t_in["d"].rearrange("(p o) -> p o", o=1)),
            (fcb_col[:], t_in["fcb"].rearrange("(p o) -> p o", o=1)),
            (k.b1c[:], t_in["b1"].rearrange("(k p) -> p k", p=P)),
            (a_rows[:].rearrange("p a d -> p (a d)"), t_in["ag"].rearrange("f o -> (f o)").partition_broadcast(P)),
            (acol[:], t_in["aL2"].rearrange("h (e o) -> (h e) o", o=1)),
            (edge_i[:, 0, :], t_in["src"].partition_broadcast(P)),
            (edge_i[:, 1, :], t_in["dst"].partition_broadcast(P)),
            (edge_ci[:, 0, :], t_in["src"].rearrange("(t p) -> p t", p=P)),
            (edge_ci[:, 1, :], t_in["dst"].rearrange("(t p) -> p t", p=P)),
        ] + [(k.rowv[:, i, :], t_in[n].partition_broadcast(P)) for i, n in enumerate(ROWS)]
        LOADED = 16 * len(loads)

        block = c.enter_context(nc.Block())

        @block.sync
        def _(sp):
            for dst, src in loads:
                sp.dma_start(dst, src, allow_slow_non_contiguous=True).then_inc(sem("tables_loaded"), 16)

        @block.gpsimd
        def _(pool):
            nc.gpsimd.memset(k.ones[:], 1.0).then_inc(sem("zeroed"), 1)
            nc.gpsimd.memset(k.ident[:], 0.0).then_inc(sem("zeroed"), 1)
            nc.gpsimd.memset(k.head_a[:], 0.0).then_inc(sem("zeroed"), 1)
            nc.gpsimd.memset(k.head_a4[:], 0.0).then_inc(sem("zeroed"), 1)
            nc.gpsimd.memset(tiny[:], 1e-8).then_inc(sem("zeroed"), 1)
            nc.gpsimd.memset(k.neg_half[:], -0.5).then_inc(sem("zeroed"), 1)
            pool.wait_ge(sem("zeroed"), 6)
            nc.gpsimd.affine_select(out=k.ident[:], in_=k.ident[:], compare_op=ALU.not_equal, fill=1.0, base=0,
                                    pattern=[[-1, P]], channel_multiplier=1).then_inc(sem("ident_ready"), 1)
            nc.gpsimd.iota(node_row[:], [[1, N]], base=0, channel_multiplier=0,
                           allow_small_or_imprecise_dtypes=True).then_inc(sem("node_numbers"), 1)
            nc.gpsimd.iota(node_col[:], [[P, NT]], base=0, channel_multiplier=1,
                           allow_small_or_imprecise_dtypes=True).then_inc(sem("node_numbers"), 1)

        @block.scalar
        def _(act):
            act.wait_ge(sem("tables_loaded"), LOADED)
            nc.scalar.activation(sg[:, 0, :], alpha[:], ACT.Exp, scale=-1.0).then_inc(sem("exp_alpha"), 1)
            act.wait_ge(sem("edge_weight"), ET)
            act.wait_ge(sem("zeroed"), 5)
            nc.scalar.activation(k.logA[:], a0e[:], ACT.Ln, bias=tiny[:]).then_inc(sem("log_edge"), 1)
            for q in range(SQUARINGS):
                act.wait_ge(sem("square_scaled"), NT * q + 1)
                need(act, sem("norm_part"), q)
                nc.scalar.activation(sqr[:], S[q % 2][:].rearrange("p t m -> p (t m)").bitcast(F32), ACT.Square,
                                     accum_out=ssq[:, q:q + 1]).then_inc(sem("norm_part"), 1)

        @block.vector
        def _(dve):
            dve.wait_ge(sem("tables_loaded"), LOADED)
            dve.wait_ge(sem("zeroed"), 5)
            dve.wait_ge(sem("exp_alpha"), 1)
            nc.vector.tensor_scalar(sg[:, 1, :], sg[:, 0, :], 1.0, None, ALU.add).then_inc(sem("sig"), 1)
            dve.wait_ge(sem("sig"), 1)
            nc.vector.reciprocal(sg[:, 2, :], sg[:, 1, :]).then_inc(sem("sig"), 1)
            dve.wait_ge(sem("sig"), 2)
            nc.vector.tensor_scalar(sg[:, 3, :], sg[:, 2, :], DT / 2, None, ALU.mult).then_inc(sem("sig"), 1)
            nc.vector.tensor_scalar(dclip[:], dcol[:], 0.0, 1.0, ALU.max, ALU.min).then_inc(sem("dclip"), 1)
            nc.vector.tensor_scalar(fcb_b[:], k.ones[:], fcb_col[:], None, ALU.mult).then_inc(sem("fcb_wide"), 1)
            dve.wait_ge(sem("ident_ready"), 1)
            for t in range(NT):
                nc.vector.tensor_copy(P_row[:, t, :], k.adj[:, t, :]).then_inc(sem("p_row"), 1)
            dve.wait_ge(sem("p_row"), NT)
            for t in range(NT):
                nc.vector.tensor_tensor(P_row[:, t, t * P:(t + 1) * P], k.adj[:, t, t * P:(t + 1) * P], k.ident[:],
                                        ALU.subtract).then_inc(sem("p_row"), 1)
            dve.wait_ge(sem("p_row"), 2 * NT)
            dve.wait_ge(sem("sig"), 3)
            for t in range(NT):
                nc.vector.tensor_scalar(P_row[:, t, :], P_row[:, t, :], sg[:, 3, t:t + 1], None,
                                        ALU.mult).then_inc(sem("p_row"), 1)
            dve.wait_ge(sem("weights_turned"), 4)
            nc.vector.tensor_copy(wT[:], bank[0][:, 0:P]).then_inc(sem("wT"), 1)
            nc.vector.tensor_scalar(wTd[:], bank[0][:, 0:P], dclip[:], None, ALU.mult).then_inc(sem("wT"), 1)
            for i, n in enumerate(["WlinT", "WvalT", "WoutT"]):
                nc.vector.tensor_copy(W[n][:], bank[0][:, (i + 1) * P:(i + 2) * P]).then_inc(sem("wT"), 1)
            dve.wait_ge(sem("fc_turned"), 1)
            nc.vector.tensor_copy(FR[:, 0, :], bank[1][:, 0:P]).then_inc(sem("FR"), 1)
            for s in range(NT):
                dve.wait_ge(sem("adj_turned"), s + 1)
                nc.vector.tensor_copy(adjT[:, s, :], bank[4 + s][:]).then_inc(sem("adjT"), 1)
            for s in range(NT):
                dve.wait_ge(sem("p_turned"), s + 1)
                nc.vector.tensor_copy(PT[:, s, :], bank[4 + s][:]).then_inc(sem("PT"), 1)
            dve.wait_ge(sem("adjT"), NT)
            nc.vector.tensor_tensor(asym[:], k.adj[:], adjT[:], ALU.add).then_inc(sem("asym"), 1)
            dve.wait_ge(sem("asym"), 1)
            nc.vector.tensor_scalar(asym[:], asym[:], 0.5, None, ALU.mult).then_inc(sem("asym"), 1)
            dve.wait_ge(sem("asym"), 2)
            nc.vector.tensor_copy(S[0][:], asym[:]).then_inc(sem("square_scaled"), 1)
            dve.wait_ge(sem("w_eff"), 1)
            nc.vector.tensor_scalar(Rp[:, 1, :], bank[1][:, P:2 * P], DT, None, ALU.mult).then_inc(sem("R_half"), 1)
            nc.vector.tensor_copy(Rp[:, 0, :], k.ident[:]).then_inc(sem("R_half"), 1)
            dve.wait_ge(sem("R_half"), 2)
            nc.vector.scalar_tensor_tensor(Rp[:, 1, :], k.ident[:], 1.0 - DT, Rp[:, 1, :], ALU.mult,
                                           ALU.add).then_inc(sem("R_power"), 1)
            for q, (lo, hi) in enumerate([(2, 2), (3, 4), (5, 8)]):
                dve.wait_ge(sem("R_product"), q + 1)
                nc.vector.tensor_copy(Rp[:, lo:hi + 1, :],
                                      bank[2][:, 0:(hi - lo + 1) * D].rearrange("p (k d) -> p k d", d=D)
                                      ).then_inc(sem("R_power"), 1)
            for q in range(2):
                dve.wait_ge(sem("FR_product"), q + 1)
                nc.vector.tensor_copy(FR[:, 1 + 4 * q:5 + 4 * q, :], bank[q][:].rearrange("p (k d) -> p k d", d=D)
                                      ).then_inc(sem("FR"), 1)
            nc.vector.tensor_copy(k.gb[:, 0, :], row["fcb"]).then_inc(sem("gb"), 1)
            for q in range(2):
                dve.wait_ge(sem("bR_product"), q + 1)
                for m in range(4):
                    i = 1 + 4 * q + m
                    nc.vector.tensor_scalar(k.gb[:, i, :], bank[2 + q][:, m * D:(m + 1) * D], float(comb(STEPS, i)),
                                            None, ALU.mult).then_inc(sem("gb"), 1)
            dve.wait_ge(sem("FR"), 3)
            done = 0
            for i in range(STEPS + 1):
                nc.vector.tensor_scalar(G[:, i, :], FR[:, i, :], float(comb(STEPS, i)), None,
                                        ALU.mult).then_inc(sem("G_sum"), 1)
                done += 1
            dve.wait_ge(sem("R_power"), 4)
            for m in range(STEPS):
                dve.wait_ge(sem("G_sum"), done)
                for i in range(m + 1, STEPS + 1):
                    nc.vector.scalar_tensor_tensor(G[:, i, :], Rp[:, m, :], DT * comb(STEPS - i + m, STEPS - i),
                                                   G[:, i, :], ALU.mult, ALU.add).then_inc(sem("G_sum"), 1)
                    done += 1
            dve.wait_ge(sem("G_sum"), done)
            dve.wait_ge(sem("PT"), NT)
            nc.vector.tensor_copy(k.G_hi[:], G[:]).then_inc(sem("split_hi"), 1)
            nc.vector.tensor_copy(k.PT_hi[:], PT[:]).then_inc(sem("split_hi"), 1)
            nc.vector.tensor_copy(k.adjT_hi[:], adjT[:]).then_inc(sem("split_hi"), 1)
            dve.wait_ge(sem("split_hi"), 3)
            nc.vector.tensor_tensor(k.G_lo[:], G[:], k.G_hi[:].bitcast(F32), ALU.subtract).then_inc(sem("split_lo"), 1)
            nc.vector.tensor_tensor(k.PT_lo[:], PT[:], k.PT_hi[:].bitcast(F32), ALU.subtract
                                    ).then_inc(sem("split_lo"), 1)
            nc.vector.tensor_tensor(k.adjT_lo[:], adjT[:], k.adjT_hi[:].bitcast(F32), ALU.subtract
                                    ).then_inc(sem("split_lo"), 1)
            nc.vector.tensor_scalar(k.mask_gat[:], k.adj[:], 0.0, -BIG, ALU.is_equal, ALU.mult
                                    ).then_inc(sem("masks"), 1)
            nc.vector.tensor_scalar(k.mask_att[:], k.adj[:], 0.0, MASKED / QK_SCALE, ALU.is_le, ALU.mult
                                    ).then_inc(sem("masks"), 1)
            for q in range(2):
                nc.vector.tensor_tensor_reduce(junk2[:, q, :], W["W1g"][:], a_rows[:, q, :], 1.0, 0.0, ALU.mult,
                                               ALU.add, k.gat_a[:, q:q + 1]).then_inc(sem("gat_a"), 1)
            dve.wait_ge(sem("gat_a"), 2)
            nc.vector.tensor_scalar(k.gat_a2b[:], k.ones[:], k.gat_a[:, 1:2], None, ALU.mult
                                    ).then_inc(sem("gat_a"), 1)
            for h in range(H):
                r = slice(HD * h, HD * h + HD)
                nc.vector.tensor_copy(k.head_a4[r, h:h + 1], acol[r, :]).then_inc(sem("head_a"), 1)
                nc.vector.tensor_scalar(k.head_a[r, h, :], k.ones[r, :], acol[r, :], None, ALU.mult
                                        ).then_inc(sem("head_a"), 1)
            nc.vector.tensor_copy(edge_f[:], edge_i[:]).then_inc(sem("edge_f"), 1)
            nc.vector.tensor_copy(edge_c[:], edge_ci[:]).then_inc(sem("edge_f"), 1)
            dve.wait_ge(sem("edge_f"), 2)
            dve.wait_ge(sem("node_numbers"), 2)
            for t in range(NT):
                nc.vector.tensor_scalar(pick_s[:, t, :], edge_f[:, 0, :], node_col[:, t:t + 1], None, ALU.is_equal
                                        ).then_inc(sem("pick"), 1)
                nc.vector.tensor_scalar(k.edge_pick[:, t, E:], edge_f[:, 1, :], node_col[:, t:t + 1], None,
                                        ALU.is_equal).then_inc(sem("pick"), 1)
            dve.wait_ge(sem("pick"), 2 * NT)
            nc.vector.tensor_tensor(k.edge_pick[:, :, 0:E], pick_s[:], k.edge_pick[:, :, E:], ALU.add
                                    ).then_inc(sem("pick"), 1)
            for e in range(ET):
                nc.vector.tensor_scalar(k.src_rows[:, e, :], node_row[:], edge_c[:, 0, e:e + 1], None, ALU.is_equal
                                        ).then_inc(sem("rows"), 1)
                nc.vector.tensor_scalar(dst_rows[:, e, :], node_row[:], edge_c[:, 1, e:e + 1], None, ALU.is_equal
                                        ).then_inc(sem("rows"), 1)
                nc.vector.tensor_scalar(k.same_src[:, e, :], edge_f[:, 0, :], edge_c[:, 0, e:e + 1], None,
                                        ALU.is_equal).then_inc(sem("rows"), 1)
            dve.wait_ge(sem("rows"), 3 * ET)
            for e in range(ET):
                dve.wait_ge(sem("adj_picked"), e + 1)
                nc.vector.tensor_tensor_reduce(junk[:, e, :], bank[2 + e][:], dst_rows[:, e, :], 1.0, 0.0, ALU.mult,
                                               ALU.add, a0e[:, e:e + 1]).then_inc(sem("edge_weight"), 1)
            nc.vector.tensor_scalar(k.seg_bias[:], k.same_src[:], BIG, -BIG, ALU.mult, ALU.add
                                    ).then_inc(sem("seg"), 1)
            dve.wait_ge(sem("log_edge"), 1)
            for e in range(ET):
                nc.vector.tensor_scalar(logAb[:, e, :], k.ones[:], k.logA[:, e:e + 1], None, ALU.mult
                                        ).then_inc(sem("logAb"), 1)
            dve.wait_ge(sem("seg"), 1)
            dve.wait_ge(sem("log_row"), 1)
            for e in range(ET):
                nc.vector.tensor_tensor(k.seg_bias[:, e, :], k.seg_bias[:, e, :], bank[0][:, 0:E], ALU.add
                                        ).then_inc(sem("seg"), 1)
            for q in range(SQUARINGS):
                dve.wait_ge(sem("norm_sum"), q + 1)
                nc.vector.reciprocal(nrm[:, q:q + 1], bank[0][:, q:q + 1] if q else bank[0][:, 0:1]
                                     ).then_inc(sem("nrm"), 1)
                dve.wait_ge(sem("nrm"), q + 1)
                for t in range(NT):
                    dve.wait_ge(sem("square"), NT * q + t + 1)
                    nc.vector.tensor_scalar(S[(q + 1) % 2][:, t, :], bank[4 + t][:], nrm[:, q:q + 1], None,
                                            ALU.mult).then_inc(sem("square_scaled"), 1)
            dve.wait_ge(sem("square_scaled"), NT * SQUARINGS + 1)
            nc.vector.tensor_reduce(vec[:, 0, :], S[SQUARINGS % 2][:].bitcast(F32), AX, ALU.add
                                    ).then_inc(sem("vec"), 1)
            for q in range(2):
                dve.wait_ge(sem("A_vec"), q + 1)
                nc.vector.tensor_copy(vec[:, q + 1, :], bank[1][:, 0:NT]).then_inc(sem("vec"), 1)
            dve.wait_ge(sem("vec"), 3)
            for q in range(2):
                nc.vector.tensor_tensor_reduce(junk2[:, 2 + q, 0:NT], vec[:, 1, :], vec[:, 2 - q, :], 1.0, 0.0,
                                               ALU.mult, ALU.add, dots[:, q:q + 1]).then_inc(sem("dots"), 1)
            dve.wait_ge(sem("dot_sums"), 1)
            nc.vector.reciprocal(lam[:, 0:1], bank[2][:, 1:2]).then_inc(sem("lam"), 1)
            dve.wait_ge(sem("lam"), 1)
            nc.vector.tensor_tensor(lam[:, 1:2], lam[:, 0:1], bank[2][:, 0:1], ALU.mult).then_inc(sem("lam"), 1)
            dve.wait_ge(sem("lam"), 2)
            nc.vector.tensor_scalar(lam[:, 2:3], lam[:, 1:2], 1e-8, None, ALU.add).then_inc(sem("lam"), 1)
            dve.wait_ge(sem("lam"), 3)
            nc.vector.reciprocal(lam[:, 3:4], lam[:, 2:3]).then_inc(sem("lam"), 1)
            dve.wait_ge(sem("lam"), 4)
            nc.vector.tensor_scalar(k.two_lam[:], lam[:, 3:4], 2.0, None, ALU.mult).then_inc(sem("lam"), 1)

        @block.tensor
        def _(pe):
            pe.wait_ge(sem("tables_loaded"), LOADED)
            pe.wait_ge(sem("ident_ready"), 1)
            for i, n in enumerate(["w", "Wlin", "Wval", "Wout"]):
                nc.tensor.transpose(bank[0][:, i * P:(i + 1) * P], raw[n][:], k.ident[:]
                                    ).then_inc(sem("weights_turned"), 1)
            nc.tensor.transpose(bank[1][:, 0:P], raw["fcw"][:], k.ident[:]).then_inc(sem("fc_turned"), 1)
            for s in range(NT):
                for t in range(NT):
                    mm = nc.tensor.transpose(bank[4 + s][:, t * P:(t + 1) * P], k.adj[:, t, s * P:(s + 1) * P],
                                             k.ident[:])
                mm.then_inc(sem("adj_turned"), 1)
            pe.wait_ge(sem("p_row"), 3 * NT)
            for s in range(NT):
                pe.wait_ge(sem("adjT"), s + 1)
                for t in range(NT):
                    mm = nc.tensor.transpose(bank[4 + s][:, t * P:(t + 1) * P], P_row[:, t, s * P:(s + 1) * P],
                                             k.ident[:])
                mm.then_inc(sem("p_turned"), 1)
            pe.wait_ge(sem("wT"), 5)
            pe.wait_ge(sem("FR"), 1)
            nc.tensor.matmul(bank[1][:, P:2 * P], wTd[:], wT[:], start=True, stop=True).then_inc(sem("w_eff"), 1)
            for q, (left, lo, hi) in enumerate([(1, 1, 1), (2, 1, 2), (4, 1, 4)]):
                pe.wait_ge(sem("R_power"), q + 1)
                nc.tensor.matmul(bank[2][:, 0:(hi - lo + 1) * D], Rp[:, left, :],
                                 Rp[:, lo:hi + 1, :], start=True, stop=True
                                 ).then_inc(sem("R_product"), 1)
            pe.wait_ge(sem("R_power"), 4)
            for q in range(2):
                nc.tensor.matmul(bank[q][:], raw["fcw"][:], Rp[:, 1 + 4 * q:5 + 4 * q, :], start=True, stop=True
                                 ).then_inc(sem("FR_product"), 1)
            pe.wait_ge(sem("fcb_wide"), 1)
            for q in range(2):
                nc.tensor.matmul(bank[2 + q][:], fcb_b[:], Rp[:, 1 + 4 * q:5 + 4 * q, :], start=True, stop=True
                                 ).then_inc(sem("bR_product"), 1)
            pe.wait_ge(sem("pick"), 2 * NT)
            pe.wait_ge(sem("gb"), STEPS + 1)
            for e in range(ET):
                for t in range(NT):
                    mm = nc.tensor.matmul(bank[2 + e][:], pick_s[:, t, e * P:(e + 1) * P], k.adj[:, t, :],
                                          start=(t == 0), stop=(t == NT - 1))
                mm.then_inc(sem("adj_picked"), 1)
            pe.wait_ge(sem("logAb"), ET)
            pe.wait_ge(sem("FR"), 3)
            for e in range(ET):
                mm = nc.tensor.matmul(bank[0][:, e * P:(e + 1) * P], logAb[:, e, :], k.ident[:], start=True, stop=True)
            mm.then_inc(sem("log_row"), 1)
            pe.wait_ge(sem("PT"), NT)
            pe.wait_ge(sem("seg"), 1 + ET)
            for q in range(SQUARINGS):
                pe.wait_ge(sem("norm_part"), q + 1)
                need(pe, sem("nrm"), q)
                nc.tensor.matmul(bank[0][:, q:q + 1], k.ones[:], ssq[:, q:q + 1], start=True, stop=True
                                 ).then_inc(sem("norm_sum"), 1)
                pe.wait_ge(sem("square_scaled"), NT * q + 1)
                for t in range(NT):
                    for s in range(NT):
                        mm = nc.tensor.matmul(bank[4 + t][:], S[q % 2][:, s, t * P:(t + 1) * P], S[q % 2][:, s, :],
                                              start=(s == 0), stop=(s == NT - 1))
                    mm.then_inc(sem("square"), 1)
            for q in range(2):
                pe.wait_ge(sem("vec"), q + 1)
                for t in range(NT):
                    for s in range(NT):
                        mm = nc.tensor.matmul(bank[1][:, t:t + 1], asym[:, s, t * P:(t + 1) * P],
                                              vec[:, q, s:s + 1], start=(s == 0), stop=(s == NT - 1))
                mm.then_inc(sem("A_vec"), 1)
            pe.wait_ge(sem("dots"), 2)
            nc.tensor.matmul(bank[2][:, 0:2], k.ones[:], dots[:], start=True, stop=True).then_inc(sem("dot_sums"), 1)


def build_layer0(nc, k):
    t_in, bank, sem = k.t_in, k.bank, k.sem
    LEVELS = STEPS + 1
    with ExitStack() as c:
        def sb(name, shape, dt=F32):
            return c.enter_context(nc.sbuf_tensor(name, shape, dt))

        xin = [sb(f"l0_x{u}", [P, NT, D]) for u in range(2)]
        stats = sb("l0_stats", [P, 2, NT, 6])
        mv = sb("l0_mv", [P, 2, NT, 2])
        rs = sb("l0_rs", [P, 2, 2, NT])
        z = [sb(f"l0_z{u}", [P, NT, D]) for u in range(2)]
        zT = [sb(f"l0_zT{u}", [P, N]) for u in range(2)]
        x0T_hi = sb("x0T_hi", [P, HB, N], R32)
        x0T_lo = sb("x0T_lo", [P, HB, N], R32)
        Z_hi = sb("Z_hi", [P, NT, HB * D], R32)
        Z_lo = sb("Z_lo", [P, NT, HB * D], R32)
        zs = sb("l0_sum", [P, NC, NT, CB * D])
        xres = sb("l0_res", [P, NT, CB * D])

        block = c.enter_context(nc.Block())

        def chunk_dram(ap, half, ch, t):
            b0 = half * HB + ch * CB
            return ap[bass.ds(b0, CB), t * P:(t + 1) * P, :].rearrange("b p d -> p b d")

        @block.sync
        def _(sp):
            with sp.Fori(0, 2) as half:
                with sp.Fori(0, HB // 2) as pair:
                    n = half * (HB // 2) + pair
                    for u in range(2):
                        sp.wait_ge(sem(f"l0_normed{u}"), n * NT + 1)
                        sp.dma_start(xin[u][:], k.nodes1(t_in["x"], half * HB + pair * 2 + u)
                                     ).then_inc(sem(f"l0_loaded{u}"), 16)
                for ch in range(NC):
                    for t in range(NT):
                        sp.wait_ge(sem(f"l0_stored{t}"), (half * NC + ch) * 16 + 1)
                        sp.dma_start(xres[:, t, :].rearrange("p (b d) -> p b d", d=D),
                                     chunk_dram(t_in["x"], half, ch, t)).then_inc(sem(f"l0_res{t}"), 16)
                    for t in range(NT):
                        sp.wait_ge(sem(f"l0_final{t}"), half * NC + ch + 1)
                        sp.dma_start(chunk_dram(k.x1_dram, half, ch, t),
                                     xres[:, t, :].rearrange("p (b d) -> p b d", d=D)
                                     ).then_inc(sem(f"l0_stored{t}"), 16)
            for t in range(NT):
                sp.wait_ge(sem(f"l0_stored{t}"), 2 * NC * 16 + 1)

        @block.gpsimd
        def _(pool):
            for u in range(2):
                pool.sem_inc(sem(f"l0_turned{u}"))
                pool.sem_inc(sem(f"l0_normed{u}"))
                pool.sem_inc(sem(f"l0_x0lo{u}"))
                pool.sem_inc(sem(f"l0_zT{u}"))
            for t in range(NT):
                pool.sem_inc(sem(f"l0_stored{t}"))
            with pool.Fori(0, 2) as half:
                with pool.Fori(0, HB // 2) as pair:
                    n = half * (HB // 2) + pair
                    for u in range(2):
                        wait_alone(pool, sem(f"l0_aggr{u}"), (n + 1) * NT, sem("waits_passed"))
                        nc.gpsimd.tensor_scalar(rs[:, u, 0, :], mv[:, u, :, 1], EPS, None, ALU.add
                                                ).then_inc(sem(f"l0_vareps{u}"), 1)
                        pool.wait_ge(sem(f"l0_vareps{u}"), n + 1)
                        nc.gpsimd.tensor_tensor(rs[:, u, 1, :], rs[:, u, 0, :], k.neg_half[:], ALU.pow
                                                ).then_inc(sem(f"l0_rstd{u}"), 1)

        @block.scalar
        def _(act):
            with act.Fori(0, 2) as half:
                with act.Fori(0, HB // 2) as pair:
                    n = half * (HB // 2) + pair
                    for u in range(2):
                        act.wait_ge(sem(f"l0_turned{u}"), n + 2)
                        act.wait_ge(sem(f"l0_x0lo{u}"), n + 1)
                        nc.scalar.activation(zT[u][:], bank[u][:], ACT.Relu).then_inc(sem(f"l0_zT{u}"), 1)
                with act.Fori(0, LEVELS - 1) as lev:
                    m = half * (LEVELS - 1) + lev
                    for ch in range(NC):
                        act.wait_ge(sem(f"l0_level{ch}"), half * LEVELS * NT + lev * NT + NT)
                        for t in range(NT):
                            act.wait_ge(sem(f"l0_sum{ch}"), m * NT + t + 1)
                            nc.scalar.copy(Z_hi[:, t, ch * CB * D:(ch + 1) * CB * D], zs[:, ch, t, :]
                                           ).then_inc(sem(f"l0_Zhi{ch}"), 1)

        @block.vector
        def _(dve):
            with dve.Fori(0, 2) as half:
                with dve.Fori(0, HB // 2) as pair:
                    n = half * (HB // 2) + pair
                    for u in range(2):
                        dve.wait_ge(sem(f"l0_loaded{u}"), (n + 1) * 16)
                        for t in range(NT):
                            nc.vector.bn_stats(stats[:, u, t, :], xin[u][:, t, :]).then_inc(sem(f"l0_stats{u}"), 1)
                        wait_alone(dve, sem(f"l0_stats{u}"), (n + 1) * NT, sem("waits_passed"))
                        for t in range(NT):
                            nc.vector.bn_aggr(mv[:, u, t, :], stats[:, u, t, :]).then_inc(sem(f"l0_aggr{u}"), 1)
                    for u in range(2):
                        dve.wait_ge(sem(f"l0_rstd{u}"), n + 1)
                        dve.wait_ge(sem(f"l0_turned{u}"), n + 1)
                        for t in range(NT):
                            nc.vector.tensor_scalar(z[u][:, t, :], xin[u][:, t, :], mv[:, u, t, 0:1],
                                                    rs[:, u, 1, t:t + 1], ALU.subtract, ALU.mult
                                                    ).then_inc(sem(f"l0_normed{u}"), 1)
                    for u in range(2):
                        dve.wait_ge(sem(f"l0_zT{u}"), n + 2)
                        nc.vector.tensor_copy(x0T_hi[:, pair * 2 + u, :], zT[u][:]).then_inc(sem(f"l0_x0hi{u}"), 1)
                        dve.wait_ge(sem(f"l0_x0hi{u}"), n + 1)
                        nc.vector.tensor_tensor(x0T_lo[:, pair * 2 + u, :], zT[u][:],
                                                x0T_hi[:, pair * 2 + u, :].bitcast(F32), ALU.subtract
                                                ).then_inc(sem(f"l0_x0lo{u}"), 1)

                with dve.Fori(0, LEVELS - 1) as lev:
                    m = half * (LEVELS - 1) + lev
                    for ch in range(NC):
                        for t in range(NT):
                            dve.wait_ge(sem(f"l0_level{ch}"), half * LEVELS * NT + lev * NT + t + 1)
                            nc.vector.tensor_tensor(zs[:, ch, t, :].rearrange("p (b d) -> p b d", d=D),
                                                    bank[ch * NT + t][:].rearrange("p (b d) -> p b d", d=D),
                                                    k.gb[:, bass.ds(lev, 1), :].broadcast_to([P, CB, D]),
                                                    ALU.add).then_inc(sem(f"l0_sum{ch}"), 1)
                        for t in range(NT):
                            dve.wait_ge(sem(f"l0_Zhi{ch}"), m * NT + t + 1)
                            sl = slice(ch * CB * D, (ch + 1) * CB * D)
                            nc.vector.tensor_tensor(Z_lo[:, t, sl], zs[:, ch, t, :], Z_hi[:, t, sl].bitcast(F32),
                                                    ALU.subtract).then_inc(sem(f"l0_Zlo{ch}"), 1)
                for ch in range(NC):
                    for t in range(NT):
                        dve.wait_ge(sem(f"l0_level{ch}"), (half + 1) * LEVELS * NT - NT + t + 1)
                        nc.vector.tensor_tensor(zs[:, ch, t, :].rearrange("p (b d) -> p b d", d=D),
                                                bank[ch * NT + t][:].rearrange("p (b d) -> p b d", d=D),
                                                k.gb[:, LEVELS - 1:LEVELS, :].broadcast_to([P, CB, D]),
                                                ALU.add).then_inc(sem(f"l0_last{ch}"), 1)
                        dve.wait_ge(sem(f"l0_last{ch}"), half * NT + t + 1)
                        dve.wait_ge(sem(f"l0_res{t}"), (half * NC + ch + 1) * 16)
                        nc.vector.tensor_tensor(xres[:, t, :], zs[:, ch, t, :], xres[:, t, :], ALU.add
                                                ).then_inc(sem(f"l0_final{t}"), 1)

        @block.tensor
        def _(pe):
            def x0_times(ch, t, g, first):
                out = bank[ch * NT + t]
                for b in range(CB):
                    bb = ch * CB + b
                    cols = slice(b * D, (b + 1) * D)
                    n0 = slice(t * P, (t + 1) * P)
                    nc.tensor.matmul(out[:, cols], x0T_hi[:, bb, n0], g(k.G_hi), start=first, stop=False)
                    nc.tensor.matmul(out[:, cols], x0T_hi[:, bb, n0], g(k.G_lo), start=False, stop=False)
                    mm = nc.tensor.matmul(out[:, cols], x0T_lo[:, bb, n0], g(k.G_hi), start=False,
                                          stop=first or b == CB - 1)
                return mm

            def p_times(ch, t):
                sl = slice(ch * CB * D, (ch + 1) * CB * D)
                n0 = slice(t * P, (t + 1) * P)
                for s in range(NT):
                    for i, (left, right) in enumerate([(k.PT_hi, Z_hi), (k.PT_hi, Z_lo), (k.PT_lo, Z_hi)]):
                        nc.tensor.matmul(bank[ch * NT + t][:], left[:, s, n0], right[:, s, sl],
                                         start=(s == 0 and i == 0), stop=False)

            with pe.Fori(0, 2) as half:
                with pe.Fori(0, HB // 2) as pair:
                    n = half * (HB // 2) + pair
                    for u in range(2):
                        pe.wait_ge(sem(f"l0_normed{u}"), (n + 1) * NT + 1)
                        pe.wait_ge(sem(f"l0_zT{u}"), n + 1)
                        for t in range(NT):
                            mm = nc.tensor.transpose(bank[u][:, t * P:(t + 1) * P], z[u][:, t, :], k.ident[:])
                        mm.then_inc(sem(f"l0_turned{u}"), 1)
                for u in range(2):
                    pe.wait_ge(sem(f"l0_x0lo{u}"), (half + 1) * (HB // 2) + 1)
                for ch in range(NC):
                    for t in range(NT):
                        x0_times(ch, t, lambda G: G[:, 0, :], True).then_inc(sem(f"l0_level{ch}"), 1)
                with pe.Fori(1, LEVELS) as lev:
                    m = half * (LEVELS - 1) + lev
                    for ch in range(NC):
                        pe.wait_ge(sem(f"l0_Zlo{ch}"), m * NT)
                        for t in range(NT):
                            p_times(ch, t)
                            x0_times(ch, t, lambda G: G[:, bass.ds(lev, 1), :].rearrange("p o d -> p (o d)"), False
                                     ).then_inc(sem(f"l0_level{ch}"), 1)
                for ch in range(NC):
                    pe.wait_ge(sem(f"l0_last{ch}"), (half + 1) * NT)


def wait_alone(eng, semaphore, value, passed):
    need(eng, semaphore, value)
    if not isinstance(value, int):
        eng.sem_inc(passed)


STAGES = ["gat", "edge", "cheb", "att", "ffn"]
LAG = {s: i for i, s in enumerate(STAGES)}
TILES = H * NT
RING_T, RING_E = 3, 4

SCHEDULE = [
    (0, "gat", "gat_stats"), (0, "cheb", "cheb_stats"), (0, "ffn", "ffn_wo"),
    (0, "ffn", "ffn_res"), (0, "gat", "gat_rstd"), (0, "cheb", "cheb_rstd"),
    (1, "gat", "gat_apply"), (1, "cheb", "cheb_apply"), (1, "ffn", "ffn_y2"), (1, "ffn", "n2_rstd"),
    (2, "gat", "gat_turn"), (2, "cheb", "cheb_turn"), (2, "gat", "gat_hT"), (2, "cheb", "cheb_hT"),
    (2, "ffn", "n2_apply"), (2, "ffn", "n2_affine"),
    (3, "gat", "gat_wh"), (3, "cheb", "cheb_g"), (3, "gat", "gat_wh_out"), (3, "cheb", "cheb_gf"),
    (3, "cheb", "cheb_gm"),
    (4, "gat", "gat_s2"), (4, "cheb", "cheb_split"), (4, "ffn", "ffn_turn"), (4, "ffn", "ffn_x2T"),
    (5, "gat", "gat_scores"), (5, "cheb", "cheb_prop"), (5, "ffn", "ffn_up"), (5, "ffn", "ffn_b2"), (5, "gat", "gat_low"),
    (6, "cheb", "cheb_y"), (6, "cheb", "n1_rstd"), (6, "edge", "edge_stats"), (6, "edge", "edge_rstd"),
    (6, "ffn", "ffn_gelu"),
    (7, "gat", "gat_max"), (7, "cheb", "n1_apply"), (7, "cheb", "n1_affine"), (7, "ffn", "ffn_down"),
    (7, "gat", "gat_exp"), (7, "edge", "edge_apply"),
    (8, "ffn", "ffn_y3"), (8, "ffn", "n3_rstd"), (8, "edge", "edge_gather"), (8, "cheb", "cheb_x1"),
    (9, "ffn", "n3_apply"), (9, "ffn", "n3_affine"), (9, "edge", "edge_hg"), (9, "cheb", "cheb_res"),
    (9, "cheb", "cheb_x1turn"), (9, "cheb", "cheb_x1T"), (9, "edge", "edge_x"), (9, "edge", "edge_xz"),
    (10, "ffn", "ffn_final"), (10, "edge", "edge_z"), (10, "cheb", "cheb_q"), (10, "cheb", "cheb_qsplit"),
    (10, "gat", "gat_eturn0"), (10, "edge", "edge_lb"), (10, "gat", "gat_eT0"),
    (11, "edge", "edge_max"), (11, "cheb", "cheb_k"), (11, "gat", "gat_eturn2"), (11, "cheb", "cheb_ksplit"),
    (11, "gat", "gat_eT2"),
    (12, "edge", "edge_lcol"), (12, "edge", "edge_le"), (12, "edge", "edge_exp"), (12, "cheb", "cheb_v"),
    (12, "cheb", "cheb_vout"), (12, "gat", "gat_pv"),
    (13, "edge", "edge_den"), (13, "edge", "edge_u"),
    (14, "edge", "edge_scatter"), (14, "edge", "edge_yT"),
    (15, "edge", "edge_out"), (15, "edge", "edge_x3"), (15, "gat", "gat_x2"),
]


def build_layers(nc, k):
    bank, sem, W, row4 = k.bank, k.sem, k.W, k.row4
    with ExitStack() as c:
        def sb(name, shape, dt=F32):
            return c.enter_context(nc.sbuf_tensor(name, shape, dt))

        def tile(name):
            return sb(name, [P, NT, D])

        ln_mem = {}
        for tag in ["gat", "edge", "cheb", "n1", "n2", "n3"]:
            ln_mem[tag] = (sb(tag + "_stat", [P, NT, 6]), sb(tag + "_mv", [P, NT, 2]), sb(tag + "_rs", [P, 2, NT]))
        xA, zA, WhA, x2 = tile("gat_xin"), tile("gat_z"), tile("gat_whs"), tile("x2")
        hTA = sb("gat_hTs", [P, N])
        gat_T, gat_V, gat_ET = (sb(n, [P, NT, N]) for n in ["gat_Ts", "gat_Vs", "gat_ETs"])
        gat_E = gat_T
        gat_small = sb("gat_small", [P, 8, NT])
        h2, x3 = tile("edge_hs"), tile("x3")
        hg = sb("edge_hgs", [P, 2 * E])
        xz = sb("edge_xzs", [P, E])
        zT = xz
        edge_junk = sb("edge_junk", [P, ET * H, E], BF16)
        edge_small = sb("edge_small", [P, 5, ET * H])
        U = sb("edge_us", [P, ET * D])
        YT = hg
        h3, gf, gm, y1, x1 = (tile("cheb_" + n) for n in ["hs", "gfs", "gms", "y1", "x1s"])
        h3T = x1T = sb("cheb_xTs", [P, N])
        g_hi, g_lo = sb("g_hi", [P, N], R32), sb("g_lo", [P, N], R32)
        qk_hi = [sb(f"{n}_hi", [P, N], R32) for n in "qk"]
        qk_lo = [sb(f"{n}_lo", [P, N], R32) for n in "qk"]
        vS, vD = tile("v_out"), tile("v_in")
        Qs, Ks = sb("Q_parts", [P, H, N], R32), sb("K_parts", [P, H, N], R32)
        att_T, att_E = sb("att_Ts", [P, RING_T, N]), sb("att_Es", [P, RING_E, N])
        att_PT = sb("att_PTs", [P, H, NT, N])
        att_small = sb("att_small", [P, 3, TILES])
        oT = sb("att_oTs", [P, N])
        xrE, y2, y3, x3E = (tile("ffn_" + n) for n in ["xr", "y2s", "y3s", "x3"])
        mT = sb("ffn_mT", [P, 2, N])
        x2T = mT[:, 1, :]

        a0, a1, b0, b1, c0, c1, c2, c3 = bank

        def cols(t):
            return slice(t * P, (t + 1) * P)

        def flat(x):
            return x[:].rearrange("p t d -> p (t d)")

        def ready(eng, name, n, count=1, per=1):
            need(eng, sem(name), n * per + count)

        def freed(eng, name, n, per=1):
            need(eng, sem(name), n * per)

        def ready_alone(eng, name, n, count=1, per=1):
            wait_alone(eng, sem(name), n * per + count, sem("waits_passed"))

        def freed_alone(eng, name, n, per=1):
            wait_alone(eng, sem(name), n * per, sem("waits_passed"))

        def ln_stats(dve, tag, n, src):
            stat, mv, _ = ln_mem[tag]
            for t in range(NT):
                nc.vector.bn_stats(stat[:, t, :], src[:, t, :]).then_inc(sem(tag + "_stat"), 1)
            ready_alone(dve, tag + "_stat", n, NT, NT)
            for t in range(NT):
                nc.vector.bn_aggr(mv[:, t, :], stat[:, t, :]).then_inc(sem(tag + "_aggr"), 1)

        def ln_rstd(pool, tag, n):
            _, mv, rs = ln_mem[tag]
            ready_alone(pool, tag + "_aggr", n, NT, NT)
            nc.gpsimd.tensor_scalar(rs[:, 0, :], mv[:, :, 1], EPS, None, ALU.add).then_inc(sem(tag + "_vareps"), 1)
            ready(pool, tag + "_vareps", n)
            nc.gpsimd.tensor_tensor(rs[:, 1, :], rs[:, 0, :], k.neg_half[:], ALU.pow).then_inc(sem(tag + "_rs"), 1)

        def ln_apply(dve, tag, n, src, dst):
            _, mv, rs = ln_mem[tag]
            ready(dve, tag + "_rs", n)
            for t in range(NT):
                nc.vector.tensor_scalar(dst[:, t, :], src[:, t, :], mv[:, t, 0:1], rs[:, 1, t:t + 1], ALU.subtract,
                                        ALU.mult).then_inc(sem(tag + "_normed"), 1)

        def affine(pool, tag, n, x, g, b):
            ready(pool, tag + "_normed", n, NT, NT)
            nc.gpsimd.tensor_tensor(x[:], x[:], row4(g), ALU.mult).then_inc(sem(tag + "_aff"), 1)
            ready(pool, tag + "_aff", n, 1, 2)
            nc.gpsimd.tensor_tensor(x[:], x[:], row4(b), ALU.add).then_inc(sem(tag + "_aff"), 1)

        def run(eng, fori, steps, att, start=None, end=None):
            def iteration(i):
                def n_of(stage):
                    n = i - LAG[stage]
                    return n if not isinstance(i, int) or 0 <= n < B else None

                if start:
                    start(n_of)
                at = 0
                for j in range(TILES + 3):
                    if att and n_of("att") is not None:
                        att(n_of("att"), j)
                    while at < len(SCHEDULE) and SCHEDULE[at][0] <= j:
                        _, stage, step = SCHEDULE[at]
                        if step in steps and n_of(stage) is not None:
                            steps[step](n_of(stage))
                        at += 1
                if end:
                    end(n_of)

            fill = len(STAGES)
            for i in range(fill):
                iteration(i)
            with fori(fill, B) as i:
                iteration(i)
            for i in range(B, B + fill - 1):
                iteration(i)

        block = c.enter_context(nc.Block())

        @block.sync
        def _(sp):
            def load_x(n):
                freed_alone(sp, "gat_done", n, NT)
                sp.dma_start(xA[:], k.nodes1(k.x1_dram, n)).then_inc(sem("gat_loaded"), 16)

            def store_x3(n):
                ready_alone(sp, "edge_done", n)
                sp.dma_start(k.nodes1(k.x3_dram, n), x3[:]).then_inc(sem("x3_stored"), 16)

            def store_res(n):
                ready_alone(sp, "cheb_x1", n)
                sp.dma_start(k.nodes1(k.res_dram, n), x1[:]).then_inc(sem("res_stored"), 16)

            def store_v(n):
                ready_alone(sp, "v_out", n)
                sp.dma_start(k.nodes1(k.v_dram, n), vS[:]).then_inc(sem("v_stored"), 16)

            def load_v(n):
                ready_alone(sp, "v_stored", n, 16, 16)
                freed_alone(sp, "att_pv", n)
                sp.dma_start(vD[:], k.nodes1(k.v_dram, n)).then_inc(sem("att_v"), 16)

            def stack(n, which, h):
                ready_alone(sp, f"{'qk'[which]}_lo", n)
                wait_alone(sp, sem("att_score"), n * TILES - TILES + NT * (h + 1), sem("waits_passed"))
                dst = [Qs, Ks][which]
                order = [[0, 0, 1, 1], [0, 1, 0, 1]][which]
                for g in range(4):
                    src = [qk_hi, qk_lo][order[g]][which]
                    sp.dma_start(dst[HD * g:HD * (g + 1), h, :].bitcast(F32), src[HD * h:HD * (h + 1), :].bitcast(F32)
                                 ).then_inc(sem(f"parts{h}"), 16)

            def load_ffn(n):
                ready_alone(sp, "res_stored", n, 16, 16)
                freed_alone(sp, "ffn_y2", n)
                sp.dma_start(xrE[:], k.nodes1(k.res_dram, n)).then_inc(sem("ffn_xr"), 16)
                ready_alone(sp, "x3_stored", n, 16, 16)
                freed_alone(sp, "ffn_fin", n)
                sp.dma_start(x3E[:], k.nodes1(k.x3_dram, n)).then_inc(sem("ffn_x3"), 16)

            def store_out(n):
                ready_alone(sp, "ffn_fin", n)
                sp.dma_start(k.nodes1(k.out, n), y3[:]).then_inc(sem("out_stored"), 16)

            def first(n_of):
                for stage, step in [("gat", load_x), ("att", load_v), ("ffn", load_ffn)]:
                    if n_of(stage) is not None:
                        step(n_of(stage))

            def last(n_of):
                n = n_of("cheb")
                if n is not None:
                    for h in range(H):
                        for which in range(2):
                            stack(n, which, h)
                if n_of("edge") is not None:
                    store_x3(n_of("edge"))

            run(sp, sp.Fori, {"cheb_res": store_res, "cheb_vout": store_v, "ffn_final": store_out}, None,
                first, last)
            for name in ["x3_stored", "res_stored", "v_stored", "out_stored"]:
                sp.wait_ge(sem(name), 16 * B)

        @block.gpsimd
        def _(pool):
            def gat_low(n):
                ready_alone(pool, "gat_small", n, 4, 4)
                wait_alone(pool, sem("gat_exp"), n * NT, sem("waits_passed"))
                for t in range(NT):
                    nc.gpsimd.tensor_scalar(gat_V[:, t, :], gat_T[:, t, :], 0.2, gat_small[:, 5, t:t + 1], ALU.mult,
                                            ALU.add).then_inc(sem("gat_low"), 1)

            def cheb_gm(n):
                ready(pool, "cheb_gf", n)
                freed(pool, "cheb_y", n)
                nc.gpsimd.tensor_tensor(gm[:], gf[:], row4("bc"), ALU.subtract).then_inc(sem("cheb_gm"), 1)

            def ffn_res(n):
                ready(pool, "ffn_xr", n, 16, 16)
                nc.gpsimd.tensor_tensor(xrE[:], xrE[:], row4("bo"), ALU.add).then_inc(sem("ffn_res"), 1)

            def n2_affine(n):
                affine(pool, "n2", n, y2, "g2", "be2")

            def ffn_b2(n):
                ready(pool, "ffn_turned", n)
                nc.gpsimd.tensor_tensor(y2[:], y2[:], row4("b2"), ALU.add).then_inc(sem("ffn_x2b"), 1)

            def att(n, j):
                j -= 1
                if not 0 <= j < TILES:
                    return
                ready_alone(pool, "att_rv", n, j + 1, TILES)
                e = att_E[:, j % RING_E, :]
                nc.gpsimd.tensor_scalar(e, e, att_small[:, 2, j:j + 1], 1.0, ALU.mult, ALU.mult
                                        ).then_inc(sem("att_norm"), 1)

            run(pool, pool.Fori, {
                "gat_low": gat_low, "cheb_gm": cheb_gm, "ffn_res": ffn_res, "n2_affine": n2_affine, "ffn_b2": ffn_b2,
                "gat_rstd": lambda n: ln_rstd(pool, "gat", n), "edge_rstd": lambda n: ln_rstd(pool, "edge", n),
                "cheb_rstd": lambda n: ln_rstd(pool, "cheb", n), "n1_rstd": lambda n: ln_rstd(pool, "n1", n),
                "n2_rstd": lambda n: ln_rstd(pool, "n2", n), "n3_rstd": lambda n: ln_rstd(pool, "n3", n),
                "n1_affine": lambda n: affine(pool, "n1", n, y1, "g1", "be1"),
                "n3_affine": lambda n: affine(pool, "n3", n, y3, "g3", "be3"),
            }, att)

        @block.scalar
        def _(act):
            def copy(n, dst, src, made, done, last_reader=None, func=ACT.Copy, **kw):
                ready(act, made, n)
                if last_reader:
                    freed(act, last_reader, n)
                nc.scalar.activation(dst, src, func, **kw).then_inc(sem(done), 1)

            def gat_exp(n):
                for t in range(NT):
                    ready(act, "gat_max", n, t + 1, NT)
                    nc.scalar.activation(gat_E[:, t, :], gat_V[:, t, :], ACT.Exp, bias=gat_small[:, 4, t:t + 1],
                                         accum_out=gat_small[:, 6, t:t + 1]).then_inc(sem("gat_exp"), 1)

            def gat_eT(n, t0):
                freed(act, "gat_pv", n)
                for t in (t0, t0 + 1):
                    ready(act, "gat_eturn", n, t + 1, NT)
                    nc.scalar.copy(gat_ET[:, :, cols(t)], [a0, a1][t % 2][:].rearrange("p (s q) -> p s q", q=P)
                                   ).then_inc(sem("gat_eT"), 1)

            def ffn_gelu(n):
                freed(act, "ffn_downed", n)
                for q in range(2):
                    ready(act, "ffn_up", n, q + 1, 2)
                    nc.scalar.activation(mT[:, q, :], [b0, b1][q][:], ACT.Gelu, bias=k.b1c[:, q:q + 1]
                                         ).then_inc(sem("ffn_gelu"), 1)

            def edge_exp(n):
                ready(act, "edge_le", n, ET, ET)
                nc.scalar.activation(edge_small[:, 2, :], edge_small[:, 1, :], ACT.Exp).then_inc(sem("edge_exp"), 1)

            def att(n, j):
                if j < TILES:
                    ready(act, "att_T", n, j + 1, TILES)
                    need(act, sem("att_turn"), n * TILES + j + 1 - RING_E)
                    nc.scalar.activation(att_E[:, j % RING_E, :], att_T[:, j % RING_T, :], ACT.Exp, scale=-1.0,
                                         bias=att_small[:, 0, j:j + 1], accum_out=att_small[:, 1, j:j + 1]
                                         ).then_inc(sem("att_exp"), 1)
                i = j - 2
                if 0 <= i < TILES:
                    ready(act, "att_turn", n, i + 1, TILES)
                    if i == 0:
                        freed(act, "att_pv", n)
                    nc.scalar.copy(att_PT[:, i // NT, :, cols(i % NT)], c2[:].rearrange("p (s q) -> p s q", q=P)
                                   ).then_inc(sem("att_pt"), 1)
                if j == TILES + 2:
                    copy(n, oT[:], c2[:], "att_pv", "att_oT", "ffn_wo")

            run(act, act.Fori, {
                "gat_hT": lambda n: copy(n, hTA[:], a0[:], "gat_turned", "gat_hT", "gat_s2", ACT.Relu),
                "gat_wh_out": lambda n: copy(n, flat(WhA), a1[:], "gat_wh", "gat_whs", "gat_pv"),
                "gat_exp": gat_exp, "gat_eT0": lambda n: gat_eT(n, 0), "gat_eT2": lambda n: gat_eT(n, 2),
                "edge_hg": lambda n: copy(n, hg[:], b0[:], "edge_gathered", "edge_hg", "edge_outed"),
                "edge_xz": lambda n: copy(n, xz[:], b1[:, 0:E], "edge_x", "edge_xz", "edge_lcol"),
                "edge_exp": edge_exp,
                "edge_yT": lambda n: copy(n, YT[:], b0[:], "edge_scattered", "edge_yT", "edge_outed"),
                "cheb_hT": lambda n: copy(n, h3T[:], c3[:], "cheb_turned", "cheb_hT", "cheb_g"),
                "cheb_gf": lambda n: (freed(act, "cheb_gm", n),
                                      copy(n, flat(gf), c3[:], "cheb_g", "cheb_gf", "cheb_glo")),
                "cheb_x1T": lambda n: copy(n, x1T[:], c3[:], "x1_turned", "cheb_x1T", "cheb_v"),
                "cheb_qsplit": lambda n: (need(act, sem("parts3"), n * 128),
                                          copy(n, qk_hi[0][:], c3[:], "cheb_q", "q_hi")),
                "cheb_ksplit": lambda n: copy(n, qk_hi[1][:], c3[:], "cheb_k", "k_hi"),
                "cheb_vout": lambda n: (freed(act, "v_stored", n, 16), copy(n, flat(vS), c3[:], "cheb_v", "v_out")),
                "ffn_x2T": lambda n: copy(n, x2T, b0[:], "ffn_turned", "ffn_x2T", "ffn_downed"),
                "ffn_gelu": ffn_gelu,
            }, att)

        @block.vector
        def _(dve):
            def gat_stats(n):
                ready(dve, "gat_loaded", n, 16, 16)
                ln_stats(dve, "gat", n, xA)

            def gat_apply(n):
                freed(dve, "gat_turned", n)
                ln_apply(dve, "gat", n, xA, zA)

            def gat_wh_out(n):
                ready(dve, "gat_s1", n)
                nc.vector.tensor_copy(gat_small[:, 0, :], a0[:, 0:NT]).then_inc(sem("gat_s1s"), 1)

            def gat_scores(n):
                freed(dve, "gat_eturn", n, NT)
                ready_alone(dve, "gat_s2", n)
                for t in range(NT):
                    nc.vector.tensor_tensor_reduce(gat_T[:, t, :], a1[:], k.mask_gat[:, t, :], 1.0, -HUGE, ALU.add,
                                                   ALU.max, gat_small[:, 1, t:t + 1]).then_inc(sem("gat_T"), 1)
                s = gat_small
                ready(dve, "gat_T", n, NT, NT)
                ready(dve, "gat_s1s", n)
                nc.vector.tensor_tensor(s[:, 2, :], s[:, 0, :], s[:, 1, :], ALU.add).then_inc(sem("gat_small"), 1)
                ready(dve, "gat_small", n, 1, 4)
                nc.vector.scalar_tensor_tensor(s[:, 3, :], s[:, 2, :], 0.2, s[:, 2, :], ALU.mult, ALU.max
                                               ).then_inc(sem("gat_small"), 1)
                ready(dve, "gat_small", n, 2, 4)
                nc.vector.tensor_tensor(s[:, 4, :], s[:, 0, :], s[:, 3, :], ALU.subtract
                                        ).then_inc(sem("gat_small"), 1)
                nc.vector.tensor_scalar(s[:, 5, :], s[:, 0, :], -0.8, None, ALU.mult).then_inc(sem("gat_small"), 1)

            def gat_max(n):
                for t in range(NT):
                    ready(dve, "gat_low", n, t + 1, NT)
                    nc.vector.tensor_tensor(gat_V[:, t, :], gat_T[:, t, :], gat_V[:, t, :], ALU.max
                                            ).then_inc(sem("gat_max"), 1)

            def gat_x2(n):
                ready(dve, "gat_exp", n, NT, NT)
                nc.vector.reciprocal(gat_small[:, 7, :], gat_small[:, 6, :]).then_inc(sem("gat_rinv"), 1)
                ready(dve, "gat_rinv", n)
                ready(dve, "gat_pv", n)
                freed(dve, "edge_done", n)
                for t in range(NT):
                    nc.vector.scalar_tensor_tensor(x2[:, t, :], a0[:, cols(t)], gat_small[:, 7, t:t + 1],
                                                   xA[:, t, :], ALU.mult, ALU.add).then_inc(sem("gat_done"), 1)

            def edge_stats(n):
                ready(dve, "gat_done", n, NT, NT)
                ln_stats(dve, "edge", n, x2)

            def relu(n, tag, x):
                ready(dve, tag + "_normed", n, NT, NT)
                nc.vector.tensor_scalar(x[:], x[:], 0.0, None, ALU.max).then_inc(sem(tag + "_h"), 1)

            def edge_apply(n):
                freed(dve, "edge_gathered", n)
                ln_apply(dve, "edge", n, x2, h2)
                relu(n, "edge", h2)

            def edge_z(n):
                ready(dve, "edge_xz", n)
                nc.vector.scalar_tensor_tensor(zT[:], xz[:], 0.2, xz[:], ALU.mult, ALU.max
                                               ).then_inc(sem("edge_z"), 1)

            def edge_max(n):
                for h in range(H):
                    if h % 2 == 0:
                        ready_alone(dve, "edge_lb", n, h // 2 + 1, 2)
                    for e in range(ET):
                        nc.vector.tensor_tensor_reduce(
                            edge_junk[:, e * H + h, :], [b0, b1][h // 2][:, (h % 2) * E:(h % 2) * E + E],
                            k.seg_bias[:, e, :], 1.0, -HUGE, ALU.add, ALU.max,
                            edge_small[:, 0, e * H + h:e * H + h + 1]).then_inc(sem("edge_max"), 1)

            def edge_le(n):
                ready(dve, "edge_max", n, ET * H, ET * H)
                ready(dve, "edge_lcol", n)
                for e in range(ET):
                    r = slice(e * H, e * H + H)
                    nc.vector.scalar_tensor_tensor(edge_small[:, 1, r], b0[:, r], k.logA[:, e:e + 1],
                                                   edge_small[:, 0, r], ALU.add, ALU.subtract
                                                   ).then_inc(sem("edge_le"), 1)

            def edge_u(n):
                ready(dve, "edge_den", n)
                nc.vector.reciprocal(edge_small[:, 3, :], b0[:, 0:ET * H]).then_inc(sem("edge_rden"), 1)
                ready(dve, "edge_rden", n)
                nc.vector.tensor_tensor(edge_small[:, 4, :], edge_small[:, 2, :], edge_small[:, 3, :], ALU.mult
                                        ).then_inc(sem("edge_attn"), 1)
                ready(dve, "edge_attn", n)
                ready(dve, "edge_v", n)
                freed(dve, "edge_scattered", n)
                nc.vector.tensor_tensor(U[:].rearrange("p (g d) -> p g d", d=HD),
                                        b1[:, 0:ET * D].rearrange("p (g d) -> p g d", d=HD),
                                        edge_small[:, 4, :].unsqueeze(2).broadcast_to([P, ET * H, HD]), ALU.mult
                                        ).then_inc(sem("edge_u"), 1)

            def edge_x3(n):
                ready(dve, "edge_outed", n)
                freed(dve, "x3_stored", n, 16)
                freed(dve, "cheb_normed", n, NT)
                nc.vector.tensor_tensor(flat(x3), b1[:], flat(x2), ALU.add).then_inc(sem("edge_done"), 1)

            def cheb_stats(n):
                ready(dve, "edge_done", n)
                ln_stats(dve, "cheb", n, x3)

            def cheb_apply(n):
                freed(dve, "cheb_turned", n)
                freed(dve, "cheb_x1", n)
                ln_apply(dve, "cheb", n, x3, h3)
                relu(n, "cheb", h3)

            def cheb_split(n):
                ready(dve, "cheb_gf", n)
                freed(dve, "cheb_prop", n)
                nc.vector.tensor_copy(g_hi[:], flat(gf)).then_inc(sem("cheb_ghi"), 1)
                ready(dve, "cheb_ghi", n)
                nc.vector.tensor_tensor(g_lo[:], flat(gf), g_hi[:].bitcast(F32), ALU.subtract
                                        ).then_inc(sem("cheb_glo"), 1)

            def cheb_y(n):
                ready(dve, "cheb_prop", n)
                ready(dve, "cheb_gm", n)
                nc.vector.scalar_tensor_tensor(flat(y1), c3[:], k.two_lam[:], flat(gm), ALU.mult, ALU.subtract
                                               ).then_inc(sem("cheb_y"), 1)
                ready(dve, "cheb_y", n)
                ln_stats(dve, "n1", n, y1)

            def n1_apply(n):
                ln_apply(dve, "n1", n, y1, y1)

            def cheb_x1(n):
                ready(dve, "n1_aff", n, 2, 2)
                freed(dve, "x1_turned", n)
                freed(dve, "res_stored", n, 16)
                nc.vector.scalar_tensor_tensor(flat(x1), flat(y1), 0.0, flat(h3), ALU.max, ALU.add
                                               ).then_inc(sem("cheb_x1"), 1)

            def split_lo(n, which):
                name = "qk"[which]
                ready(dve, name + "_hi", n)
                need(dve, sem("parts3"), n * 128)
                nc.vector.tensor_tensor(qk_lo[which][:], c3[:], qk_hi[which][:].bitcast(F32), ALU.subtract
                                        ).then_inc(sem(name + "_lo"), 1)

            def att(n, j):
                if j < TILES:
                    need(dve, sem("att_exp"), n * TILES + j + 1 - RING_T)
                    ready_alone(dve, "att_score", n, j + 1, TILES)
                    nc.vector.tensor_tensor_reduce(att_T[:, j % RING_T, :], [c0, c1][j % 2][:],
                                                   k.mask_att[:, j % NT, :], -QK_SCALE, HUGE, ALU.add, ALU.min,
                                                   att_small[:, 0, j:j + 1]).then_inc(sem("att_T"), 1)
                if 1 <= j <= TILES:
                    ready(dve, "att_exp", n, j, TILES)
                    nc.vector.reciprocal(att_small[:, 2, j - 1:j], att_small[:, 1, j - 1:j]
                                         ).then_inc(sem("att_rv"), 1)

            def ffn_y2(n):
                ready(dve, "ffn_wo", n)
                ready(dve, "ffn_res", n)
                nc.vector.tensor_tensor(flat(y2), b1[:], flat(xrE), ALU.add).then_inc(sem("ffn_y2"), 1)
                ready(dve, "ffn_y2", n)
                ln_stats(dve, "n2", n, y2)

            def n2_apply(n):
                ln_apply(dve, "n2", n, y2, y2)

            def ffn_y3(n):
                ready(dve, "ffn_downed", n)
                ready(dve, "ffn_x2b", n)
                freed(dve, "out_stored", n, 16)
                nc.vector.tensor_tensor(flat(y3), b0[:], flat(y2), ALU.add).then_inc(sem("ffn_y3"), 1)
                ready(dve, "ffn_y3", n)
                ln_stats(dve, "n3", n, y3)

            def n3_apply(n):
                ln_apply(dve, "n3", n, y3, y3)

            def ffn_final(n):
                ready(dve, "n3_aff", n, 2, 2)
                ready(dve, "ffn_x3", n, 16, 16)
                nc.vector.tensor_tensor(flat(y3), flat(y3), flat(x3E), ALU.add).then_inc(sem("ffn_fin"), 1)

            run(dve, dve.Fori, {
                "gat_stats": gat_stats, "gat_apply": gat_apply, "gat_wh_out": gat_wh_out, "gat_scores": gat_scores,
                "gat_max": gat_max, "gat_x2": gat_x2,
                "edge_stats": edge_stats, "edge_apply": edge_apply, "edge_z": edge_z, "edge_max": edge_max,
                "edge_le": edge_le, "edge_u": edge_u, "edge_x3": edge_x3,
                "cheb_stats": cheb_stats, "cheb_apply": cheb_apply, "cheb_split": cheb_split, "cheb_y": cheb_y,
                "n1_apply": n1_apply, "cheb_x1": cheb_x1,
                "cheb_qsplit": lambda n: split_lo(n, 0), "cheb_ksplit": lambda n: split_lo(n, 1),
                "ffn_y2": ffn_y2, "n2_apply": n2_apply, "ffn_y3": ffn_y3, "n3_apply": n3_apply,
                "ffn_final": ffn_final,
            }, att)

        @block.tensor
        def _(pe):
            def turn(dst, src):
                for t in range(NT):
                    mm = nc.tensor.transpose(dst[:, cols(t)], src[:, t, :], k.ident[:])
                return mm

            def by_nodes(dst, left, right):
                for t in range(NT):
                    mm = nc.tensor.matmul(dst[:, cols(t)], left[:, cols(t)], right, start=True, stop=True)
                return mm

            def one(dst, left, right):
                return nc.tensor.matmul(dst, left, right, start=True, stop=True)

            def gat_turn(n):
                ready(pe, "gat_normed", n, NT, NT)
                freed(pe, "gat_done", n, NT)
                turn(a0, zA).then_inc(sem("gat_turned"), 1)

            def gat_wh(n):
                ready(pe, "gat_hT", n)
                freed(pe, "gat_eT", n, NT)
                by_nodes(a1, hTA, W["W1g"][:]).then_inc(sem("gat_wh"), 1)
                for t in range(NT):
                    mm = one(a0[:, t:t + 1], hTA[:, cols(t)], k.gat_a[:, 0:1])
                mm.then_inc(sem("gat_s1"), 1)

            def gat_s2(n):
                ready(pe, "gat_whs", n)
                one(a1[:], k.gat_a2b[:], hTA[:]).then_inc(sem("gat_s2"), 1)

            def gat_eturn(n, t0):
                for t in (t0, t0 + 1):
                    ready(pe, "gat_exp", n, t + 1, NT)
                    if t == 0:
                        ready(pe, "gat_s1s", n)
                    elif t == 1:
                        ready(pe, "gat_T", n, NT, NT)
                    else:
                        ready(pe, "gat_eT", n, t - 1, NT)
                    for s in range(NT):
                        mm = nc.tensor.transpose([a0, a1][t % 2][:, cols(s)], gat_E[:, t, cols(s)], k.ident[:])
                    mm.then_inc(sem("gat_eturn"), 1)

            def gat_pv(n):
                ready(pe, "gat_eT", n, NT, NT)
                for t in range(NT):
                    for s in range(NT):
                        mm = nc.tensor.matmul(a0[:, cols(t)], gat_ET[:, s, cols(t)], WhA[:, s, :], start=(s == 0),
                                              stop=(s == NT - 1))
                mm.then_inc(sem("gat_pv"), 1)

            def edge_gather(n):
                ready(pe, "edge_h", n)
                need(pe, sem("ffn_y3"), min(n - 2, B) if isinstance(n, int) else n - 2)
                freed(pe, "edge_yT", n)
                for t in range(NT):
                    mm = nc.tensor.matmul(b0[:], h2[:, t, :], k.edge_pick[:, t, :], start=(t == 0),
                                          stop=(t == NT - 1))
                mm.then_inc(sem("edge_gathered"), 1)

            def edge_x(n):
                ready(pe, "edge_hg", n)
                freed(pe, "edge_done", n)
                one(b1[:, 0:E], W["WlinT"][:], hg[:, 0:E]).then_inc(sem("edge_x"), 1)

            def edge_lb(n):
                ready(pe, "edge_z", n)
                for h in range(H):
                    mm = one([b0, b1][h // 2][:, (h % 2) * E:(h % 2) * E + E], k.head_a[:, h, :], zT[:])
                    if h % 2:
                        mm.then_inc(sem("edge_lb"), 1)

            def edge_lcol(n):
                ready(pe, "edge_max", n, ET * H, ET * H)
                for e in range(ET):
                    mm = one(b0[:, e * H:e * H + H], zT[:, cols(e)], k.head_a4[:])
                mm.then_inc(sem("edge_lcol"), 1)
                for e in range(ET):
                    mm = one(b1[:, cols(e)], hg[:, E + e * P:E + (e + 1) * P], W["WvalT"][:])
                mm.then_inc(sem("edge_v"), 1)

            def edge_den(n):
                ready(pe, "edge_exp", n)
                for e in range(ET):
                    for f in range(ET):
                        mm = nc.tensor.matmul(b0[:, e * H:e * H + H], k.same_src[:, f, cols(e)],
                                              edge_small[:, 2, f * H:f * H + H], start=(f == 0), stop=(f == ET - 1))
                mm.then_inc(sem("edge_den"), 1)

            def edge_scatter(n):
                ready(pe, "edge_u", n)
                for e in range(ET):
                    mm = nc.tensor.matmul(b0[:], U[:, cols(e)], k.src_rows[:, e, :], start=(e == 0),
                                          stop=(e == ET - 1))
                mm.then_inc(sem("edge_scattered"), 1)

            def edge_out(n):
                ready(pe, "edge_yT", n)
                by_nodes(b1, YT, W["WoutT"][:]).then_inc(sem("edge_outed"), 1)

            def cheb_turn(n):
                ready(pe, "cheb_h", n)
                freed(pe, "v_out", n)
                turn(c3, h3).then_inc(sem("cheb_turned"), 1)

            def cheb_g(n):
                ready(pe, "cheb_hT", n)
                by_nodes(c3, h3T, W["Wc"][:]).then_inc(sem("cheb_g"), 1)

            def cheb_prop(n):
                ready(pe, "cheb_glo", n)
                for t in range(NT):
                    for s in range(NT):
                        for i, (left, right) in enumerate([(k.adjT_hi, g_hi), (k.adjT_hi, g_lo), (k.adjT_lo, g_hi)]):
                            mm = nc.tensor.matmul(c3[:, cols(t)], left[:, s, cols(t)], right[:, cols(s)],
                                                  start=(s == 0 and i == 0), stop=(s == NT - 1 and i == 2))
                mm.then_inc(sem("cheb_prop"), 1)

            def cheb_x1turn(n):
                ready(pe, "cheb_x1", n)
                turn(c3, x1).then_inc(sem("x1_turned"), 1)

            def cheb_q(n):
                ready(pe, "cheb_x1T", n)
                one(c3[:], W["Wq"][:], x1T[:]).then_inc(sem("cheb_q"), 1)

            def cheb_k(n):
                ready(pe, "q_lo", n)
                one(c3[:], W["Wk"][:], x1T[:]).then_inc(sem("cheb_k"), 1)

            def cheb_v(n):
                ready(pe, "k_lo", n)
                by_nodes(c3, x1T, W["Wv"][:]).then_inc(sem("cheb_v"), 1)

            def att(n, j):
                if j < TILES:
                    h, t = j // NT, j % NT
                    if t == 0:
                        ready(pe, f"parts{h}", n, 128, 128)
                    need(pe, sem("att_T"), n * TILES + j - 1)
                    one([c0, c1][j % 2][:], Qs[:, h, cols(t)], Ks[:, h, :]).then_inc(sem("att_score"), 1)
                i = j - 2
                if 0 <= i < TILES:
                    if i == 0:
                        freed(pe, "att_oT", n)
                    ready(pe, "att_norm", n, i + 1, TILES)
                    need(pe, sem("att_pt"), n * TILES + i)
                    for s in range(NT):
                        mm = nc.tensor.transpose(c2[:, cols(s)], att_E[:, i % RING_E, cols(s)], k.ident[:])
                    mm.then_inc(sem("att_turn"), 1)
                if j == TILES + 2:
                    ready(pe, "att_pt", n, TILES, TILES)
                    ready(pe, "att_v", n, 16, 16)
                    for s in range(NT):
                        for h in range(H):
                            r = slice(HD * h, HD * (h + 1))
                            mm = nc.tensor.matmul(c2[r, :], vD[:, s, r], att_PT[:, h, s, :], start=(s == 0),
                                                  stop=(s == NT - 1))
                    mm.then_inc(sem("att_pv"), 1)

            def ffn_wo(n):
                ready(pe, "att_oT", n)
                need(pe, sem("edge_done"), min(n + 3, B) if isinstance(n, int) else n + 3)
                by_nodes(b1, oT, W["Wo"][:]).then_inc(sem("ffn_wo"), 1)

            def ffn_turn(n):
                ready(pe, "n2_aff", n, 2, 2)
                turn(b0, y2).then_inc(sem("ffn_turned"), 1)

            def ffn_up(n):
                ready(pe, "ffn_x2T", n)
                for q in range(2):
                    one([b0, b1][q][:], k.W1[:, cols(q)], x2T).then_inc(sem("ffn_up"), 1)

            def ffn_down(n):
                ready(pe, "ffn_gelu", n, 2, 2)
                for t in range(NT):
                    for q in range(2):
                        mm = nc.tensor.matmul(b0[:, cols(t)], mT[:, q, cols(t)], k.W2[:, q, :], start=(q == 0),
                                              stop=(q == 1))
                mm.then_inc(sem("ffn_downed"), 1)

            run(pe, pe.Fori, {
                "gat_turn": gat_turn, "gat_wh": gat_wh, "gat_s2": gat_s2, "gat_eturn0": lambda n: gat_eturn(n, 0),
                "gat_eturn2": lambda n: gat_eturn(n, 2), "gat_pv": gat_pv,
                "edge_gather": edge_gather, "edge_x": edge_x, "edge_lb": edge_lb, "edge_lcol": edge_lcol,
                "edge_den": edge_den, "edge_scatter": edge_scatter, "edge_out": edge_out,
                "cheb_turn": cheb_turn, "cheb_g": cheb_g, "cheb_prop": cheb_prop, "cheb_x1turn": cheb_x1turn,
                "cheb_q": cheb_q, "cheb_k": cheb_k, "cheb_v": cheb_v,
                "ffn_wo": ffn_wo, "ffn_turn": ffn_turn, "ffn_up": ffn_up, "ffn_down": ffn_down,
            }, att)


_INS = {"x": "x", "adj": "adj", "alpha": "L0_gnn_alpha_train", "w": "L0_gnn_w", "d": "L0_gnn_d",
        "fcw": "L0_gnn_fc_in_w", "fcb": "L0_gnn_fc_in_b", "W1g": "L1_gnn_W", "ag": "L1_gnn_a",
        "Wlin": "L2_gnn_W_lin", "Wval": "L2_gnn_W_val", "aL2": "L2_gnn_a", "Wout": "L2_gnn_W_out",
        "src": "L2_gnn_src", "dst": "L2_gnn_dst"} | {n: "L3_gnn_" + n for n in NAMES[15:]}


def kernel(**inputs):
    import numpy as np
    import concourse.bacc as bacc
    from concourse.bass_utils import run_bass_kernel_spmd as run

    nc = bacc.Bacc("TRN2", target_bir_lowering=False, num_devices=1)
    arrays, t_in = {}, {}
    for name in NAMES:
        a = np.ascontiguousarray(inputs[_INS[name]])
        arrays["in_" + name] = a
        t_in[name] = nc.dram_tensor("in_" + name, a.shape, mybir.dt.from_np(a.dtype), kind="ExternalInput").ap()
    out = nc.dram_tensor("out_x", (B, N, D), F32, kind="ExternalOutput").ap()
    build(nc, t_in, out)
    r = run(nc, [arrays], core_ids=[0])
    return r.results[0]["out_x"]
```

```python
from contextlib import ExitStack
from math import comb

import concourse.bass as bass
from concourse import mybir

F32 = mybir.dt.float32
R32 = mybir.dt.float32r
I32 = mybir.dt.int32
BF16 = mybir.dt.bfloat16
ALU = mybir.AluOpType
ACT = mybir.ActivationFunctionType
AX = mybir.AxisListType.X

B, N, D = 16, 512, 128
P = 128
NT = N // P
H = 4
HD = D // H
E = 256
ET = E // P
HID = 2 * D
EPS = 1e-5
STEPS = 8
DT = 1.0 / STEPS
HB = B // 2
CB = 4
NC = HB // CB
SQUARINGS = 9
BIG = 1.0e30
HUGE = 3.0e38
QK_SCALE = float(HD) ** -0.5
MASKED = -1.0e9

NAMES = ["x", "adj", "alpha", "w", "d", "fcw", "fcb", "W1g", "ag", "Wlin", "Wval", "aL2", "Wout", "src", "dst",
         "Wc", "bc", "g1", "be1", "Wq", "Wk", "Wv", "Wo", "bo", "g2", "be2", "W1", "b1", "W2", "b2", "g3", "be3"]
ROWS = ["fcb", "bc", "g1", "be1", "bo", "g2", "be2", "b2", "g3", "be3"]


def need(eng, sem, value):
    if isinstance(value, int) and value <= 0:
        return
    eng.wait_ge(sem, value)


class Shared(dict):
    __getattr__ = dict.__getitem__


def build(nc, t_in, out):
    ctx = ExitStack()
    with ctx:
        def sb(name, shape, dt=F32, c=None):
            return (c or ctx).enter_context(nc.sbuf_tensor(name, shape, dt))

        sems, part = {}, ["start"]

        def sem(name):
            if name not in sems:
                sems[name] = nc.alloc_semaphore(f"{name}_{part[0]}")
            return sems[name]

        bank = [ctx.enter_context(nc.psum_tensor(f"bank{i}", [P, 512], F32)) for i in range(8)]
        x1_dram = nc.dram_tensor("x_after_l0", (B, N, D), F32, kind="Internal").ap()
        x3_dram = nc.dram_tensor("x_after_l2", (B, N, D), F32, kind="Internal").ap()
        res_dram = nc.dram_tensor("attn_residual", (B, N, D), F32, kind="Internal").ap()
        v_dram = nc.dram_tensor("values", (B, N, D), F32, kind="Internal").ap()

        def nodes1(ap, b):
            return ap[bass.ds(b, 1)].rearrange("o (t p) d -> p (o t) d", p=P)

        ident = sb("ident", [P, P])
        ones = sb("ones", [P, P])
        adjT_hi = sb("adjT_hi", [P, NT, N], R32)
        adjT_lo = sb("adjT_lo", [P, NT, N], R32)
        mask_gat = sb("mask_gat", [P, NT, N], BF16)
        mask_att = sb("mask_att", [P, NT, N], BF16)
        edge_pick = sb("edge_pick", [P, NT, 2 * E])
        src_rows = sb("src_rows", [P, ET, N])
        seg_bias = sb("seg_bias", [P, ET, E])
        same_src = sb("same_src", [P, ET, E])
        logA = sb("logA", [P, ET])
        W = {n: sb("w_" + n, [P, D]) for n in ["W1g", "Wc", "Wq", "Wk", "Wv", "Wo", "WlinT", "WvalT", "WoutT"]}
        W1 = sb("w_W1", [P, HID])
        W2 = sb("w_W2", [P, 2, D])
        rowv = sb("rowv", [P, len(ROWS), D])
        row = {n: rowv[:, i, :] for i, n in enumerate(ROWS)}
        b1c = sb("b1c", [P, 2])
        neg_half = sb("neg_half", [P, NT])
        gat_a = sb("gat_a", [P, 2])
        gat_a2b = sb("gat_a2b", [P, P])
        head_a = sb("head_a", [P, H, P])
        head_a4 = sb("head_a4", [P, H])
        two_lam = sb("two_lam", [P, 1])

        def row4(name, c=NT):
            return row[name].unsqueeze(1).broadcast_to([P, c, D])

        k = Shared(t_in=t_in, out=out, bank=bank, sem=sem, nodes1=nodes1, row=row, row4=row4, W=W, W1=W1, W2=W2,
                   x1_dram=x1_dram, x3_dram=x3_dram, res_dram=res_dram, v_dram=v_dram, rowv=rowv, b1c=b1c,
                   ident=ident, ones=ones, neg_half=neg_half, adjT_hi=adjT_hi, adjT_lo=adjT_lo, mask_gat=mask_gat,
                   mask_att=mask_att, edge_pick=edge_pick, src_rows=src_rows, seg_bias=seg_bias,
                   same_src=same_src, logA=logA, gat_a=gat_a, gat_a2b=gat_a2b, head_a=head_a, head_a4=head_a4,
                   two_lam=two_lam)

        one = ExitStack()
        with one:
            def s1(name, shape, dt=F32):
                return sb(name, shape, dt, one)

            adj = s1("adj", [P, NT, N])
            PT_hi = s1("PT_hi", [P, NT, N], R32)
            PT_lo = s1("PT_lo", [P, NT, N], R32)
            G = s1("G", [P, STEPS + 1, D])
            x0T = s1("x0T", [P, B, N])
            gb = s1("gb", [P, STEPS + 1, D])
            k_one = Shared(k, adj=adj, PT_hi=PT_hi, PT_lo=PT_lo, G=G, x0T=x0T, gb=gb)
            build_tables(nc, k_one)
            build_layer0(nc, k_one)

        nc.all_engine_barrier()
        nc.clear_and_free_semaphores(list(sems.values()))
        sems.clear()
        part[0] = "layers"
        nc.all_engine_barrier()

        build_layers(nc, k)


def build_tables(nc, k):
    t_in, bank, sem, W, row = k.t_in, k.bank, k.sem, k.W, k.row
    with ExitStack() as c:
        def sb(name, shape, dt=F32):
            return c.enter_context(nc.sbuf_tensor(name, shape, dt))

        asym = sb("asym", [P, NT, N])
        adjT = sb("adjT", [P, NT, N])
        P_row = k.x0T[:, HB:HB + NT, :]
        PT = k.x0T[:, HB + NT:HB + 2 * NT, :]
        S = [sb(f"S{i}", [P, NT, N], R32) for i in range(2)]
        sqr = sb("sqr", [P, NT * N])
        raw = {n: sb("raw_" + n, [P, D]) for n in ["w", "fcw", "Wlin", "Wval", "Wout"]}
        wT = sb("wT", [P, D])
        wTd = sb("wTd", [P, D])
        Rp = sb("Rp", [P, STEPS + 1, D])
        FR = sb("FR", [P, STEPS + 1, D])
        alpha = sb("alpha_c", [P, NT])
        sg = sb("sg", [P, 4, NT])
        dcol = sb("dcol", [P, 1])
        dclip = sb("dclip", [P, 1])
        fcb_col = sb("fcb_col", [P, 1])
        fcb_b = sb("fcb_b", [P, P])
        a_rows = sb("a_rows", [P, 2, D])
        acol = sb("acol", [P, 1])
        edge_i = sb("edge_i", [P, 2, E], I32)
        edge_f = sb("edge_f", [P, 2, E])
        edge_ci = sb("edge_ci", [P, 2, ET], I32)
        edge_c = sb("edge_c", [P, 2, ET])
        node_row = sb("node_row", [P, N])
        node_col = sb("node_col", [P, NT])
        pick_s = sb("pick_s", [P, NT, E])
        dst_rows = sb("dst_rows", [P, ET, N])
        a0e = sb("a0e", [P, ET])
        logAb = sb("logAb", [P, ET, P])
        junk = sb("junk", [P, ET, N])
        junk2 = sb("junk2", [P, 4, D])
        ssq = sb("ssq", [P, SQUARINGS])
        nrm = sb("nrm", [P, SQUARINGS])
        vec = sb("vec", [P, 3, NT])
        dots = sb("dots", [P, 2])
        lam = sb("lam", [P, 4])
        tiny = sb("tiny", [P, 1])

        loads = [
            (k.adj[:], t_in["adj"].rearrange("(t p) m -> p t m", p=P)),
            (raw["w"][:], t_in["w"]), (raw["fcw"][:], t_in["fcw"]), (raw["Wlin"][:], t_in["Wlin"]),
            (raw["Wval"][:], t_in["Wval"]), (raw["Wout"][:], t_in["Wout"]),
            (W["W1g"][:], t_in["W1g"]), (W["Wc"][:], t_in["Wc"]), (W["Wq"][:], t_in["Wq"]),
            (W["Wk"][:], t_in["Wk"]), (W["Wv"][:], t_in["Wv"]), (W["Wo"][:], t_in["Wo"]),
            (k.W1[:], t_in["W1"]), (k.W2[:], t_in["W2"].rearrange("(k p) d -> p k d", p=P)),
            (alpha[:], t_in["alpha"].rearrange("(t p) -> p t", p=P)),
            (dcol[:], t_in["d"].rearrange("(p o) -> p o", o=1)),
            (fcb_col[:], t_in["fcb"].rearrange("(p o) -> p o", o=1)),
            (k.b1c[:], t_in["b1"].rearrange("(k p) -> p k", p=P)),
            (a_rows[:].rearrange("p a d -> p (a d)"), t_in["ag"].rearrange("f o -> (f o)").partition_broadcast(P)),
            (acol[:], t_in["aL2"].rearrange("h (e o) -> (h e) o", o=1)),
            (edge_i[:, 0, :], t_in["src"].partition_broadcast(P)),
            (edge_i[:, 1, :], t_in["dst"].partition_broadcast(P)),
            (edge_ci[:, 0, :], t_in["src"].rearrange("(t p) -> p t", p=P)),
            (edge_ci[:, 1, :], t_in["dst"].rearrange("(t p) -> p t", p=P)),
        ] + [(k.rowv[:, i, :], t_in[n].partition_broadcast(P)) for i, n in enumerate(ROWS)]
        LOADED = 16 * len(loads)

        block = c.enter_context(nc.Block())

        @block.sync
        def _(sp):
            for dst, src in loads:
                sp.dma_start(dst, src, allow_slow_non_contiguous=True).then_inc(sem("tables_loaded"), 16)

        @block.gpsimd
        def _(pool):
            nc.gpsimd.memset(k.ones[:], 1.0).then_inc(sem("zeroed"), 1)
            nc.gpsimd.memset(k.ident[:], 0.0).then_inc(sem("zeroed"), 1)
            nc.gpsimd.memset(k.head_a[:], 0.0).then_inc(sem("zeroed"), 1)
            nc.gpsimd.memset(k.head_a4[:], 0.0).then_inc(sem("zeroed"), 1)
            nc.gpsimd.memset(tiny[:], 1e-8).then_inc(sem("zeroed"), 1)
            nc.gpsimd.memset(k.neg_half[:], -0.5).then_inc(sem("zeroed"), 1)
            pool.wait_ge(sem("zeroed"), 6)
            nc.gpsimd.affine_select(out=k.ident[:], in_=k.ident[:], compare_op=ALU.not_equal, fill=1.0, base=0,
                                    pattern=[[-1, P]], channel_multiplier=1).then_inc(sem("ident_ready"), 1)
            nc.gpsimd.iota(node_row[:], [[1, N]], base=0, channel_multiplier=0,
                           allow_small_or_imprecise_dtypes=True).then_inc(sem("node_numbers"), 1)
            nc.gpsimd.iota(node_col[:], [[P, NT]], base=0, channel_multiplier=1,
                           allow_small_or_imprecise_dtypes=True).then_inc(sem("node_numbers"), 1)

        @block.scalar
        def _(act):
            act.wait_ge(sem("tables_loaded"), LOADED)
            nc.scalar.activation(sg[:, 0, :], alpha[:], ACT.Exp, scale=-1.0).then_inc(sem("exp_alpha"), 1)
            act.wait_ge(sem("edge_weight"), ET)
            act.wait_ge(sem("zeroed"), 5)
            nc.scalar.activation(k.logA[:], a0e[:], ACT.Ln, bias=tiny[:]).then_inc(sem("log_edge"), 1)
            for q in range(SQUARINGS):
                act.wait_ge(sem("square_scaled"), NT * q + 1)
                need(act, sem("norm_part"), q)
                nc.scalar.activation(sqr[:], S[q % 2][:].rearrange("p t m -> p (t m)").bitcast(F32), ACT.Square,
                                     accum_out=ssq[:, q:q + 1]).then_inc(sem("norm_part"), 1)

        @block.vector
        def _(dve):
            dve.wait_ge(sem("tables_loaded"), LOADED)
            dve.wait_ge(sem("zeroed"), 5)
            dve.wait_ge(sem("exp_alpha"), 1)
            nc.vector.tensor_scalar(sg[:, 1, :], sg[:, 0, :], 1.0, None, ALU.add).then_inc(sem("sig"), 1)
            dve.wait_ge(sem("sig"), 1)
            nc.vector.reciprocal(sg[:, 2, :], sg[:, 1, :]).then_inc(sem("sig"), 1)
            dve.wait_ge(sem("sig"), 2)
            nc.vector.tensor_scalar(sg[:, 3, :], sg[:, 2, :], DT / 2, None, ALU.mult).then_inc(sem("sig"), 1)
            nc.vector.tensor_scalar(dclip[:], dcol[:], 0.0, 1.0, ALU.max, ALU.min).then_inc(sem("dclip"), 1)
            nc.vector.tensor_scalar(fcb_b[:], k.ones[:], fcb_col[:], None, ALU.mult).then_inc(sem("fcb_wide"), 1)
            dve.wait_ge(sem("ident_ready"), 1)
            for t in range(NT):
                nc.vector.tensor_copy(P_row[:, t, :], k.adj[:, t, :]).then_inc(sem("p_row"), 1)
            dve.wait_ge(sem("p_row"), NT)
            for t in range(NT):
                nc.vector.tensor_tensor(P_row[:, t, t * P:(t + 1) * P], k.adj[:, t, t * P:(t + 1) * P], k.ident[:],
                                        ALU.subtract).then_inc(sem("p_row"), 1)
            dve.wait_ge(sem("p_row"), 2 * NT)
            dve.wait_ge(sem("sig"), 3)
            for t in range(NT):
                nc.vector.tensor_scalar(P_row[:, t, :], P_row[:, t, :], sg[:, 3, t:t + 1], None,
                                        ALU.mult).then_inc(sem("p_row"), 1)
            dve.wait_ge(sem("weights_turned"), 4)
            nc.vector.tensor_copy(wT[:], bank[0][:, 0:P]).then_inc(sem("wT"), 1)
            nc.vector.tensor_scalar(wTd[:], bank[0][:, 0:P], dclip[:], None, ALU.mult).then_inc(sem("wT"), 1)
            for i, n in enumerate(["WlinT", "WvalT", "WoutT"]):
                nc.vector.tensor_copy(W[n][:], bank[0][:, (i + 1) * P:(i + 2) * P]).then_inc(sem("wT"), 1)
            dve.wait_ge(sem("fc_turned"), 1)
            nc.vector.tensor_copy(FR[:, 0, :], bank[1][:, 0:P]).then_inc(sem("FR"), 1)
            for s in range(NT):
                dve.wait_ge(sem("adj_turned"), s + 1)
                nc.vector.tensor_copy(adjT[:, s, :], bank[4 + s][:]).then_inc(sem("adjT"), 1)
            for s in range(NT):
                dve.wait_ge(sem("p_turned"), s + 1)
                nc.vector.tensor_copy(PT[:, s, :], bank[4 + s][:]).then_inc(sem("PT"), 1)
            dve.wait_ge(sem("adjT"), NT)
            nc.vector.tensor_tensor(asym[:], k.adj[:], adjT[:], ALU.add).then_inc(sem("asym"), 1)
            dve.wait_ge(sem("asym"), 1)
            nc.vector.tensor_scalar(asym[:], asym[:], 0.5, None, ALU.mult).then_inc(sem("asym"), 1)
            dve.wait_ge(sem("asym"), 2)
            nc.vector.tensor_copy(S[0][:], asym[:]).then_inc(sem("square_scaled"), 1)
            dve.wait_ge(sem("w_eff"), 1)
            nc.vector.tensor_scalar(Rp[:, 1, :], bank[1][:, P:2 * P], DT, None, ALU.mult).then_inc(sem("R_half"), 1)
            nc.vector.tensor_copy(Rp[:, 0, :], k.ident[:]).then_inc(sem("R_half"), 1)
            dve.wait_ge(sem("R_half"), 2)
            nc.vector.scalar_tensor_tensor(Rp[:, 1, :], k.ident[:], 1.0 - DT, Rp[:, 1, :], ALU.mult,
                                           ALU.add).then_inc(sem("R_power"), 1)
            for q, (lo, hi) in enumerate([(2, 2), (3, 4), (5, 8)]):
                dve.wait_ge(sem("R_product"), q + 1)
                nc.vector.tensor_copy(Rp[:, lo:hi + 1, :],
                                      bank[2][:, 0:(hi - lo + 1) * D].rearrange("p (k d) -> p k d", d=D)
                                      ).then_inc(sem("R_power"), 1)
            for q in range(2):
                dve.wait_ge(sem("FR_product"), q + 1)
                nc.vector.tensor_copy(FR[:, 1 + 4 * q:5 + 4 * q, :], bank[q][:].rearrange("p (k d) -> p k d", d=D)
                                      ).then_inc(sem("FR"), 1)
            nc.vector.tensor_copy(k.gb[:, 0, :], row["fcb"]).then_inc(sem("gb"), 1)
            for q in range(2):
                dve.wait_ge(sem("bR_product"), q + 1)
                for m in range(4):
                    i = 1 + 4 * q + m
                    nc.vector.tensor_scalar(k.gb[:, i, :], bank[2 + q][:, m * D:(m + 1) * D], float(comb(STEPS, i)),
                                            None, ALU.mult).then_inc(sem("gb"), 1)
            dve.wait_ge(sem("FR"), 3)
            done = 0
            for i in range(STEPS + 1):
                nc.vector.tensor_scalar(k.G[:, i, :], FR[:, i, :], float(comb(STEPS, i)), None,
                                        ALU.mult).then_inc(sem("G_sum"), 1)
                done += 1
            dve.wait_ge(sem("R_power"), 4)
            for m in range(STEPS):
                dve.wait_ge(sem("G_sum"), done)
                for i in range(m + 1, STEPS + 1):
                    nc.vector.scalar_tensor_tensor(k.G[:, i, :], Rp[:, m, :], DT * comb(STEPS - i + m, STEPS - i),
                                                   k.G[:, i, :], ALU.mult, ALU.add).then_inc(sem("G_sum"), 1)
                    done += 1
            dve.wait_ge(sem("G_sum"), done)
            dve.wait_ge(sem("PT"), NT)
            nc.vector.tensor_copy(k.PT_hi[:], PT).then_inc(sem("split_hi"), 1)
            nc.vector.tensor_copy(k.adjT_hi[:], adjT[:]).then_inc(sem("split_hi"), 1)
            dve.wait_ge(sem("split_hi"), 2)
            nc.vector.tensor_tensor(k.PT_lo[:], PT, k.PT_hi[:].bitcast(F32), ALU.subtract
                                    ).then_inc(sem("split_lo"), 1)
            nc.vector.tensor_tensor(k.adjT_lo[:], adjT[:], k.adjT_hi[:].bitcast(F32), ALU.subtract
                                    ).then_inc(sem("split_lo"), 1)
            nc.vector.tensor_scalar(k.mask_gat[:], k.adj[:], 0.0, -BIG, ALU.is_equal, ALU.mult
                                    ).then_inc(sem("masks"), 1)
            nc.vector.tensor_scalar(k.mask_att[:], k.adj[:], 0.0, MASKED / QK_SCALE, ALU.is_le, ALU.mult
                                    ).then_inc(sem("masks"), 1)
            for q in range(2):
                nc.vector.tensor_tensor_reduce(junk2[:, q, :], W["W1g"][:], a_rows[:, q, :], 1.0, 0.0, ALU.mult,
                                               ALU.add, k.gat_a[:, q:q + 1]).then_inc(sem("gat_a"), 1)
            dve.wait_ge(sem("gat_a"), 2)
            nc.vector.tensor_scalar(k.gat_a2b[:], k.ones[:], k.gat_a[:, 1:2], None, ALU.mult
                                    ).then_inc(sem("gat_a"), 1)
            for h in range(H):
                r = slice(HD * h, HD * h + HD)
                nc.vector.tensor_copy(k.head_a4[r, h:h + 1], acol[r, :]).then_inc(sem("head_a"), 1)
                nc.vector.tensor_scalar(k.head_a[r, h, :], k.ones[r, :], acol[r, :], None, ALU.mult
                                        ).then_inc(sem("head_a"), 1)
            nc.vector.tensor_copy(edge_f[:], edge_i[:]).then_inc(sem("edge_f"), 1)
            nc.vector.tensor_copy(edge_c[:], edge_ci[:]).then_inc(sem("edge_f"), 1)
            dve.wait_ge(sem("edge_f"), 2)
            dve.wait_ge(sem("node_numbers"), 2)
            for t in range(NT):
                nc.vector.tensor_scalar(pick_s[:, t, :], edge_f[:, 0, :], node_col[:, t:t + 1], None, ALU.is_equal
                                        ).then_inc(sem("pick"), 1)
                nc.vector.tensor_scalar(k.edge_pick[:, t, E:], edge_f[:, 1, :], node_col[:, t:t + 1], None,
                                        ALU.is_equal).then_inc(sem("pick"), 1)
            dve.wait_ge(sem("pick"), 2 * NT)
            nc.vector.tensor_tensor(k.edge_pick[:, :, 0:E], pick_s[:], k.edge_pick[:, :, E:], ALU.add
                                    ).then_inc(sem("pick"), 1)
            for e in range(ET):
                nc.vector.tensor_scalar(k.src_rows[:, e, :], node_row[:], edge_c[:, 0, e:e + 1], None, ALU.is_equal
                                        ).then_inc(sem("rows"), 1)
                nc.vector.tensor_scalar(dst_rows[:, e, :], node_row[:], edge_c[:, 1, e:e + 1], None, ALU.is_equal
                                        ).then_inc(sem("rows"), 1)
                nc.vector.tensor_scalar(k.same_src[:, e, :], edge_f[:, 0, :], edge_c[:, 0, e:e + 1], None,
                                        ALU.is_equal).then_inc(sem("rows"), 1)
            dve.wait_ge(sem("rows"), 3 * ET)
            for e in range(ET):
                dve.wait_ge(sem("adj_picked"), e + 1)
                nc.vector.tensor_tensor_reduce(junk[:, e, :], bank[2 + e][:], dst_rows[:, e, :], 1.0, 0.0, ALU.mult,
                                               ALU.add, a0e[:, e:e + 1]).then_inc(sem("edge_weight"), 1)
            nc.vector.tensor_scalar(k.seg_bias[:], k.same_src[:], BIG, -BIG, ALU.mult, ALU.add
                                    ).then_inc(sem("seg"), 1)
            dve.wait_ge(sem("log_edge"), 1)
            for e in range(ET):
                nc.vector.tensor_scalar(logAb[:, e, :], k.ones[:], k.logA[:, e:e + 1], None, ALU.mult
                                        ).then_inc(sem("logAb"), 1)
            dve.wait_ge(sem("seg"), 1)
            dve.wait_ge(sem("log_row"), 1)
            for e in range(ET):
                nc.vector.tensor_tensor(k.seg_bias[:, e, :], k.seg_bias[:, e, :], bank[0][:, 0:E], ALU.add
                                        ).then_inc(sem("seg"), 1)
            for q in range(SQUARINGS):
                dve.wait_ge(sem("norm_sum"), q + 1)
                nc.vector.reciprocal(nrm[:, q:q + 1], bank[0][:, q:q + 1] if q else bank[0][:, 0:1]
                                     ).then_inc(sem("nrm"), 1)
                dve.wait_ge(sem("nrm"), q + 1)
                for t in range(NT):
                    dve.wait_ge(sem("square"), NT * q + t + 1)
                    nc.vector.tensor_scalar(S[(q + 1) % 2][:, t, :], bank[4 + t][:], nrm[:, q:q + 1], None,
                                            ALU.mult).then_inc(sem("square_scaled"), 1)
            dve.wait_ge(sem("square_scaled"), NT * SQUARINGS + 1)
            nc.vector.tensor_reduce(vec[:, 0, :], S[SQUARINGS % 2][:].bitcast(F32), AX, ALU.add
                                    ).then_inc(sem("vec"), 1)
            for q in range(2):
                dve.wait_ge(sem("A_vec"), q + 1)
                nc.vector.tensor_copy(vec[:, q + 1, :], bank[1][:, 0:NT]).then_inc(sem("vec"), 1)
            dve.wait_ge(sem("vec"), 3)
            for q in range(2):
                nc.vector.tensor_tensor_reduce(junk2[:, 2 + q, 0:NT], vec[:, 1, :], vec[:, 2 - q, :], 1.0, 0.0,
                                               ALU.mult, ALU.add, dots[:, q:q + 1]).then_inc(sem("dots"), 1)
            dve.wait_ge(sem("dot_sums"), 1)
            nc.vector.reciprocal(lam[:, 0:1], bank[2][:, 1:2]).then_inc(sem("lam"), 1)
            dve.wait_ge(sem("lam"), 1)
            nc.vector.tensor_tensor(lam[:, 1:2], lam[:, 0:1], bank[2][:, 0:1], ALU.mult).then_inc(sem("lam"), 1)
            dve.wait_ge(sem("lam"), 2)
            nc.vector.tensor_scalar(lam[:, 2:3], lam[:, 1:2], 1e-8, None, ALU.add).then_inc(sem("lam"), 1)
            dve.wait_ge(sem("lam"), 3)
            nc.vector.reciprocal(lam[:, 3:4], lam[:, 2:3]).then_inc(sem("lam"), 1)
            dve.wait_ge(sem("lam"), 4)
            nc.vector.tensor_scalar(k.two_lam[:], lam[:, 3:4], 2.0, None, ALU.mult).then_inc(sem("lam"), 1)

        @block.tensor
        def _(pe):
            pe.wait_ge(sem("tables_loaded"), LOADED)
            pe.wait_ge(sem("ident_ready"), 1)
            for i, n in enumerate(["w", "Wlin", "Wval", "Wout"]):
                nc.tensor.transpose(bank[0][:, i * P:(i + 1) * P], raw[n][:], k.ident[:]
                                    ).then_inc(sem("weights_turned"), 1)
            nc.tensor.transpose(bank[1][:, 0:P], raw["fcw"][:], k.ident[:]).then_inc(sem("fc_turned"), 1)
            for s in range(NT):
                for t in range(NT):
                    mm = nc.tensor.transpose(bank[4 + s][:, t * P:(t + 1) * P], k.adj[:, t, s * P:(s + 1) * P],
                                             k.ident[:])
                mm.then_inc(sem("adj_turned"), 1)
            pe.wait_ge(sem("p_row"), 3 * NT)
            for s in range(NT):
                pe.wait_ge(sem("adjT"), s + 1)
                for t in range(NT):
                    mm = nc.tensor.transpose(bank[4 + s][:, t * P:(t + 1) * P], P_row[:, t, s * P:(s + 1) * P],
                                             k.ident[:])
                mm.then_inc(sem("p_turned"), 1)
            pe.wait_ge(sem("wT"), 5)
            pe.wait_ge(sem("FR"), 1)
            nc.tensor.matmul(bank[1][:, P:2 * P], wTd[:], wT[:], start=True, stop=True).then_inc(sem("w_eff"), 1)
            for q, (left, lo, hi) in enumerate([(1, 1, 1), (2, 1, 2), (4, 1, 4)]):
                pe.wait_ge(sem("R_power"), q + 1)
                nc.tensor.matmul(bank[2][:, 0:(hi - lo + 1) * D], Rp[:, left, :],
                                 Rp[:, lo:hi + 1, :], start=True, stop=True
                                 ).then_inc(sem("R_product"), 1)
            pe.wait_ge(sem("R_power"), 4)
            for q in range(2):
                nc.tensor.matmul(bank[q][:], raw["fcw"][:], Rp[:, 1 + 4 * q:5 + 4 * q, :], start=True, stop=True
                                 ).then_inc(sem("FR_product"), 1)
            pe.wait_ge(sem("fcb_wide"), 1)
            for q in range(2):
                nc.tensor.matmul(bank[2 + q][:], fcb_b[:], Rp[:, 1 + 4 * q:5 + 4 * q, :], start=True, stop=True
                                 ).then_inc(sem("bR_product"), 1)
            pe.wait_ge(sem("pick"), 2 * NT)
            pe.wait_ge(sem("gb"), STEPS + 1)
            for e in range(ET):
                for t in range(NT):
                    mm = nc.tensor.matmul(bank[2 + e][:], pick_s[:, t, e * P:(e + 1) * P], k.adj[:, t, :],
                                          start=(t == 0), stop=(t == NT - 1))
                mm.then_inc(sem("adj_picked"), 1)
            pe.wait_ge(sem("logAb"), ET)
            pe.wait_ge(sem("FR"), 3)
            for e in range(ET):
                mm = nc.tensor.matmul(bank[0][:, e * P:(e + 1) * P], logAb[:, e, :], k.ident[:], start=True, stop=True)
            mm.then_inc(sem("log_row"), 1)
            pe.wait_ge(sem("PT"), NT)
            pe.wait_ge(sem("seg"), 1 + ET)
            for q in range(SQUARINGS):
                pe.wait_ge(sem("norm_part"), q + 1)
                need(pe, sem("nrm"), q)
                nc.tensor.matmul(bank[0][:, q:q + 1], k.ones[:], ssq[:, q:q + 1], start=True, stop=True
                                 ).then_inc(sem("norm_sum"), 1)
                pe.wait_ge(sem("square_scaled"), NT * q + 1)
                for t in range(NT):
                    for s in range(NT):
                        mm = nc.tensor.matmul(bank[4 + t][:], S[q % 2][:, s, t * P:(t + 1) * P], S[q % 2][:, s, :],
                                              start=(s == 0), stop=(s == NT - 1))
                    mm.then_inc(sem("square"), 1)
            for q in range(2):
                pe.wait_ge(sem("vec"), q + 1)
                for t in range(NT):
                    for s in range(NT):
                        mm = nc.tensor.matmul(bank[1][:, t:t + 1], asym[:, s, t * P:(t + 1) * P],
                                              vec[:, q, s:s + 1], start=(s == 0), stop=(s == NT - 1))
                mm.then_inc(sem("A_vec"), 1)
            pe.wait_ge(sem("dots"), 2)
            nc.tensor.matmul(bank[2][:, 0:2], k.ones[:], dots[:], start=True, stop=True).then_inc(sem("dot_sums"), 1)




def build_layer0(nc, k):
    t_in, bank, sem, x0T = k.t_in, k.bank, k.sem, k.x0T
    LEVELS = STEPS + 1
    PAIRS = HB // 2
    with ExitStack() as c:
        def sb(name, shape, dt=F32):
            return c.enter_context(nc.sbuf_tensor(name, shape, dt))

        xin = [sb(f"l0_x{u}", [P, NT, D]) for u in range(2)]
        stats = sb("l0_stats", [P, 2, NT, 6])
        mv = sb("l0_mv", [P, 2, NT, 2])
        rs = sb("l0_rs", [P, 2, 2, NT])
        z = [sb(f"l0_z{u}", [P, NT, D]) for u in range(2)]
        Z_hi = sb("Z_hi", [P, NT, HB * D], R32)
        Z_lo = sb("Z_lo", [P, NT, HB * D], R32)
        zs = sb("l0_sum", [P, NC, NT, CB * D])
        xres = sb("l0_res", [P, NT, CB * D])

        block = c.enter_context(nc.Block())

        def chunk_dram(ap, half, ch, t):
            b0 = half * HB + ch * CB
            return ap[b0:b0 + CB, t * P:(t + 1) * P, :].rearrange("b p d -> p b d")

        def load(sp, u, use, b):
            sp.wait_ge(sem(f"l0_normed{u}"), use * NT + 1)
            sp.dma_start(xin[u][:], k.nodes1(t_in["x"], b)).then_inc(sem(f"l0_loaded{u}"), 16)

        def statistics(dve, u, use):
            dve.wait_ge(sem(f"l0_loaded{u}"), (use + 1) * 16)
            for t in range(NT):
                nc.vector.bn_stats(stats[:, u, t, :], xin[u][:, t, :]).then_inc(sem(f"l0_stats{u}"), 1)
            wait_alone(dve, sem(f"l0_stats{u}"), (use + 1) * NT, sem("waits_passed"))
            for t in range(NT):
                nc.vector.bn_aggr(mv[:, u, t, :], stats[:, u, t, :]).then_inc(sem(f"l0_aggr{u}"), 1)

        def rstd(pool, u, use):
            wait_alone(pool, sem(f"l0_aggr{u}"), (use + 1) * NT, sem("waits_passed"))
            nc.gpsimd.tensor_scalar(rs[:, u, 0, :], mv[:, u, :, 1], EPS, None, ALU.add
                                    ).then_inc(sem(f"l0_vareps{u}"), 1)
            pool.wait_ge(sem(f"l0_vareps{u}"), use + 1)
            nc.gpsimd.tensor_tensor(rs[:, u, 1, :], rs[:, u, 0, :], k.neg_half[:], ALU.pow
                                    ).then_inc(sem(f"l0_rstd{u}"), 1)

        def normalise(dve, u, use):
            dve.wait_ge(sem(f"l0_rstd{u}"), use + 1)
            dve.wait_ge(sem(f"l0_turned{u}"), use + 1)
            for t in range(NT):
                nc.vector.tensor_scalar(z[u][:, t, :], xin[u][:, t, :], mv[:, u, t, 0:1], rs[:, u, 1, t:t + 1],
                                        ALU.subtract, ALU.mult).then_inc(sem(f"l0_normed{u}"), 1)

        def turn(pe, u, use, dst):
            pe.wait_ge(sem(f"l0_normed{u}"), (use + 1) * NT + 1)
            pe.wait_ge(sem(f"l0_x0{u}"), use + 1)
            for t in range(NT):
                mm = nc.tensor.transpose(dst[:, t * P:(t + 1) * P], z[u][:, t, :], k.ident[:])
            mm.then_inc(sem(f"l0_turned{u}"), 1)

        def keep(act, u, use, src, b):
            act.wait_ge(sem(f"l0_turned{u}"), use + 2)
            nc.scalar.activation(x0T[:, bass.ds(b, 1), :].rearrange("p o n -> p (o n)"), src[:], ACT.Relu
                                 ).then_inc(sem(f"l0_x0{u}"), 1)

        @block.sync
        def _(sp):
            with sp.Fori(0, PAIRS) as pair:
                for u in range(2):
                    load(sp, u, pair, pair * 2 + u)
            with sp.Fori(0, HB) as b:
                load(sp, 0, b + PAIRS, b + HB)
            for half in range(2):
                for ch in range(NC):
                    for t in range(NT):
                        need(sp, sem(f"l0_stored{t}"), (half * NC + ch) * 16)
                        sp.dma_start(xres[:, t, :].rearrange("p (b d) -> p b d", d=D),
                                     chunk_dram(t_in["x"], half, ch, t)).then_inc(sem(f"l0_res{t}"), 16)
                    for t in range(NT):
                        sp.wait_ge(sem(f"l0_final{t}"), half * NC + ch + 1)
                        sp.dma_start(chunk_dram(k.x1_dram, half, ch, t),
                                     xres[:, t, :].rearrange("p (b d) -> p b d", d=D)
                                     ).then_inc(sem(f"l0_stored{t}"), 16)
            for t in range(NT):
                sp.wait_ge(sem(f"l0_stored{t}"), 2 * NC * 16)

        @block.gpsimd
        def _(pool):
            for u in range(2):
                pool.sem_inc(sem(f"l0_turned{u}"))
                pool.sem_inc(sem(f"l0_normed{u}"))
                pool.sem_inc(sem(f"l0_x0{u}"))
            with pool.Fori(0, PAIRS) as pair:
                for u in range(2):
                    rstd(pool, u, pair)
            with pool.Fori(0, HB) as b:
                rstd(pool, 0, b + PAIRS)

        @block.scalar
        def _(act):
            def level(lev, half):
                for ch in range(NC):
                    act.wait_ge(sem(f"l0_level{ch}"), half * LEVELS * NT + lev * NT + NT)
                    for t in range(NT):
                        act.wait_ge(sem(f"l0_sum{ch}"), half * STEPS * NT + lev * NT + t + 1)
                        nc.scalar.copy(Z_hi[:, t, ch * CB * D:(ch + 1) * CB * D], zs[:, ch, t, :]
                                       ).then_inc(sem(f"l0_Zhi{ch}"), 1)

            with act.Fori(0, PAIRS) as pair:
                for u in range(2):
                    keep(act, u, pair, bank[u], pair * 2 + u)
            with act.Fori(0, STEPS) as lev:
                level(lev, 0)
                keep(act, 0, lev + PAIRS, bank[-1], lev + HB)
            with act.Fori(0, STEPS) as lev:
                level(lev, 1)

        @block.vector
        def _(dve):
            def sums(lev, half, ch):
                sl = slice(ch * CB * D, (ch + 1) * CB * D)
                for t in range(NT):
                    dve.wait_ge(sem(f"l0_level{ch}"), half * LEVELS * NT + lev * NT + t + 1)
                    nc.vector.tensor_tensor(zs[:, ch, t, :].rearrange("p (b d) -> p b d", d=D),
                                            bank[ch * NT + t][:].rearrange("p (b d) -> p b d", d=D),
                                            k.gb[:, bass.ds(lev, 1), :].broadcast_to([P, CB, D]),
                                            ALU.add).then_inc(sem(f"l0_sum{ch}"), 1)
                for t in range(NT):
                    dve.wait_ge(sem(f"l0_Zhi{ch}"), half * STEPS * NT + lev * NT + t + 1)
                    nc.vector.tensor_tensor(Z_lo[:, t, sl], zs[:, ch, t, :], Z_hi[:, t, sl].bitcast(F32),
                                            ALU.subtract).then_inc(sem(f"l0_Zlo{ch}"), 1)

            def end(half):
                for ch in range(NC):
                    for t in range(NT):
                        dve.wait_ge(sem(f"l0_level{ch}"), (half + 1) * LEVELS * NT - NT + t + 1)
                        nc.vector.tensor_tensor(zs[:, ch, t, :].rearrange("p (b d) -> p b d", d=D),
                                                bank[ch * NT + t][:].rearrange("p (b d) -> p b d", d=D),
                                                k.gb[:, LEVELS - 1:LEVELS, :].broadcast_to([P, CB, D]),
                                                ALU.add).then_inc(sem(f"l0_last{ch}"), 1)
                        dve.wait_ge(sem(f"l0_last{ch}"), half * NT + t + 1)
                        dve.wait_ge(sem(f"l0_res{t}"), (half * NC + ch + 1) * 16)
                        nc.vector.tensor_tensor(xres[:, t, :], zs[:, ch, t, :], xres[:, t, :], ALU.add
                                                ).then_inc(sem(f"l0_final{t}"), 1)

            with dve.Fori(0, PAIRS) as pair:
                for u in range(2):
                    statistics(dve, u, pair)
                for u in range(2):
                    normalise(dve, u, pair)
            with dve.Fori(0, STEPS) as lev:
                statistics(dve, 0, lev + PAIRS)
                sums(lev, 0, 0)
                normalise(dve, 0, lev + PAIRS)
                sums(lev, 0, 1)
            end(0)
            with dve.Fori(0, STEPS) as lev:
                for ch in range(NC):
                    sums(lev, 1, ch)
            end(1)

        @block.tensor
        def _(pe):
            def x0_times(half, ch, t, g, first):
                for b in range(CB):
                    mm = nc.tensor.matmul(bank[ch * NT + t][:, b * D:(b + 1) * D],
                                          x0T[:, half * HB + ch * CB + b, t * P:(t + 1) * P], g, start=first,
                                          stop=first or b == CB - 1)
                mm.then_inc(sem(f"l0_level{ch}"), 1)

            def p_times(ch, t):
                sl = slice(ch * CB * D, (ch + 1) * CB * D)
                n0 = slice(t * P, (t + 1) * P)
                for s in range(NT):
                    for i, (left, right) in enumerate([(k.PT_hi, Z_hi), (k.PT_hi, Z_lo), (k.PT_lo, Z_hi)]):
                        nc.tensor.matmul(bank[ch * NT + t][:], left[:, s, n0], right[:, s, sl],
                                         start=(s == 0 and i == 0), stop=False)

            with pe.Fori(0, PAIRS) as pair:
                for u in range(2):
                    turn(pe, u, pair, bank[u])
            for half in range(2):
                for ch in range(NC):
                    for t in range(NT):
                        if half == 0 and ch == 0 and t < 2:
                            pe.wait_ge(sem(f"l0_x0{t}"), PAIRS + 1)
                        elif half == 1:
                            pe.wait_ge(sem(f"l0_last{ch}"), t + 1)
                            pe.wait_ge(sem("l0_x00"), PAIRS + HB + 1)
                        x0_times(half, ch, t, k.G[:, 0, :], True)
                with pe.Fori(1, LEVELS) as lev:
                    for ch in range(NC):
                        pe.wait_ge(sem(f"l0_Zlo{ch}"), half * STEPS * NT + lev * NT)
                        for t in range(NT):
                            if half == 0 and ch == 1 and t == 0:
                                pe.wait_ge(sem("l0_sum1"), lev * NT)
                                turn(pe, 0, lev + PAIRS - 1, bank[-1])
                            elif half == 0 and ch == 1 and t == NT - 1:
                                pe.wait_ge(sem("l0_x00"), lev + PAIRS + 1)
                            p_times(ch, t)
                            x0_times(half, ch, t, k.G[:, bass.ds(lev, 1), :].rearrange("p o d -> p (o d)"), False)


def wait_alone(eng, semaphore, value, passed):
    need(eng, semaphore, value)
    if not isinstance(value, int):
        eng.sem_inc(passed)


STAGES = ["gat", "edge", "cheb", "att", "ffn"]
LAG = {s: i for i, s in enumerate(STAGES)}
TILES = H * NT
RING_T, RING_E = 3, 4

SCHEDULE = [
    (-1, "cheb", "cheb_rstd"), (-1, "edge", "edge_stats"), (-1, "gat", "load_x"), (-1, "cheb", "cheb_stats"),
    (2, "ffn", "ffn_wo"), (2, "edge", "edge_rstd"), (2, "ffn", "ffn_res"), (2, "cheb", "cheb_apply"),
    (2, "cheb", "cheb_hT"), (2, "gat", "gat_stats"), (2, "gat", "gat_rstd"),
    (3, "ffn", "n2_rstd"), (3, "ffn", "ffn_y2"), (3, "cheb", "cheb_turn"), (3, "cheb", "cheb_g"),
    (3, "gat", "gat_apply"), (3, "cheb", "cheb_gf"), (3, "ffn", "n2_apply"), (3, "ffn", "n2_affine"),
    (3, "gat", "gat_turn"), (3, "gat", "gat_hT"), (3, "gat", "gat_wh_out"),
    (4, "gat", "gat_wh"), (4, "gat", "gat_s2"),
    (6, "cheb", "cheb_split"), (6, "gat", "gat_scores"), (6, "edge", "edge_apply"), (6, "ffn", "ffn_x2T"),
    (6, "gat", "gat_low"), (6, "ffn", "ffn_gelu"), (6, "ffn", "ffn_turn"),
    (7, "gat", "gat_exp"), (7, "ffn", "load_ffn"), (7, "ffn", "ffn_up"), (7, "cheb", "cheb_prop"),
    (7, "ffn", "ffn_down"), (7, "gat", "gat_max"), (7, "cheb", "cheb_gm"), (7, "cheb", "cheb_y"),
    (7, "ffn", "ffn_b2"), (7, "gat", "gat_eturn0"), (7, "cheb", "n1_rstd"), (7, "gat", "gat_eT0"),
    (7, "ffn", "ffn_y3"), (7, "cheb", "n1_apply"), (7, "cheb", "n1_affine"),
    (8, "edge", "edge_hg"), (8, "att", "load_v"), (8, "edge", "edge_gather"),
    (9, "edge", "edge_xz"), (9, "cheb", "cheb_x1"), (9, "cheb", "cheb_x1T"), (9, "edge", "edge_x"),
    (9, "cheb", "cheb_x1turn"),
    (10, "cheb", "cheb_q"), (10, "edge", "edge_z"), (10, "ffn", "n3_rstd"), (10, "gat", "gat_eturn2"),
    (10, "cheb", "cheb_qsplit"), (10, "cheb", "stack1"),
    (11, "ffn", "n3_apply"), (11, "ffn", "n3_affine"), (11, "cheb", "cheb_ksplit"), (11, "cheb", "stack2"),
    (11, "cheb", "cheb_k"), (11, "gat", "gat_eT2"), (11, "edge", "edge_lb"),
    (12, "edge", "edge_max"), (12, "cheb", "cheb_res"), (12, "gat", "gat_pv"), (12, "edge", "edge_exp"),
    (12, "edge", "edge_le"),
    (13, "edge", "edge_lcol"), (13, "cheb", "cheb_v"),
    (14, "edge", "edge_u"), (14, "cheb", "stack0"), (14, "edge", "edge_den"), (14, "cheb", "cheb_vout"),
    (15, "edge", "edge_scatter"), (15, "edge", "edge_yT"), (15, "cheb", "stack3"),
    (17, "ffn", "ffn_final"), (17, "edge", "edge_x3"), (17, "edge", "edge_out"),
    (18, "edge", "edge_store"), (18, "gat", "gat_x2"),
]




def build_layers(nc, k):
    bank, sem, W, row4 = k.bank, k.sem, k.W, k.row4
    with ExitStack() as c:
        def sb(name, shape, dt=F32):
            return c.enter_context(nc.sbuf_tensor(name, shape, dt))

        def tile(name):
            return sb(name, [P, NT, D])

        ln_mem = {}
        for tag in ["gat", "edge", "cheb", "n1", "n2", "n3"]:
            ln_mem[tag] = (sb(tag + "_stat", [P, NT, 6]), sb(tag + "_mv", [P, NT, 2]), sb(tag + "_rs", [P, 2, NT]))
        xA, zA, WhA, x2 = tile("gat_xin"), tile("gat_z"), tile("gat_whs"), tile("x2")
        hTA = sb("gat_hTs", [P, N])
        gat_T, gat_V, gat_ET = (sb(n, [P, NT, N]) for n in ["gat_Ts", "gat_Vs", "gat_ETs"])
        gat_E = gat_T
        gat_small = sb("gat_small", [P, 8, NT])
        h2, x3 = tile("edge_hs"), tile("x3")
        hg = sb("edge_hgs", [P, 2 * E])
        xz = sb("edge_xzs", [P, E])
        zT = xz
        edge_junk = sb("edge_junk", [P, ET * H, E], BF16)
        edge_small = sb("edge_small", [P, 5, ET * H])
        U = sb("edge_us", [P, ET * D])
        YT = hg
        h3, gf, gm, y1, x1 = (tile("cheb_" + n) for n in ["hs", "gfs", "gms", "y1", "x1s"])
        h3T = x1T = sb("cheb_xTs", [P, N])
        g_hi, g_lo = sb("g_hi", [P, N], R32), sb("g_lo", [P, N], R32)
        qk_hi = [sb(f"{n}_hi", [P, N], R32) for n in "qk"]
        qk_lo = [sb(f"{n}_lo", [P, N], R32) for n in "qk"]
        vS, vD = tile("v_out"), tile("v_in")
        Qs, Ks = sb("Q_parts", [P, H, N], R32), sb("K_parts", [P, H, N], R32)
        att_T, att_E = sb("att_Ts", [P, RING_T, N]), sb("att_Es", [P, RING_E, N])
        att_PT = sb("att_PTs", [P, H, NT, N])
        att_small = sb("att_small", [P, 3, TILES])
        oT = sb("att_oTs", [P, N])
        xrE, y2, y3, x3E = (tile("ffn_" + n) for n in ["xr", "y2s", "y3s", "x3"])
        mT = sb("ffn_mT", [P, 2, N])
        x2T = mT[:, 1, :]

        a0, a1, b0, b1, c0, c1, c2, c3 = bank

        def cols(t):
            return slice(t * P, (t + 1) * P)

        def flat(x):
            return x[:].rearrange("p t d -> p (t d)")

        def ready(eng, name, n, count=1, per=1):
            need(eng, sem(name), n * per + count)

        def freed(eng, name, n, per=1):
            need(eng, sem(name), n * per)

        def ready_alone(eng, name, n, count=1, per=1):
            wait_alone(eng, sem(name), n * per + count, sem("waits_passed"))

        def freed_alone(eng, name, n, per=1):
            wait_alone(eng, sem(name), n * per, sem("waits_passed"))

        def ln_stats(dve, tag, n, src):
            stat, mv, _ = ln_mem[tag]
            for t in range(NT):
                nc.vector.bn_stats(stat[:, t, :], src[:, t, :]).then_inc(sem(tag + "_stat"), 1)
            ready_alone(dve, tag + "_stat", n, NT, NT)
            for t in range(NT):
                nc.vector.bn_aggr(mv[:, t, :], stat[:, t, :]).then_inc(sem(tag + "_aggr"), 1)

        def ln_rstd(pool, tag, n):
            _, mv, rs = ln_mem[tag]
            ready_alone(pool, tag + "_aggr", n, NT, NT)
            nc.gpsimd.tensor_scalar(rs[:, 0, :], mv[:, :, 1], EPS, None, ALU.add).then_inc(sem(tag + "_vareps"), 1)
            ready(pool, tag + "_vareps", n)
            nc.gpsimd.tensor_tensor(rs[:, 1, :], rs[:, 0, :], k.neg_half[:], ALU.pow).then_inc(sem(tag + "_rs"), 1)

        def ln_apply(dve, tag, n, src, dst):
            _, mv, rs = ln_mem[tag]
            ready(dve, tag + "_rs", n)
            for t in range(NT):
                nc.vector.tensor_scalar(dst[:, t, :], src[:, t, :], mv[:, t, 0:1], rs[:, 1, t:t + 1], ALU.subtract,
                                        ALU.mult).then_inc(sem(tag + "_normed"), 1)

        def affine(pool, tag, n, x, g, b):
            ready(pool, tag + "_normed", n, NT, NT)
            nc.gpsimd.tensor_tensor(x[:], x[:], row4(g), ALU.mult).then_inc(sem(tag + "_aff"), 1)
            ready(pool, tag + "_aff", n, 1, 2)
            nc.gpsimd.tensor_tensor(x[:], x[:], row4(b), ALU.add).then_inc(sem(tag + "_aff"), 1)

        def run(eng, fori, steps, att):
            def iteration(i):
                def n_of(stage):
                    n = i - LAG[stage]
                    return n if not isinstance(i, int) or 0 <= n < B else None

                at = 0
                for j in range(-1, TILES + 3):
                    if j >= 0 and att and n_of("att") is not None:
                        att(n_of("att"), j)
                    while at < len(SCHEDULE) and SCHEDULE[at][0] <= j:
                        _, stage, step = SCHEDULE[at]
                        if step in steps and n_of(stage) is not None:
                            steps[step](n_of(stage))
                        at += 1

            fill = len(STAGES)
            for i in range(fill):
                iteration(i)
            with fori(fill, B) as i:
                iteration(i)
            for i in range(B, B + fill - 1):
                iteration(i)

        block = c.enter_context(nc.Block())

        @block.sync
        def _(sp):
            def load_x(n):
                freed_alone(sp, "gat_done", n, NT)
                sp.dma_start(xA[:], k.nodes1(k.x1_dram, n)).then_inc(sem("gat_loaded"), 16)

            def store_x3(n):
                ready_alone(sp, "edge_done", n)
                sp.dma_start(k.nodes1(k.x3_dram, n), x3[:]).then_inc(sem("x3_stored"), 16)

            def store_res(n):
                ready_alone(sp, "cheb_x1", n)
                sp.dma_start(k.nodes1(k.res_dram, n), x1[:]).then_inc(sem("res_stored"), 16)

            def store_v(n):
                ready_alone(sp, "v_out", n)
                sp.dma_start(k.nodes1(k.v_dram, n), vS[:]).then_inc(sem("v_stored"), 16)

            def load_v(n):
                ready_alone(sp, "v_stored", n, 16, 16)
                freed_alone(sp, "att_pv", n)
                sp.dma_start(vD[:], k.nodes1(k.v_dram, n)).then_inc(sem("att_v"), 16)

            def stack(n, which, h):
                ready_alone(sp, f"{'qk'[which]}_lo", n)
                wait_alone(sp, sem("att_score"), n * TILES - TILES + NT * (h + 1), sem("waits_passed"))
                dst = [Qs, Ks][which]
                order = [[0, 0, 1, 1], [0, 1, 0, 1]][which]
                for g in range(4):
                    src = [qk_hi, qk_lo][order[g]][which]
                    sp.dma_start(dst[HD * g:HD * (g + 1), h, :].bitcast(F32), src[HD * h:HD * (h + 1), :].bitcast(F32)
                                 ).then_inc(sem(f"parts{h}"), 16)

            def load_ffn(n):
                ready_alone(sp, "res_stored", n, 16, 16)
                freed_alone(sp, "ffn_y2", n)
                sp.dma_start(xrE[:], k.nodes1(k.res_dram, n)).then_inc(sem("ffn_xr"), 16)
                ready_alone(sp, "x3_stored", n, 16, 16)
                freed_alone(sp, "ffn_fin", n)
                sp.dma_start(x3E[:], k.nodes1(k.x3_dram, n)).then_inc(sem("ffn_x3"), 16)

            def store_out(n):
                ready_alone(sp, "ffn_fin", n)
                sp.dma_start(k.nodes1(k.out, n), y3[:]).then_inc(sem("out_stored"), 16)

            def stack_head(h):
                def step(n):
                    for which in range(2):
                        stack(n, which, h)
                return step

            run(sp, sp.Fori, {
                "load_x": load_x, "load_v": load_v, "load_ffn": load_ffn, "cheb_res": store_res,
                "cheb_vout": store_v, "ffn_final": store_out, "edge_store": store_x3,
                "stack0": stack_head(0), "stack1": stack_head(1), "stack2": stack_head(2), "stack3": stack_head(3),
            }, None)
            for name in ["x3_stored", "res_stored", "v_stored", "out_stored"]:
                sp.wait_ge(sem(name), 16 * B)

        @block.gpsimd
        def _(pool):
            def gat_low(n):
                ready_alone(pool, "gat_small", n, 4, 4)
                wait_alone(pool, sem("gat_exp"), n * NT, sem("waits_passed"))
                for t in range(NT):
                    nc.gpsimd.tensor_scalar(gat_V[:, t, :], gat_T[:, t, :], 0.2, gat_small[:, 5, t:t + 1], ALU.mult,
                                            ALU.add).then_inc(sem("gat_low"), 1)

            def cheb_gm(n):
                ready(pool, "cheb_gf", n)
                freed(pool, "cheb_y", n)
                nc.gpsimd.tensor_tensor(gm[:], gf[:], row4("bc"), ALU.subtract).then_inc(sem("cheb_gm"), 1)

            def ffn_res(n):
                ready(pool, "ffn_xr", n, 16, 16)
                nc.gpsimd.tensor_tensor(xrE[:], xrE[:], row4("bo"), ALU.add).then_inc(sem("ffn_res"), 1)

            def n2_affine(n):
                affine(pool, "n2", n, y2, "g2", "be2")

            def ffn_b2(n):
                ready(pool, "ffn_turned", n)
                nc.gpsimd.tensor_tensor(y2[:], y2[:], row4("b2"), ALU.add).then_inc(sem("ffn_x2b"), 1)

            def att(n, j):
                j -= 1
                if not 0 <= j < TILES:
                    return
                ready_alone(pool, "att_rv", n, j + 1, TILES)
                e = att_E[:, j % RING_E, :]
                nc.gpsimd.tensor_scalar(e, e, att_small[:, 2, j:j + 1], 1.0, ALU.mult, ALU.mult
                                        ).then_inc(sem("att_norm"), 1)

            run(pool, pool.Fori, {
                "gat_low": gat_low, "cheb_gm": cheb_gm, "ffn_res": ffn_res, "n2_affine": n2_affine, "ffn_b2": ffn_b2,
                "gat_rstd": lambda n: ln_rstd(pool, "gat", n), "edge_rstd": lambda n: ln_rstd(pool, "edge", n),
                "cheb_rstd": lambda n: ln_rstd(pool, "cheb", n), "n1_rstd": lambda n: ln_rstd(pool, "n1", n),
                "n2_rstd": lambda n: ln_rstd(pool, "n2", n), "n3_rstd": lambda n: ln_rstd(pool, "n3", n),
                "n1_affine": lambda n: affine(pool, "n1", n, y1, "g1", "be1"),
                "n3_affine": lambda n: affine(pool, "n3", n, y3, "g3", "be3"),
            }, att)

        @block.scalar
        def _(act):
            def copy(n, dst, src, made, done, last_reader=None, func=ACT.Copy, **kw):
                ready(act, made, n)
                if last_reader:
                    freed(act, last_reader, n)
                nc.scalar.activation(dst, src, func, **kw).then_inc(sem(done), 1)

            def gat_exp(n):
                for t in range(NT):
                    ready(act, "gat_max", n, t + 1, NT)
                    nc.scalar.activation(gat_E[:, t, :], gat_V[:, t, :], ACT.Exp, bias=gat_small[:, 4, t:t + 1],
                                         accum_out=gat_small[:, 6, t:t + 1]).then_inc(sem("gat_exp"), 1)

            def gat_eT(n, t0):
                freed(act, "gat_pv", n)
                for t in (t0, t0 + 1):
                    ready(act, "gat_eturn", n, t + 1, NT)
                    nc.scalar.copy(gat_ET[:, :, cols(t)], [a0, a1][t % 2][:].rearrange("p (s q) -> p s q", q=P)
                                   ).then_inc(sem("gat_eT"), 1)

            def ffn_gelu(n):
                freed(act, "ffn_downed", n)
                for q in range(2):
                    ready(act, "ffn_up", n, q + 1, 2)
                    nc.scalar.activation(mT[:, q, :], [b0, b1][q][:], ACT.Gelu, bias=k.b1c[:, q:q + 1]
                                         ).then_inc(sem("ffn_gelu"), 1)

            def edge_exp(n):
                ready(act, "edge_le", n, ET, ET)
                nc.scalar.activation(edge_small[:, 2, :], edge_small[:, 1, :], ACT.Exp).then_inc(sem("edge_exp"), 1)

            def att(n, j):
                if j < TILES:
                    ready(act, "att_T", n, j + 1, TILES)
                    need(act, sem("att_turn"), n * TILES + j + 1 - RING_E)
                    nc.scalar.activation(att_E[:, j % RING_E, :], att_T[:, j % RING_T, :], ACT.Exp, scale=-1.0,
                                         bias=att_small[:, 0, j:j + 1], accum_out=att_small[:, 1, j:j + 1]
                                         ).then_inc(sem("att_exp"), 1)
                i = j - 2
                if 0 <= i < TILES:
                    ready(act, "att_turn", n, i + 1, TILES)
                    if i == 0:
                        freed(act, "att_pv", n)
                    nc.scalar.copy(att_PT[:, i // NT, :, cols(i % NT)], c2[:].rearrange("p (s q) -> p s q", q=P)
                                   ).then_inc(sem("att_pt"), 1)
                if j == TILES + 2:
                    copy(n, oT[:], c2[:], "att_pv", "att_oT", "ffn_wo")

            run(act, act.Fori, {
                "gat_hT": lambda n: copy(n, hTA[:], a0[:], "gat_turned", "gat_hT", "gat_s2", ACT.Relu),
                "gat_wh_out": lambda n: copy(n, flat(WhA), a1[:], "gat_wh", "gat_whs", "gat_pv"),
                "gat_exp": gat_exp, "gat_eT0": lambda n: gat_eT(n, 0), "gat_eT2": lambda n: gat_eT(n, 2),
                "edge_hg": lambda n: copy(n, hg[:], b0[:], "edge_gathered", "edge_hg", "edge_outed"),
                "edge_xz": lambda n: copy(n, xz[:], b1[:, 0:E], "edge_x", "edge_xz", "edge_lcol"),
                "edge_exp": edge_exp,
                "edge_yT": lambda n: copy(n, YT[:], b0[:], "edge_scattered", "edge_yT", "edge_outed"),
                "cheb_hT": lambda n: copy(n, h3T[:], c3[:], "cheb_turned", "cheb_hT", "cheb_g"),
                "cheb_gf": lambda n: (freed(act, "cheb_gm", n),
                                      copy(n, flat(gf), c3[:], "cheb_g", "cheb_gf", "cheb_glo")),
                "cheb_x1T": lambda n: copy(n, x1T[:], c3[:], "x1_turned", "cheb_x1T", "cheb_v"),
                "cheb_qsplit": lambda n: (need(act, sem("parts3"), n * 128),
                                          copy(n, qk_hi[0][:], c3[:], "cheb_q", "q_hi")),
                "cheb_ksplit": lambda n: copy(n, qk_hi[1][:], c3[:], "cheb_k", "k_hi"),
                "cheb_vout": lambda n: (freed(act, "v_stored", n, 16), copy(n, flat(vS), c3[:], "cheb_v", "v_out")),
                "ffn_x2T": lambda n: copy(n, x2T, b0[:], "ffn_turned", "ffn_x2T", "ffn_downed"),
                "ffn_gelu": ffn_gelu,
            }, att)

        @block.vector
        def _(dve):
            def gat_stats(n):
                ready(dve, "gat_loaded", n, 16, 16)
                ln_stats(dve, "gat", n, xA)

            def gat_apply(n):
                freed(dve, "gat_turned", n)
                ln_apply(dve, "gat", n, xA, zA)

            def gat_wh_out(n):
                ready(dve, "gat_s1", n)
                nc.vector.tensor_copy(gat_small[:, 0, :], a0[:, 0:NT]).then_inc(sem("gat_s1s"), 1)

            def gat_scores(n):
                freed(dve, "gat_eturn", n, NT)
                ready_alone(dve, "gat_s2", n)
                for t in range(NT):
                    nc.vector.tensor_tensor_reduce(gat_T[:, t, :], a1[:], k.mask_gat[:, t, :], 1.0, -HUGE, ALU.add,
                                                   ALU.max, gat_small[:, 1, t:t + 1]).then_inc(sem("gat_T"), 1)
                s = gat_small
                ready(dve, "gat_T", n, NT, NT)
                ready(dve, "gat_s1s", n)
                nc.vector.tensor_tensor(s[:, 2, :], s[:, 0, :], s[:, 1, :], ALU.add).then_inc(sem("gat_small"), 1)
                ready(dve, "gat_small", n, 1, 4)
                nc.vector.scalar_tensor_tensor(s[:, 3, :], s[:, 2, :], 0.2, s[:, 2, :], ALU.mult, ALU.max
                                               ).then_inc(sem("gat_small"), 1)
                ready(dve, "gat_small", n, 2, 4)
                nc.vector.tensor_tensor(s[:, 4, :], s[:, 0, :], s[:, 3, :], ALU.subtract
                                        ).then_inc(sem("gat_small"), 1)
                nc.vector.tensor_scalar(s[:, 5, :], s[:, 0, :], -0.8, None, ALU.mult).then_inc(sem("gat_small"), 1)

            def gat_max(n):
                for t in range(NT):
                    ready(dve, "gat_low", n, t + 1, NT)
                    nc.vector.tensor_tensor(gat_V[:, t, :], gat_T[:, t, :], gat_V[:, t, :], ALU.max
                                            ).then_inc(sem("gat_max"), 1)

            def gat_x2(n):
                ready(dve, "gat_exp", n, NT, NT)
                nc.vector.reciprocal(gat_small[:, 7, :], gat_small[:, 6, :]).then_inc(sem("gat_rinv"), 1)
                ready(dve, "gat_rinv", n)
                ready(dve, "gat_pv", n)
                freed(dve, "edge_done", n)
                for t in range(NT):
                    nc.vector.scalar_tensor_tensor(x2[:, t, :], a0[:, cols(t)], gat_small[:, 7, t:t + 1],
                                                   xA[:, t, :], ALU.mult, ALU.add).then_inc(sem("gat_done"), 1)

            def edge_stats(n):
                ready(dve, "gat_done", n, NT, NT)
                ln_stats(dve, "edge", n, x2)

            def relu(n, tag, x):
                ready(dve, tag + "_normed", n, NT, NT)
                nc.vector.tensor_scalar(x[:], x[:], 0.0, None, ALU.max).then_inc(sem(tag + "_h"), 1)

            def edge_apply(n):
                freed(dve, "edge_gathered", n)
                ln_apply(dve, "edge", n, x2, h2)
                relu(n, "edge", h2)

            def edge_z(n):
                ready(dve, "edge_xz", n)
                nc.vector.scalar_tensor_tensor(zT[:], xz[:], 0.2, xz[:], ALU.mult, ALU.max
                                               ).then_inc(sem("edge_z"), 1)

            def edge_max(n):
                for h in range(H):
                    if h % 2 == 0:
                        ready_alone(dve, "edge_lb", n, h // 2 + 1, 2)
                    for e in range(ET):
                        nc.vector.tensor_tensor_reduce(
                            edge_junk[:, e * H + h, :], [b0, b1][h // 2][:, (h % 2) * E:(h % 2) * E + E],
                            k.seg_bias[:, e, :], 1.0, -HUGE, ALU.add, ALU.max,
                            edge_small[:, 0, e * H + h:e * H + h + 1]).then_inc(sem("edge_max"), 1)

            def edge_le(n):
                ready(dve, "edge_max", n, ET * H, ET * H)
                ready(dve, "edge_lcol", n)
                for e in range(ET):
                    r = slice(e * H, e * H + H)
                    nc.vector.scalar_tensor_tensor(edge_small[:, 1, r], b0[:, r], k.logA[:, e:e + 1],
                                                   edge_small[:, 0, r], ALU.add, ALU.subtract
                                                   ).then_inc(sem("edge_le"), 1)

            def edge_u(n):
                ready(dve, "edge_den", n)
                nc.vector.reciprocal(edge_small[:, 3, :], b0[:, 0:ET * H]).then_inc(sem("edge_rden"), 1)
                ready(dve, "edge_rden", n)
                nc.vector.tensor_tensor(edge_small[:, 4, :], edge_small[:, 2, :], edge_small[:, 3, :], ALU.mult
                                        ).then_inc(sem("edge_attn"), 1)
                ready(dve, "edge_attn", n)
                ready(dve, "edge_v", n)
                freed(dve, "edge_scattered", n)
                nc.vector.tensor_tensor(U[:].rearrange("p (g d) -> p g d", d=HD),
                                        b1[:, 0:ET * D].rearrange("p (g d) -> p g d", d=HD),
                                        edge_small[:, 4, :].unsqueeze(2).broadcast_to([P, ET * H, HD]), ALU.mult
                                        ).then_inc(sem("edge_u"), 1)

            def edge_x3(n):
                ready(dve, "edge_outed", n)
                freed(dve, "x3_stored", n, 16)
                freed(dve, "cheb_normed", n, NT)
                nc.vector.tensor_tensor(flat(x3), b1[:], flat(x2), ALU.add).then_inc(sem("edge_done"), 1)

            def cheb_stats(n):
                ready(dve, "edge_done", n)
                ln_stats(dve, "cheb", n, x3)

            def cheb_apply(n):
                freed(dve, "cheb_turned", n)
                freed(dve, "cheb_x1", n)
                ln_apply(dve, "cheb", n, x3, h3)
                relu(n, "cheb", h3)

            def cheb_split(n):
                ready(dve, "cheb_gf", n)
                freed(dve, "cheb_prop", n)
                nc.vector.tensor_copy(g_hi[:], flat(gf)).then_inc(sem("cheb_ghi"), 1)
                ready(dve, "cheb_ghi", n)
                nc.vector.tensor_tensor(g_lo[:], flat(gf), g_hi[:].bitcast(F32), ALU.subtract
                                        ).then_inc(sem("cheb_glo"), 1)

            def cheb_y(n):
                ready(dve, "cheb_prop", n)
                ready(dve, "cheb_gm", n)
                nc.vector.scalar_tensor_tensor(flat(y1), c3[:], k.two_lam[:], flat(gm), ALU.mult, ALU.subtract
                                               ).then_inc(sem("cheb_y"), 1)
                ready(dve, "cheb_y", n)
                ln_stats(dve, "n1", n, y1)

            def n1_apply(n):
                ln_apply(dve, "n1", n, y1, y1)

            def cheb_x1(n):
                ready(dve, "n1_aff", n, 2, 2)
                freed(dve, "x1_turned", n)
                freed(dve, "res_stored", n, 16)
                nc.vector.scalar_tensor_tensor(flat(x1), flat(y1), 0.0, flat(h3), ALU.max, ALU.add
                                               ).then_inc(sem("cheb_x1"), 1)

            def split_lo(n, which):
                name = "qk"[which]
                ready(dve, name + "_hi", n)
                need(dve, sem("parts3"), n * 128)
                nc.vector.tensor_tensor(qk_lo[which][:], c3[:], qk_hi[which][:].bitcast(F32), ALU.subtract
                                        ).then_inc(sem(name + "_lo"), 1)

            def att(n, j):
                if j < TILES:
                    need(dve, sem("att_exp"), n * TILES + j + 1 - RING_T)
                    ready_alone(dve, "att_score", n, j + 1, TILES)
                    nc.vector.tensor_tensor_reduce(att_T[:, j % RING_T, :], [c0, c1][j % 2][:],
                                                   k.mask_att[:, j % NT, :], -QK_SCALE, HUGE, ALU.add, ALU.min,
                                                   att_small[:, 0, j:j + 1]).then_inc(sem("att_T"), 1)
                if 1 <= j <= TILES:
                    ready(dve, "att_exp", n, j, TILES)
                    nc.vector.reciprocal(att_small[:, 2, j - 1:j], att_small[:, 1, j - 1:j]
                                         ).then_inc(sem("att_rv"), 1)

            def ffn_y2(n):
                ready(dve, "ffn_wo", n)
                ready(dve, "ffn_res", n)
                nc.vector.tensor_tensor(flat(y2), b1[:], flat(xrE), ALU.add).then_inc(sem("ffn_y2"), 1)
                ready(dve, "ffn_y2", n)
                ln_stats(dve, "n2", n, y2)

            def n2_apply(n):
                ln_apply(dve, "n2", n, y2, y2)

            def ffn_y3(n):
                ready(dve, "ffn_downed", n)
                ready(dve, "ffn_x2b", n)
                freed(dve, "out_stored", n, 16)
                nc.vector.tensor_tensor(flat(y3), b0[:], flat(y2), ALU.add).then_inc(sem("ffn_y3"), 1)
                ready(dve, "ffn_y3", n)
                ln_stats(dve, "n3", n, y3)

            def n3_apply(n):
                ln_apply(dve, "n3", n, y3, y3)

            def ffn_final(n):
                ready(dve, "n3_aff", n, 2, 2)
                ready(dve, "ffn_x3", n, 16, 16)
                nc.vector.tensor_tensor(flat(y3), flat(y3), flat(x3E), ALU.add).then_inc(sem("ffn_fin"), 1)

            run(dve, dve.Fori, {
                "gat_stats": gat_stats, "gat_apply": gat_apply, "gat_wh_out": gat_wh_out, "gat_scores": gat_scores,
                "gat_max": gat_max, "gat_x2": gat_x2,
                "edge_stats": edge_stats, "edge_apply": edge_apply, "edge_z": edge_z, "edge_max": edge_max,
                "edge_le": edge_le, "edge_u": edge_u, "edge_x3": edge_x3,
                "cheb_stats": cheb_stats, "cheb_apply": cheb_apply, "cheb_split": cheb_split, "cheb_y": cheb_y,
                "n1_apply": n1_apply, "cheb_x1": cheb_x1,
                "cheb_qsplit": lambda n: split_lo(n, 0), "cheb_ksplit": lambda n: split_lo(n, 1),
                "ffn_y2": ffn_y2, "n2_apply": n2_apply, "ffn_y3": ffn_y3, "n3_apply": n3_apply,
                "ffn_final": ffn_final,
            }, att)

        @block.tensor
        def _(pe):
            def turn(dst, src):
                for t in range(NT):
                    mm = nc.tensor.transpose(dst[:, cols(t)], src[:, t, :], k.ident[:])
                return mm

            def by_nodes(dst, left, right):
                for t in range(NT):
                    mm = nc.tensor.matmul(dst[:, cols(t)], left[:, cols(t)], right, start=True, stop=True)
                return mm

            def one(dst, left, right):
                return nc.tensor.matmul(dst, left, right, start=True, stop=True)

            def gat_turn(n):
                ready(pe, "gat_normed", n, NT, NT)
                freed(pe, "gat_done", n, NT)
                turn(a0, zA).then_inc(sem("gat_turned"), 1)

            def gat_wh(n):
                ready(pe, "gat_hT", n)
                freed(pe, "gat_eT", n, NT)
                by_nodes(a1, hTA, W["W1g"][:]).then_inc(sem("gat_wh"), 1)
                for t in range(NT):
                    mm = one(a0[:, t:t + 1], hTA[:, cols(t)], k.gat_a[:, 0:1])
                mm.then_inc(sem("gat_s1"), 1)

            def gat_s2(n):
                ready(pe, "gat_whs", n)
                one(a1[:], k.gat_a2b[:], hTA[:]).then_inc(sem("gat_s2"), 1)

            def gat_eturn(n, t0):
                for t in (t0, t0 + 1):
                    ready(pe, "gat_exp", n, t + 1, NT)
                    if t == 0:
                        ready(pe, "gat_s1s", n)
                    elif t == 1:
                        ready(pe, "gat_T", n, NT, NT)
                    else:
                        ready(pe, "gat_eT", n, t - 1, NT)
                    for s in range(NT):
                        mm = nc.tensor.transpose([a0, a1][t % 2][:, cols(s)], gat_E[:, t, cols(s)], k.ident[:])
                    mm.then_inc(sem("gat_eturn"), 1)

            def gat_pv(n):
                ready(pe, "gat_eT", n, NT, NT)
                for t in range(NT):
                    for s in range(NT):
                        mm = nc.tensor.matmul(a0[:, cols(t)], gat_ET[:, s, cols(t)], WhA[:, s, :], start=(s == 0),
                                              stop=(s == NT - 1))
                mm.then_inc(sem("gat_pv"), 1)

            def edge_gather(n):
                ready(pe, "edge_h", n)
                need(pe, sem("ffn_y3"), min(n - 2, B) if isinstance(n, int) else n - 2)
                freed(pe, "edge_yT", n)
                for t in range(NT):
                    mm = nc.tensor.matmul(b0[:], h2[:, t, :], k.edge_pick[:, t, :], start=(t == 0),
                                          stop=(t == NT - 1))
                mm.then_inc(sem("edge_gathered"), 1)

            def edge_x(n):
                ready(pe, "edge_hg", n)
                freed(pe, "edge_done", n)
                one(b1[:, 0:E], W["WlinT"][:], hg[:, 0:E]).then_inc(sem("edge_x"), 1)

            def edge_lb(n):
                ready(pe, "edge_z", n)
                for h in range(H):
                    mm = one([b0, b1][h // 2][:, (h % 2) * E:(h % 2) * E + E], k.head_a[:, h, :], zT[:])
                    if h % 2:
                        mm.then_inc(sem("edge_lb"), 1)

            def edge_lcol(n):
                ready(pe, "edge_max", n, ET * H, ET * H)
                for e in range(ET):
                    mm = one(b0[:, e * H:e * H + H], zT[:, cols(e)], k.head_a4[:])
                mm.then_inc(sem("edge_lcol"), 1)
                for e in range(ET):
                    mm = one(b1[:, cols(e)], hg[:, E + e * P:E + (e + 1) * P], W["WvalT"][:])
                mm.then_inc(sem("edge_v"), 1)

            def edge_den(n):
                ready(pe, "edge_exp", n)
                for e in range(ET):
                    for f in range(ET):
                        mm = nc.tensor.matmul(b0[:, e * H:e * H + H], k.same_src[:, f, cols(e)],
                                              edge_small[:, 2, f * H:f * H + H], start=(f == 0), stop=(f == ET - 1))
                mm.then_inc(sem("edge_den"), 1)

            def edge_scatter(n):
                ready(pe, "edge_u", n)
                for e in range(ET):
                    mm = nc.tensor.matmul(b0[:], U[:, cols(e)], k.src_rows[:, e, :], start=(e == 0),
                                          stop=(e == ET - 1))
                mm.then_inc(sem("edge_scattered"), 1)

            def edge_out(n):
                ready(pe, "edge_yT", n)
                by_nodes(b1, YT, W["WoutT"][:]).then_inc(sem("edge_outed"), 1)

            def cheb_turn(n):
                ready(pe, "cheb_h", n)
                freed(pe, "v_out", n)
                turn(c3, h3).then_inc(sem("cheb_turned"), 1)

            def cheb_g(n):
                ready(pe, "cheb_hT", n)
                by_nodes(c3, h3T, W["Wc"][:]).then_inc(sem("cheb_g"), 1)

            def cheb_prop(n):
                ready(pe, "cheb_glo", n)
                for t in range(NT):
                    for s in range(NT):
                        for i, (left, right) in enumerate([(k.adjT_hi, g_hi), (k.adjT_hi, g_lo), (k.adjT_lo, g_hi)]):
                            mm = nc.tensor.matmul(c3[:, cols(t)], left[:, s, cols(t)], right[:, cols(s)],
                                                  start=(s == 0 and i == 0), stop=(s == NT - 1 and i == 2))
                mm.then_inc(sem("cheb_prop"), 1)

            def cheb_x1turn(n):
                ready(pe, "cheb_x1", n)
                turn(c3, x1).then_inc(sem("x1_turned"), 1)

            def cheb_q(n):
                ready(pe, "cheb_x1T", n)
                one(c3[:], W["Wq"][:], x1T[:]).then_inc(sem("cheb_q"), 1)

            def cheb_k(n):
                ready(pe, "q_lo", n)
                one(c3[:], W["Wk"][:], x1T[:]).then_inc(sem("cheb_k"), 1)

            def cheb_v(n):
                ready(pe, "k_lo", n)
                by_nodes(c3, x1T, W["Wv"][:]).then_inc(sem("cheb_v"), 1)

            def att(n, j):
                if j < TILES:
                    h, t = j // NT, j % NT
                    if t == 0:
                        ready(pe, f"parts{h}", n, 128, 128)
                    need(pe, sem("att_T"), n * TILES + j - 1)
                    one([c0, c1][j % 2][:], Qs[:, h, cols(t)], Ks[:, h, :]).then_inc(sem("att_score"), 1)
                i = j - 2
                if 0 <= i < TILES:
                    if i == 0:
                        freed(pe, "att_oT", n)
                    ready(pe, "att_norm", n, i + 1, TILES)
                    need(pe, sem("att_pt"), n * TILES + i)
                    for s in range(NT):
                        mm = nc.tensor.transpose(c2[:, cols(s)], att_E[:, i % RING_E, cols(s)], k.ident[:])
                    mm.then_inc(sem("att_turn"), 1)
                if j == TILES + 2:
                    ready(pe, "att_pt", n, TILES, TILES)
                    ready(pe, "att_v", n, 16, 16)
                    for s in range(NT):
                        for h in range(H):
                            r = slice(HD * h, HD * (h + 1))
                            mm = nc.tensor.matmul(c2[r, :], vD[:, s, r], att_PT[:, h, s, :], start=(s == 0),
                                                  stop=(s == NT - 1))
                    mm.then_inc(sem("att_pv"), 1)

            def ffn_wo(n):
                ready(pe, "att_oT", n)
                need(pe, sem("edge_done"), min(n + 3, B) if isinstance(n, int) else n + 3)
                by_nodes(b1, oT, W["Wo"][:]).then_inc(sem("ffn_wo"), 1)

            def ffn_turn(n):
                ready(pe, "n2_aff", n, 2, 2)
                turn(b0, y2).then_inc(sem("ffn_turned"), 1)

            def ffn_up(n):
                ready(pe, "ffn_x2T", n)
                for q in range(2):
                    one([b0, b1][q][:], k.W1[:, cols(q)], x2T).then_inc(sem("ffn_up"), 1)

            def ffn_down(n):
                ready(pe, "ffn_gelu", n, 2, 2)
                for t in range(NT):
                    for q in range(2):
                        mm = nc.tensor.matmul(b0[:, cols(t)], mT[:, q, cols(t)], k.W2[:, q, :], start=(q == 0),
                                              stop=(q == 1))
                mm.then_inc(sem("ffn_downed"), 1)

            run(pe, pe.Fori, {
                "gat_turn": gat_turn, "gat_wh": gat_wh, "gat_s2": gat_s2, "gat_eturn0": lambda n: gat_eturn(n, 0),
                "gat_eturn2": lambda n: gat_eturn(n, 2), "gat_pv": gat_pv,
                "edge_gather": edge_gather, "edge_x": edge_x, "edge_lb": edge_lb, "edge_lcol": edge_lcol,
                "edge_den": edge_den, "edge_scatter": edge_scatter, "edge_out": edge_out,
                "cheb_turn": cheb_turn, "cheb_g": cheb_g, "cheb_prop": cheb_prop, "cheb_x1turn": cheb_x1turn,
                "cheb_q": cheb_q, "cheb_k": cheb_k, "cheb_v": cheb_v,
                "ffn_wo": ffn_wo, "ffn_turn": ffn_turn, "ffn_up": ffn_up, "ffn_down": ffn_down,
            }, att)


_INS = {"x": "x", "adj": "adj", "alpha": "L0_gnn_alpha_train", "w": "L0_gnn_w", "d": "L0_gnn_d",
        "fcw": "L0_gnn_fc_in_w", "fcb": "L0_gnn_fc_in_b", "W1g": "L1_gnn_W", "ag": "L1_gnn_a",
        "Wlin": "L2_gnn_W_lin", "Wval": "L2_gnn_W_val", "aL2": "L2_gnn_a", "Wout": "L2_gnn_W_out",
        "src": "L2_gnn_src", "dst": "L2_gnn_dst"} | {n: "L3_gnn_" + n for n in NAMES[15:]}


def kernel(**inputs):
    import numpy as np
    import concourse.bacc as bacc
    from concourse.bass_utils import run_bass_kernel_spmd as run

    nc = bacc.Bacc("TRN2", target_bir_lowering=False, num_devices=1)
    arrays, t_in = {}, {}
    for name in NAMES:
        a = np.ascontiguousarray(inputs[_INS[name]])
        arrays["in_" + name] = a
        t_in[name] = nc.dram_tensor("in_" + name, a.shape, mybir.dt.from_np(a.dtype), kind="ExternalInput").ap()
    out = nc.dram_tensor("out_x", (B, N, D), F32, kind="ExternalOutput").ap()
    build(nc, t_in, out)
    r = run(nc, [arrays], core_ids=[0])
    return r.results[0]["out_x"]
```

```python
from contextlib import ExitStack
from math import comb

import concourse.bass as bass
from concourse import mybir

F32 = mybir.dt.float32
R32 = mybir.dt.float32r
I32 = mybir.dt.int32
BF16 = mybir.dt.bfloat16
ALU = mybir.AluOpType
ACT = mybir.ActivationFunctionType
AX = mybir.AxisListType.X

B, N, D = 16, 512, 128
P = 128
NT = N // P
H = 4
HD = D // H
E = 256
ET = E // P
HID = 2 * D
EPS = 1e-5
STEPS = 8
DT = 1.0 / STEPS
HB = B // 2
CB = 4
NC = HB // CB
SQUARINGS = 9
BIG = 1.0e30
HUGE = 3.0e38
QK_SCALE = float(HD) ** -0.5
MASKED = -1.0e9

NAMES = ["x", "adj", "alpha", "w", "d", "fcw", "fcb", "W1g", "ag", "Wlin", "Wval", "aL2", "Wout", "src", "dst",
         "Wc", "bc", "g1", "be1", "Wq", "Wk", "Wv", "Wo", "bo", "g2", "be2", "W1", "b1", "W2", "b2", "g3", "be3"]
ROWS = ["fcb", "bc", "g1", "be1", "bo", "g2", "be2", "b2", "g3", "be3"]


def need(eng, sem, value):
    if isinstance(value, int) and value <= 0:
        return
    eng.wait_ge(sem, value)


class Shared(dict):
    __getattr__ = dict.__getitem__


def build(nc, t_in, out):
    ctx = ExitStack()
    with ctx:
        def sb(name, shape, dt=F32, c=None):
            return (c or ctx).enter_context(nc.sbuf_tensor(name, shape, dt))

        sems, part = {}, ["start"]

        def sem(name):
            if name not in sems:
                sems[name] = nc.alloc_semaphore(f"{name}_{part[0]}")
            return sems[name]

        bank = [ctx.enter_context(nc.psum_tensor(f"bank{i}", [P, 512], F32)) for i in range(8)]
        x1_dram = nc.dram_tensor("x_after_l0", (B, N, D), F32, kind="Internal").ap()
        x3_dram = nc.dram_tensor("x_after_l2", (B, N, D), F32, kind="Internal").ap()
        res_dram = nc.dram_tensor("attn_residual", (B, N, D), F32, kind="Internal").ap()
        v_dram = nc.dram_tensor("values", (B, N, D), F32, kind="Internal").ap()

        def nodes1(ap, b):
            return ap[bass.ds(b, 1)].rearrange("o (t p) d -> p (o t) d", p=P)

        ident = sb("ident", [P, P])
        ones = sb("ones", [P, P])
        lap_hi = sb("lap_hi", [P, NT, N], R32)
        lap_lo = sb("lap_lo", [P, NT, N], R32)
        mask_gat = sb("mask_gat", [P, NT, N], BF16)
        mask_att = sb("mask_att", [P, NT, N], BF16)
        edge_pick = sb("edge_pick", [P, NT, 2 * E])
        src_rows = sb("src_rows", [P, ET, N])
        seg_bias = sb("seg_bias", [P, ET, E])
        same_src = sb("same_src", [P, ET, E])
        logA = sb("logA", [P, ET])
        W = {n: sb("w_" + n, [P, D]) for n in ["W1g", "Wc", "Wq", "Wk", "Wv", "Wo", "WlinT", "WvalT", "WoutT"]}
        W1 = sb("w_W1", [P, HID])
        W2 = sb("w_W2", [P, 2, D])
        rowv = sb("rowv", [P, len(ROWS), D])
        row = {n: rowv[:, i, :] for i, n in enumerate(ROWS)}
        b1c = sb("b1c", [P, 2])
        neg_half = sb("neg_half", [P, NT])
        gat_a = sb("gat_a", [P, 2])
        gat_a2b = sb("gat_a2b", [P, P])
        head_a = sb("head_a", [P, H, P])
        head_a4 = sb("head_a4", [P, H])

        def row4(name, c=NT):
            return row[name].unsqueeze(1).broadcast_to([P, c, D])

        k = Shared(t_in=t_in, out=out, bank=bank, sem=sem, nodes1=nodes1, row=row, row4=row4, W=W, W1=W1, W2=W2,
                   x1_dram=x1_dram, x3_dram=x3_dram, res_dram=res_dram, v_dram=v_dram, rowv=rowv, b1c=b1c,
                   ident=ident, ones=ones, neg_half=neg_half, lap_hi=lap_hi, lap_lo=lap_lo, mask_gat=mask_gat,
                   mask_att=mask_att, edge_pick=edge_pick, src_rows=src_rows, seg_bias=seg_bias,
                   same_src=same_src, logA=logA, gat_a=gat_a, gat_a2b=gat_a2b, head_a=head_a, head_a4=head_a4)

        one = ExitStack()
        with one:
            def s1(name, shape, dt=F32):
                return sb(name, shape, dt, one)

            adj = s1("adj", [P, NT, N])
            PT_hi = s1("PT_hi", [P, NT, N], R32)
            PT_lo = s1("PT_lo", [P, NT, N], R32)
            G = s1("G", [P, STEPS + 1, D])
            x0T = s1("x0T", [P, B, N])
            gb = s1("gb", [P, STEPS + 1, D])
            xin = [s1(f"l0_x{u}", [P, NT, D]) for u in range(2)]
            z = [s1(f"l0_z{u}", [P, NT, D]) for u in range(2)]
            stats = s1("l0_stats", [P, 2, NT, 6])
            mv = s1("l0_mv", [P, 2, NT, 2])
            rs = s1("l0_rs", [P, 2, 2, NT])
            k_one = Shared(k, xin=xin, z=z, stats=stats, mv=mv, rs=rs, adj=adj, PT_hi=PT_hi, PT_lo=PT_lo, G=G, x0T=x0T, gb=gb)
            build_tables(nc, k_one)
            build_layer0(nc, k_one)

        nc.all_engine_barrier()
        nc.clear_and_free_semaphores(list(sems.values()))
        sems.clear()
        part[0] = "layers"
        nc.all_engine_barrier()

        build_layers(nc, k)


def wait_alone(eng, semaphore, value, passed):
    need(eng, semaphore, value)
    if not isinstance(value, int):
        eng.sem_inc(passed)


def x0_steps(nc, k):
    sem, xin, z, stats, mv, rs = k.sem, k.xin, k.z, k.stats, k.mv, k.rs

    def load(sp, u, use, b):
        need(sp, sem(f"l0_normed{u}"), use * NT)
        sp.dma_start(xin[u][:], k.nodes1(k.t_in["x"], b)).then_inc(sem(f"l0_loaded{u}"), 16)

    def statistics(dve, u, use):
        dve.wait_ge(sem(f"l0_loaded{u}"), (use + 1) * 16)
        for t in range(NT):
            nc.vector.bn_stats(stats[:, u, t, :], xin[u][:, t, :]).then_inc(sem(f"l0_stats{u}"), 1)
        wait_alone(dve, sem(f"l0_stats{u}"), (use + 1) * NT, sem("waits_passed"))
        for t in range(NT):
            nc.vector.bn_aggr(mv[:, u, t, :], stats[:, u, t, :]).then_inc(sem(f"l0_aggr{u}"), 1)

    def rstd(pool, u, use):
        wait_alone(pool, sem(f"l0_aggr{u}"), (use + 1) * NT, sem("waits_passed"))
        nc.gpsimd.tensor_scalar(rs[:, u, 0, :], mv[:, u, :, 1], EPS, None, ALU.add
                                ).then_inc(sem(f"l0_vareps{u}"), 1)
        pool.wait_ge(sem(f"l0_vareps{u}"), use + 1)
        nc.gpsimd.tensor_tensor(rs[:, u, 1, :], rs[:, u, 0, :], k.neg_half[:], ALU.pow
                                ).then_inc(sem(f"l0_rstd{u}"), 1)

    def normalise(dve, u, use):
        dve.wait_ge(sem(f"l0_rstd{u}"), use + 1)
        need(dve, sem(f"l0_turned{u}"), use)
        for t in range(NT):
            nc.vector.tensor_scalar(z[u][:, t, :], xin[u][:, t, :], mv[:, u, t, 0:1], rs[:, u, 1, t:t + 1],
                                    ALU.subtract, ALU.mult).then_inc(sem(f"l0_normed{u}"), 1)

    def turn(pe, u, use, dst):
        pe.wait_ge(sem(f"l0_normed{u}"), (use + 1) * NT)
        for t in range(NT):
            mm = nc.tensor.transpose(dst[:, t * P:(t + 1) * P], z[u][:, t, :], k.ident[:])
        mm.then_inc(sem(f"l0_turned{u}"), 1)

    def keep(act, u, use, src, b):
        act.wait_ge(sem(f"l0_turned{u}"), use + 1)
        nc.scalar.activation(k.x0T[:, bass.ds(b, 1), :].rearrange("p o n -> p (o n)"), src[:], ACT.Relu
                             ).then_inc(sem(f"l0_x0{u}"), 1)

    return Shared(load=load, statistics=statistics, rstd=rstd, normalise=normalise, turn=turn, keep=keep)


def build_tables(nc, k):
    t_in, bank, sem, W, row = k.t_in, k.bank, k.sem, k.W, k.row
    with ExitStack() as c:
        def sb(name, shape, dt=F32):
            return c.enter_context(nc.sbuf_tensor(name, shape, dt))

        asym = sb("asym", [P, NT, N])
        adjT = sb("adjT", [P, NT, N])
        diag = sb("diag", [P, NT, P])
        P_row = k.x0T[:, HB:HB + NT, :]
        PT = k.x0T[:, HB + NT:HB + 2 * NT, :]
        S = [sb(f"S{i}", [P, NT, N], R32) for i in range(2)]
        sqr = sb("sqr", [P, NT * N])
        raw = {n: sb("raw_" + n, [P, D]) for n in ["w", "fcw", "Wlin", "Wval", "Wout"]}
        wT = sb("wT", [P, D])
        wTd = sb("wTd", [P, D])
        Rp = sb("Rp", [P, STEPS + 1, D])
        FR = sb("FR", [P, STEPS + 1, D])
        alpha = sb("alpha_c", [P, NT])
        sg = sb("sg", [P, 4, NT])
        dcol = sb("dcol", [P, 1])
        dclip = sb("dclip", [P, 1])
        fcb_col = sb("fcb_col", [P, 1])
        fcb_b = sb("fcb_b", [P, P])
        a_rows = sb("a_rows", [P, 2, D])
        acol = sb("acol", [P, 1])
        edge_i = sb("edge_i", [P, 2, E], I32)
        edge_f = sb("edge_f", [P, 2, E])
        edge_ci = sb("edge_ci", [P, 2, ET], I32)
        edge_c = sb("edge_c", [P, 2, ET])
        node_row = sb("node_row", [P, N])
        node_col = sb("node_col", [P, NT])
        pick_s = sb("pick_s", [P, NT, E])
        dst_rows = sb("dst_rows", [P, ET, N])
        a0e = sb("a0e", [P, ET])
        logAb = sb("logAb", [P, ET, P])
        junk = sb("junk", [P, ET, N])
        junk2 = sb("junk2", [P, 4, D])
        ssq = sb("ssq", [P, SQUARINGS])
        nrm = sb("nrm", [P, SQUARINGS])
        vec = sb("vec", [P, 2, NT])
        dots = sb("dots", [P, 2])
        lam = sb("lam", [P, 4])
        two_lam = sb("two_lam", [P, 1])
        lap = asym
        tiny = sb("tiny", [P, 1])

        x0 = x0_steps(nc, k)
        adj_load = [(k.adj[:], t_in["adj"].rearrange("(t p) m -> p t m", p=P))]
        step_loads = [
            (alpha[:], t_in["alpha"].rearrange("(t p) -> p t", p=P)),
            (raw["w"][:], t_in["w"]), (raw["fcw"][:], t_in["fcw"]),
            (dcol[:], t_in["d"].rearrange("(p o) -> p o", o=1)),
            (fcb_col[:], t_in["fcb"].rearrange("(p o) -> p o", o=1)),
            (raw["Wlin"][:], t_in["Wlin"]), (raw["Wval"][:], t_in["Wval"]), (raw["Wout"][:], t_in["Wout"]),
        ]
        edge_loads = [
            (edge_i[:, 0, :], t_in["src"].partition_broadcast(P)),
            (edge_i[:, 1, :], t_in["dst"].partition_broadcast(P)),
            (edge_ci[:, 0, :], t_in["src"].rearrange("(t p) -> p t", p=P)),
            (edge_ci[:, 1, :], t_in["dst"].rearrange("(t p) -> p t", p=P)),
            (a_rows[:].rearrange("p a d -> p (a d)"), t_in["ag"].rearrange("f o -> (f o)").partition_broadcast(P)),
            (acol[:], t_in["aL2"].rearrange("h (e o) -> (h e) o", o=1)),
            (W["W1g"][:], t_in["W1g"]),
        ] + [(k.rowv[:, i, :], t_in[n].partition_broadcast(P)) for i, n in enumerate(ROWS)]
        late_loads = [
            (W["Wc"][:], t_in["Wc"]), (W["Wq"][:], t_in["Wq"]),
            (W["Wk"][:], t_in["Wk"]), (W["Wv"][:], t_in["Wv"]), (W["Wo"][:], t_in["Wo"]),
            (k.W1[:], t_in["W1"]), (k.W2[:], t_in["W2"].rearrange("(k p) d -> p k d", p=P)),
            (k.b1c[:], t_in["b1"].rearrange("(k p) -> p k", p=P)),
        ]

        block = c.enter_context(nc.Block())

        @block.sync
        def _(sp):
            for which, loads in [("adj", adj_load), ("step", step_loads), ("edge", edge_loads), ("late", late_loads)]:
                for dst, src in loads:
                    sp.dma_start(dst, src, allow_slow_non_contiguous=True).then_inc(sem(which + "_loaded"), 16)
                if which == "step":
                    for b in range(2):
                        x0.load(sp, b, 0, b)
            for b in range(2, HB):
                x0.load(sp, b % 2, b // 2, b)
            sp.wait_ge(sem("late_loaded"), 16 * len(late_loads))

        @block.gpsimd
        def _(pool):
            nc.gpsimd.memset(k.ones[:], 1.0).then_inc(sem("zeroed"), 1)
            nc.gpsimd.memset(k.ident[:], 0.0).then_inc(sem("zeroed"), 1)
            nc.gpsimd.memset(k.head_a[:], 0.0).then_inc(sem("zeroed"), 1)
            nc.gpsimd.memset(k.head_a4[:], 0.0).then_inc(sem("zeroed"), 1)
            nc.gpsimd.memset(tiny[:], 1e-8).then_inc(sem("zeroed"), 1)
            nc.gpsimd.memset(k.neg_half[:], -0.5).then_inc(sem("zeroed"), 1)
            pool.wait_ge(sem("zeroed"), 6)
            nc.gpsimd.affine_select(out=k.ident[:], in_=k.ident[:], compare_op=ALU.not_equal, fill=1.0, base=0,
                                    pattern=[[-1, P]], channel_multiplier=1).then_inc(sem("ident_ready"), 1)
            nc.gpsimd.iota(node_row[:], [[1, N]], base=0, channel_multiplier=0,
                           allow_small_or_imprecise_dtypes=True).then_inc(sem("node_numbers"), 1)
            nc.gpsimd.iota(node_col[:], [[P, NT]], base=0, channel_multiplier=1,
                           allow_small_or_imprecise_dtypes=True).then_inc(sem("node_numbers"), 1)

            pool.wait_ge(sem("adj_loaded"), 16)
            nc.gpsimd.tensor_scalar(k.mask_gat[:], k.adj[:], 0.0, -BIG, ALU.is_equal, ALU.mult
                                    ).then_inc(sem("masks"), 1)
            nc.gpsimd.tensor_scalar(k.mask_att[:], k.adj[:], 0.0, MASKED / QK_SCALE, ALU.is_le, ALU.mult
                                    ).then_inc(sem("masks"), 1)
            for b in range(HB):
                x0.rstd(pool, b % 2, b // 2)
                if b < NT:
                    pool.wait_ge(sem("edge_f"), 2)
                    pool.wait_ge(sem("node_numbers"), 2)
                    nc.gpsimd.tensor_scalar(pick_s[:, b, :], edge_f[:, 0, :], node_col[:, b:b + 1], None,
                                            ALU.is_equal).then_inc(sem("pick"), 1)
                    nc.gpsimd.tensor_scalar(k.edge_pick[:, b, E:], edge_f[:, 1, :], node_col[:, b:b + 1], None,
                                            ALU.is_equal).then_inc(sem("pick"), 1)
                elif b < NT + ET:
                    e = b - NT
                    nc.gpsimd.tensor_scalar(k.src_rows[:, e, :], node_row[:], edge_c[:, 0, e:e + 1], None,
                                            ALU.is_equal).then_inc(sem("rows"), 1)
                    nc.gpsimd.tensor_scalar(dst_rows[:, e, :], node_row[:], edge_c[:, 1, e:e + 1], None,
                                            ALU.is_equal).then_inc(sem("rows"), 1)
                    nc.gpsimd.tensor_scalar(k.same_src[:, e, :], edge_f[:, 0, :], edge_c[:, 0, e:e + 1], None,
                                            ALU.is_equal).then_inc(sem("rows"), 1)
            pool.wait_ge(sem("pick"), 2 * NT)
            nc.gpsimd.tensor_tensor(k.edge_pick[:, :, 0:E], pick_s[:], k.edge_pick[:, :, E:], ALU.add
                                    ).then_inc(sem("pick"), 1)

        @block.scalar
        def _(act):
            def square_sum(q):
                if q:
                    act.wait_ge(sem("scaled_dve"), 2 * q)
                act.wait_ge(sem("scaled_act"), 2 * q + 1)
                need(act, sem("norm_part"), q)
                nc.scalar.activation(sqr[:], S[q % 2][:].rearrange("p t m -> p (t m)").bitcast(F32), ACT.Square,
                                     accum_out=ssq[:, q:q + 1]).then_inc(sem("norm_part"), 1)

            def scale(q):
                act.wait_ge(sem("nrm"), q + 1)
                for t in (1, 3):
                    act.wait_ge(sem("square"), NT * q + t + 1)
                    nc.scalar.activation(S[(q + 1) % 2][:, t, :], bank[4 + t][:], ACT.Copy, scale=nrm[:, q:q + 1]
                                         ).then_inc(sem("scaled_act"), 1)

            act.wait_ge(sem("step_loaded"), 16 * len(step_loads))
            nc.scalar.activation(sg[:, 0, :], alpha[:], ACT.Exp, scale=-1.0).then_inc(sem("exp_alpha"), 1)
            act.wait_ge(sem("asym"), 1)
            nc.scalar.copy(S[0][:], asym[:]).then_inc(sem("scaled_act"), 1)
            for q in range(SQUARINGS):
                square_sum(q)
                if q >= 1:
                    x0.keep(act, (q - 1) % 2, (q - 1) // 2, bank[1], q - 1)
                scale(q)
                if q == 3:
                    act.wait_ge(sem("PT"), NT)
                    nc.scalar.copy(k.PT_hi[:], PT).then_inc(sem("P_hi"), 1)
            act.wait_ge(sem("lap"), 2 * NT)
            nc.scalar.copy(k.lap_hi[:], lap[:]).then_inc(sem("lap_hi"), 1)
            act.wait_ge(sem("edge_weight"), ET)
            act.wait_ge(sem("zeroed"), 5)
            nc.scalar.activation(k.logA[:], a0e[:], ACT.Ln, bias=tiny[:]).then_inc(sem("log_edge"), 1)

        @block.vector
        def _(dve):
            def symmetric():
                for s in range(NT):
                    dve.wait_ge(sem("adj_turned"), s + 1)
                    nc.vector.tensor_copy(adjT[:, s, :], bank[4 + s][:]).then_inc(sem("adjT"), 1)
                dve.wait_ge(sem("adjT"), NT)
                dve.wait_ge(sem("adj_loaded"), 16)
                nc.vector.tensor_tensor(asym[:], k.adj[:], adjT[:], ALU.add).then_inc(sem("asym"), 1)

            def scale(q):
                dve.wait_ge(sem("norm_sum"), q + 1)
                nc.vector.reciprocal(nrm[:, q:q + 1], bank[1][:, q:q + 1]).then_inc(sem("nrm"), 1)
                dve.wait_ge(sem("nrm"), q + 1)
                for t in (0, 2):
                    dve.wait_ge(sem("square"), NT * q + t + 1)
                    nc.vector.tensor_scalar(S[(q + 1) % 2][:, t, :], bank[4 + t][:], nrm[:, q:q + 1], None,
                                            ALU.mult).then_inc(sem("scaled_dve"), 1)

            def step_weights():
                dve.wait_ge(sem("step_loaded"), 16 * len(step_loads))
                dve.wait_ge(sem("zeroed"), 5)
                dve.wait_ge(sem("exp_alpha"), 1)
                nc.vector.tensor_scalar(sg[:, 1, :], sg[:, 0, :], 1.0, None, ALU.add).then_inc(sem("sig"), 1)
                dve.wait_ge(sem("sig"), 1)
                nc.vector.reciprocal(sg[:, 2, :], sg[:, 1, :]).then_inc(sem("sig"), 1)
                dve.wait_ge(sem("sig"), 2)
                nc.vector.tensor_scalar(sg[:, 3, :], sg[:, 2, :], DT / 2, None, ALU.mult).then_inc(sem("sig"), 1)
                nc.vector.tensor_scalar(dclip[:], dcol[:], 0.0, 1.0, ALU.max, ALU.min).then_inc(sem("dclip"), 1)
                nc.vector.tensor_scalar(fcb_b[:], k.ones[:], fcb_col[:], None, ALU.mult).then_inc(sem("fcb_wide"), 1)
                dve.wait_ge(sem("dclip"), 1)
                dve.wait_ge(sem("weights_turned"), 4)
                nc.vector.tensor_copy(wT[:], bank[0][:, 0:P]).then_inc(sem("wT"), 1)
                nc.vector.tensor_scalar(wTd[:], bank[0][:, 0:P], dclip[:], None, ALU.mult).then_inc(sem("wT"), 1)
                for i, n in enumerate(["WlinT", "WvalT", "WoutT"]):
                    nc.vector.tensor_copy(W[n][:], bank[0][:, (i + 1) * P:(i + 2) * P]).then_inc(sem("wT"), 1)
                dve.wait_ge(sem("fc_turned"), 1)
                nc.vector.tensor_copy(FR[:, 0, :], bank[3][:, 0:P]).then_inc(sem("FR"), 1)
                dve.wait_ge(sem("sig"), 3)
                dve.wait_ge(sem("ident_ready"), 1)
                for t in range(NT):
                    nc.vector.tensor_scalar(P_row[:, t, :], k.adj[:, t, :], sg[:, 3, t:t + 1], None, ALU.mult
                                            ).then_inc(sem("p_row"), 1)
                    nc.vector.tensor_scalar(diag[:, t, :], k.ident[:], sg[:, 3, t:t + 1], None, ALU.mult
                                            ).then_inc(sem("p_row"), 1)
                dve.wait_ge(sem("p_row"), 2 * NT)
                for t in range(NT):
                    sl = P_row[:, t, t * P:(t + 1) * P]
                    nc.vector.tensor_tensor(sl, sl, diag[:, t, :], ALU.subtract).then_inc(sem("p_row"), 1)

            def p_turned(half):
                for s in (2 * half, 2 * half + 1):
                    dve.wait_ge(sem("p_turned"), s + 1)
                    nc.vector.tensor_copy(PT[:, s, :], bank[2 + s % 2][:]).then_inc(sem("PT"), 1)

            def r_first():
                dve.wait_ge(sem("w_eff"), 1)
                nc.vector.tensor_scalar(Rp[:, 1, :], bank[0][:, 0:P], DT, None, ALU.mult
                                        ).then_inc(sem("R_half"), 1)
                nc.vector.tensor_copy(Rp[:, 0, :], k.ident[:]).then_inc(sem("R_half"), 1)
                dve.wait_ge(sem("R_half"), 2)
                nc.vector.scalar_tensor_tensor(Rp[:, 1, :], k.ident[:], 1.0 - DT, Rp[:, 1, :], ALU.mult,
                                               ALU.add).then_inc(sem("R_power"), 1)

            def r_powers(q):
                lo, hi = [(2, 2), (3, 4), (5, 8)][q]
                dve.wait_ge(sem("R_product"), q + 1)
                nc.vector.tensor_copy(Rp[:, lo:hi + 1, :],
                                      bank[2][:, 0:(hi - lo + 1) * D].rearrange("p (k d) -> p k d", d=D)
                                      ).then_inc(sem("R_power"), 1)

            def products_with_r():
                for q in range(2):
                    dve.wait_ge(sem("FR_product"), q + 1)
                    nc.vector.tensor_copy(FR[:, 1 + 4 * q:5 + 4 * q, :],
                                          bank[3 * q][:].rearrange("p (k d) -> p k d", d=D)
                                          ).then_inc(sem("FR"), 1)

            def bias_levels():
                dve.wait_ge(sem("edge_loaded"), 16 * len(edge_loads))
                nc.vector.tensor_copy(k.gb[:, 0, :], row["fcb"]).then_inc(sem("gb"), 1)
                for q in range(2):
                    dve.wait_ge(sem("bR_product"), q + 1)
                    for m in range(4):
                        i = 1 + 4 * q + m
                        nc.vector.tensor_scalar(k.gb[:, i, :], bank[2 - 2 * q][:, m * D:(m + 1) * D],
                                                float(comb(STEPS, i)), None, ALU.mult).then_inc(sem("gb"), 1)

            def polynomial_start():
                dve.wait_ge(sem("FR"), 3)
                for i in range(STEPS + 1):
                    nc.vector.tensor_scalar(k.G[:, i, :], FR[:, i, :], float(comb(STEPS, i)), None,
                                            ALU.mult).then_inc(sem("G_sum"), 1)
                dve.wait_ge(sem("R_power"), 4)

            def polynomial(first, end):
                for m in range(first, end):
                    dve.wait_ge(sem("G_sum"), STEPS + 1 + sum(STEPS - i for i in range(m)))
                    for i in range(m + 1, STEPS + 1):
                        nc.vector.scalar_tensor_tensor(k.G[:, i, :], Rp[:, m, :], DT * comb(STEPS - i + m, STEPS - i),
                                                       k.G[:, i, :], ALU.mult, ALU.add).then_inc(sem("G_sum"), 1)

            def low_parts():
                dve.wait_ge(sem("P_hi"), 1)
                nc.vector.tensor_tensor(k.PT_lo[:], PT, k.PT_hi[:].bitcast(F32), ALU.subtract
                                        ).then_inc(sem("split_lo"), 1)

            def edge_numbers():
                dve.wait_ge(sem("edge_loaded"), 16 * len(edge_loads))
                nc.vector.tensor_copy(edge_f[:], edge_i[:]).then_inc(sem("edge_f"), 1)
                nc.vector.tensor_copy(edge_c[:], edge_ci[:]).then_inc(sem("edge_f"), 1)

            def attention_vectors():
                for q in range(2):
                    nc.vector.tensor_tensor_reduce(junk2[:, q, :], W["W1g"][:], a_rows[:, q, :], 1.0, 0.0, ALU.mult,
                                                   ALU.add, k.gat_a[:, q:q + 1]).then_inc(sem("gat_a"), 1)
                dve.wait_ge(sem("gat_a"), 2)
                nc.vector.tensor_scalar(k.gat_a2b[:], k.ones[:], k.gat_a[:, 1:2], None, ALU.mult
                                        ).then_inc(sem("gat_a"), 1)
                for h in range(H):
                    r = slice(HD * h, HD * h + HD)
                    nc.vector.tensor_copy(k.head_a4[r, h:h + 1], acol[r, :]).then_inc(sem("head_a"), 1)
                    nc.vector.tensor_scalar(k.head_a[r, h, :], k.ones[r, :], acol[r, :], None, ALU.mult
                                            ).then_inc(sem("head_a"), 1)

            def edge_weights():
                dve.wait_ge(sem("rows"), 3 * ET)
                for e in range(ET):
                    dve.wait_ge(sem("adj_picked"), e + 1)
                    nc.vector.tensor_tensor_reduce(junk[:, e, :], bank[2 + e][:], dst_rows[:, e, :], 1.0, 0.0,
                                                   ALU.mult, ALU.add, a0e[:, e:e + 1]
                                                   ).then_inc(sem("edge_weight"), 1)
                nc.vector.tensor_scalar(k.seg_bias[:], k.same_src[:], BIG, -BIG, ALU.mult, ALU.add
                                        ).then_inc(sem("seg"), 1)

            symmetric()
            x0.statistics(dve, 0, 0)
            for q in range(SQUARINGS):
                scale(q)
                if q < HB:
                    x0.normalise(dve, q % 2, q // 2)
                if q < HB - 1:
                    x0.statistics(dve, (q + 1) % 2, (q + 1) // 2)
                if q == 0:
                    step_weights()
                    edge_numbers()
                elif q == 1:
                    r_first()
                    p_turned(0)
                elif q == 2:
                    p_turned(1)
                elif q == 3:
                    r_powers(0)
                    attention_vectors()
                elif q == 4:
                    r_powers(1)
                    low_parts()
                elif q == 5:
                    r_powers(2)
                elif q == 6:
                    products_with_r()
                    polynomial_start()
                elif q == 7:
                    bias_levels()
                    polynomial(0, 1)
            dve.wait_ge(sem("scaled_dve"), 2 * SQUARINGS)
            dve.wait_ge(sem("scaled_act"), 2 * SQUARINGS + 1)
            nc.vector.tensor_reduce(vec[:, 0, :], S[SQUARINGS % 2][:].bitcast(F32), AX, ALU.add
                                    ).then_inc(sem("vec"), 1)
            polynomial(1, STEPS)
            dve.wait_ge(sem("A_vec"), 1)
            nc.vector.tensor_copy(vec[:, 1, :], bank[1][:, 32:32 + NT]).then_inc(sem("vec"), 1)
            dve.wait_ge(sem("vec"), 2)
            for q in range(2):
                nc.vector.tensor_tensor_reduce(junk2[:, 2 + q, 0:NT], vec[:, 1, :], vec[:, 1 - q, :], 1.0, 0.0,
                                               ALU.mult, ALU.add, dots[:, q:q + 1]).then_inc(sem("dots"), 1)
            dve.wait_ge(sem("dot_sums"), 1)
            nc.vector.reciprocal(lam[:, 0:1], bank[1][:, 65:66]).then_inc(sem("lam"), 1)
            dve.wait_ge(sem("lam"), 1)
            nc.vector.tensor_tensor(lam[:, 1:2], lam[:, 0:1], bank[1][:, 64:65], ALU.mult).then_inc(sem("lam"), 1)
            dve.wait_ge(sem("lam"), 2)
            nc.vector.tensor_scalar(lam[:, 2:3], lam[:, 1:2], 0.5, 1e-8, ALU.mult, ALU.add).then_inc(sem("lam"), 1)
            dve.wait_ge(sem("lam"), 3)
            nc.vector.reciprocal(lam[:, 3:4], lam[:, 2:3]).then_inc(sem("lam"), 1)
            dve.wait_ge(sem("lam"), 4)
            nc.vector.tensor_scalar(two_lam[:], lam[:, 3:4], 2.0, None, ALU.mult).then_inc(sem("lam"), 1)
            dve.wait_ge(sem("lam"), 5)
            for s in range(NT):
                nc.vector.tensor_scalar(lap[:, s, :], adjT[:, s, :], two_lam[:], None, ALU.mult
                                        ).then_inc(sem("lap"), 1)
            dve.wait_ge(sem("lap"), NT)
            for s in range(NT):
                diagonal = lap[:, s, s * P:(s + 1) * P]
                nc.vector.tensor_tensor(diagonal, diagonal, k.ident[:], ALU.subtract).then_inc(sem("lap"), 1)
            edge_weights()
            dve.wait_ge(sem("log_edge"), 1)
            for e in range(ET):
                nc.vector.tensor_scalar(logAb[:, e, :], k.ones[:], k.logA[:, e:e + 1], None, ALU.mult
                                        ).then_inc(sem("logAb"), 1)
            dve.wait_ge(sem("lap_hi"), 1)
            nc.vector.tensor_tensor(k.lap_lo[:], lap[:], k.lap_hi[:].bitcast(F32), ALU.subtract
                                    ).then_inc(sem("lap_lo"), 1)
            dve.wait_ge(sem("seg"), 1)
            dve.wait_ge(sem("log_row"), 1)
            for e in range(ET):
                nc.vector.tensor_tensor(k.seg_bias[:, e, :], k.seg_bias[:, e, :], bank[0][:, 0:E], ALU.add
                                        ).then_inc(sem("seg"), 1)

        @block.tensor
        def _(pe):
            def square(q):
                if q:
                    pe.wait_ge(sem("scaled_dve"), 2 * q)
                pe.wait_ge(sem("scaled_act"), 2 * q + 1)
                for t in range(NT):
                    if t == 2:
                        pe.wait_ge(sem("norm_part"), q + 1)
                        if q >= 1:
                            pe.wait_ge(sem(f"l0_x0{(q - 1) % 2}"), (q - 1) // 2 + 1)
                        nc.tensor.matmul(bank[1][:, q:q + 1], k.ones[:], ssq[:, q:q + 1], start=True, stop=True
                                         ).then_inc(sem("norm_sum"), 1)
                    for s in range(NT):
                        mm = nc.tensor.matmul(bank[4 + t][:], S[q % 2][:, s, t * P:(t + 1) * P], S[q % 2][:, s, :],
                                              start=(s == 0), stop=(s == NT - 1))
                    mm.then_inc(sem("square"), 1)

            def turn_weights():
                pe.wait_ge(sem("step_loaded"), 16 * len(step_loads))
                for i, n in enumerate(["w", "Wlin", "Wval", "Wout"]):
                    nc.tensor.transpose(bank[0][:, i * P:(i + 1) * P], raw[n][:], k.ident[:]
                                        ).then_inc(sem("weights_turned"), 1)
                nc.tensor.transpose(bank[3][:, 0:P], raw["fcw"][:], k.ident[:]).then_inc(sem("fc_turned"), 1)

            def turn_p(half):
                pe.wait_ge(sem("p_row"), 3 * NT)
                need(pe, sem("PT"), 2 * half)
                for s in (2 * half, 2 * half + 1):
                    for t in range(NT):
                        mm = nc.tensor.transpose(bank[2 + s % 2][:, t * P:(t + 1) * P],
                                                 P_row[:, t, s * P:(s + 1) * P], k.ident[:])
                    mm.then_inc(sem("p_turned"), 1)

            def w_eff():
                pe.wait_ge(sem("wT"), 5)
                pe.wait_ge(sem("FR"), 1)
                nc.tensor.matmul(bank[0][:, 0:P], wTd[:], wT[:], start=True, stop=True
                                 ).then_inc(sem("w_eff"), 1)

            def r_product(q):
                left, lo, hi = [(1, 1, 1), (2, 1, 2), (4, 1, 4)][q]
                pe.wait_ge(sem("PT"), NT)
                pe.wait_ge(sem("R_power"), q + 1)
                nc.tensor.matmul(bank[2][:, 0:(hi - lo + 1) * D], Rp[:, left, :],
                                 Rp[:, lo:hi + 1, :], start=True, stop=True).then_inc(sem("R_product"), 1)

            def fc_products():
                pe.wait_ge(sem("R_power"), 4)
                for q in range(2):
                    nc.tensor.matmul(bank[3 * q][:], raw["fcw"][:], Rp[:, 1 + 4 * q:5 + 4 * q, :], start=True,
                                     stop=True).then_inc(sem("FR_product"), 1)

            def bias_products():
                pe.wait_ge(sem("fcb_wide"), 1)
                pe.wait_ge(sem("FR"), 3)
                for q in range(2):
                    nc.tensor.matmul(bank[2 - 2 * q][:], fcb_b[:], Rp[:, 1 + 4 * q:5 + 4 * q, :], start=True,
                                     stop=True).then_inc(sem("bR_product"), 1)

            def pick_adj():
                pe.wait_ge(sem("pick"), 2 * NT)
                pe.wait_ge(sem("gb"), STEPS + 1)
                for e in range(ET):
                    for t in range(NT):
                        mm = nc.tensor.matmul(bank[2 + e][:], pick_s[:, t, e * P:(e + 1) * P], k.adj[:, t, :],
                                              start=(t == 0), stop=(t == NT - 1))
                    mm.then_inc(sem("adj_picked"), 1)

            pe.wait_ge(sem("adj_loaded"), 16)
            pe.wait_ge(sem("ident_ready"), 1)
            for s in range(NT):
                for t in range(NT):
                    mm = nc.tensor.transpose(bank[4 + s][:, t * P:(t + 1) * P], k.adj[:, t, s * P:(s + 1) * P],
                                             k.ident[:])
                mm.then_inc(sem("adj_turned"), 1)
            pe.wait_ge(sem("adjT"), NT)
            for q in range(SQUARINGS):
                square(q)
                if q < HB:
                    pe.wait_ge(sem("nrm"), q + 1)
                    x0.turn(pe, q % 2, q // 2, bank[1])
                if q == 0:
                    turn_weights()
                elif q == 1:
                    w_eff()
                    turn_p(0)
                elif q == 2:
                    turn_p(1)
                elif q == 3:
                    r_product(0)
                elif q == 4:
                    r_product(1)
                elif q == 5:
                    r_product(2)
                elif q == 6:
                    fc_products()
                elif q == 7:
                    bias_products()
            pe.wait_ge(sem("vec"), 1)
            for t in range(NT):
                for s in range(NT):
                    mm = nc.tensor.matmul(bank[1][:, 32 + t:33 + t], asym[:, s, t * P:(t + 1) * P],
                                          vec[:, 0, s:s + 1], start=(s == 0), stop=(s == NT - 1))
            mm.then_inc(sem("A_vec"), 1)
            pe.wait_ge(sem("dots"), 2)
            nc.tensor.matmul(bank[1][:, 64:66], k.ones[:], dots[:], start=True, stop=True).then_inc(sem("dot_sums"), 1)
            pick_adj()
            pe.wait_ge(sem("logAb"), ET)
            for e in range(ET):
                mm = nc.tensor.matmul(bank[0][:, e * P:(e + 1) * P], logAb[:, e, :], k.ident[:], start=True, stop=True)
            mm.then_inc(sem("log_row"), 1)




def build_layer0(nc, k):
    t_in, bank, sem, x0T = k.t_in, k.bank, k.sem, k.x0T
    LEVELS = STEPS + 1
    PAIRS = HB // 2
    with ExitStack() as c:
        def sb(name, shape, dt=F32):
            return c.enter_context(nc.sbuf_tensor(name, shape, dt))

        Z_hi = sb("Z_hi", [P, NT, HB * D], R32)
        Z_lo = sb("Z_lo", [P, NT, HB * D], R32)
        zs = sb("l0_sum", [P, NC, NT, CB * D])
        xres = sb("l0_res", [P, NT, CB * D])

        block = c.enter_context(nc.Block())

        def chunk_dram(ap, half, ch, t):
            b0 = half * HB + ch * CB
            return ap[b0:b0 + CB, t * P:(t + 1) * P, :].rearrange("b p d -> p b d")

        x0 = x0_steps(nc, k)

        @block.sync
        def _(sp):
            with sp.Fori(0, HB) as b:
                x0.load(sp, 0, b + PAIRS, b + HB)
            for half in range(2):
                for ch in range(NC):
                    for t in range(NT):
                        need(sp, sem(f"l0_stored{t}"), (half * NC + ch) * 16)
                        sp.dma_start(xres[:, t, :].rearrange("p (b d) -> p b d", d=D),
                                     chunk_dram(t_in["x"], half, ch, t)).then_inc(sem(f"l0_res{t}"), 16)
                    for t in range(NT):
                        sp.wait_ge(sem(f"l0_final{t}"), half * NC + ch + 1)
                        sp.dma_start(chunk_dram(k.x1_dram, half, ch, t),
                                     xres[:, t, :].rearrange("p (b d) -> p b d", d=D)
                                     ).then_inc(sem(f"l0_stored{t}"), 16)
            for t in range(NT):
                sp.wait_ge(sem(f"l0_stored{t}"), 2 * NC * 16)

        @block.gpsimd
        def _(pool):
            with pool.Fori(0, HB) as b:
                x0.rstd(pool, 0, b + PAIRS)

        @block.scalar
        def _(act):
            def level(lev, half):
                for ch in range(NC):
                    act.wait_ge(sem(f"l0_level{ch}"), half * LEVELS * NT + lev * NT + NT)
                    for t in range(NT):
                        act.wait_ge(sem(f"l0_sum{ch}"), half * STEPS * NT + lev * NT + t + 1)
                        nc.scalar.copy(Z_hi[:, t, ch * CB * D:(ch + 1) * CB * D], zs[:, ch, t, :]
                                       ).then_inc(sem(f"l0_Zhi{ch}"), 1)

            with act.Fori(0, STEPS) as lev:
                level(lev, 0)
                x0.keep(act, 0, lev + PAIRS, bank[-1], lev + HB)
            with act.Fori(0, STEPS) as lev:
                level(lev, 1)

        @block.vector
        def _(dve):
            def sums(lev, half, ch):
                sl = slice(ch * CB * D, (ch + 1) * CB * D)
                for t in range(NT):
                    dve.wait_ge(sem(f"l0_level{ch}"), half * LEVELS * NT + lev * NT + t + 1)
                    nc.vector.tensor_tensor(zs[:, ch, t, :].rearrange("p (b d) -> p b d", d=D),
                                            bank[ch * NT + t][:].rearrange("p (b d) -> p b d", d=D),
                                            k.gb[:, bass.ds(lev, 1), :].broadcast_to([P, CB, D]),
                                            ALU.add).then_inc(sem(f"l0_sum{ch}"), 1)
                for t in range(NT):
                    dve.wait_ge(sem(f"l0_Zhi{ch}"), half * STEPS * NT + lev * NT + t + 1)
                    nc.vector.tensor_tensor(Z_lo[:, t, sl], zs[:, ch, t, :], Z_hi[:, t, sl].bitcast(F32),
                                            ALU.subtract).then_inc(sem(f"l0_Zlo{ch}"), 1)

            def end(half):
                for ch in range(NC):
                    for t in range(NT):
                        dve.wait_ge(sem(f"l0_level{ch}"), (half + 1) * LEVELS * NT - NT + t + 1)
                        nc.vector.tensor_tensor(zs[:, ch, t, :].rearrange("p (b d) -> p b d", d=D),
                                                bank[ch * NT + t][:].rearrange("p (b d) -> p b d", d=D),
                                                k.gb[:, LEVELS - 1:LEVELS, :].broadcast_to([P, CB, D]),
                                                ALU.add).then_inc(sem(f"l0_last{ch}"), 1)
                        dve.wait_ge(sem(f"l0_last{ch}"), half * NT + t + 1)
                        dve.wait_ge(sem(f"l0_res{t}"), (half * NC + ch + 1) * 16)
                        nc.vector.tensor_tensor(xres[:, t, :], zs[:, ch, t, :], xres[:, t, :], ALU.add
                                                ).then_inc(sem(f"l0_final{t}"), 1)

            with dve.Fori(0, STEPS) as lev:
                x0.statistics(dve, 0, lev + PAIRS)
                sums(lev, 0, 0)
                x0.normalise(dve, 0, lev + PAIRS)
                sums(lev, 0, 1)
            end(0)
            with dve.Fori(0, STEPS) as lev:
                for ch in range(NC):
                    sums(lev, 1, ch)
            end(1)

        @block.tensor
        def _(pe):
            def x0_times(half, ch, t, g, first):
                for b in range(CB):
                    mm = nc.tensor.matmul(bank[ch * NT + t][:, b * D:(b + 1) * D],
                                          x0T[:, half * HB + ch * CB + b, t * P:(t + 1) * P], g, start=first,
                                          stop=first or b == CB - 1)
                mm.then_inc(sem(f"l0_level{ch}"), 1)

            def p_times(ch, t):
                sl = slice(ch * CB * D, (ch + 1) * CB * D)
                n0 = slice(t * P, (t + 1) * P)
                for s in range(NT):
                    for i, (left, right) in enumerate([(k.PT_hi, Z_hi), (k.PT_hi, Z_lo), (k.PT_lo, Z_hi)]):
                        nc.tensor.matmul(bank[ch * NT + t][:], left[:, s, n0], right[:, s, sl],
                                         start=(s == 0 and i == 0), stop=False)

            for half in range(2):
                for ch in range(NC):
                    for t in range(NT):
                        if half == 1:
                            pe.wait_ge(sem(f"l0_last{ch}"), t + 1)
                            pe.wait_ge(sem("l0_x00"), PAIRS + HB)
                        x0_times(half, ch, t, k.G[:, 0, :], True)
                with pe.Fori(1, LEVELS) as lev:
                    for ch in range(NC):
                        pe.wait_ge(sem(f"l0_Zlo{ch}"), half * STEPS * NT + lev * NT)
                        for t in range(NT):
                            if half == 0 and ch == 1 and t == 0:
                                pe.wait_ge(sem("l0_sum1"), lev * NT)
                                x0.turn(pe, 0, lev + PAIRS - 1, bank[-1])
                            elif half == 0 and ch == 1 and t == NT - 1:
                                pe.wait_ge(sem("l0_x00"), lev + PAIRS)
                            p_times(ch, t)
                            x0_times(half, ch, t, k.G[:, bass.ds(lev, 1), :].rearrange("p o d -> p (o d)"), False)
STAGES = ["gat", "edge", "cheb", "att", "ffn"]
LAG = {s: i for i, s in enumerate(STAGES)}
TILES = H * NT
RING_T, RING_E = 3, 4
TAIL = {f"tail{j}": j for j in range(TILES, TILES + 3)}

SCHEDULE = [
    (-1, "gat", "load_x"), (-1, "ffn", "tail16"),
    (0, "ffn", "tail17"), (0, "cheb", "cheb_rstd"), (0, "cheb", "cheb_stats"),
    (1, "edge", "edge_stats"), (1, "edge", "edge_rstd"), (1, "cheb", "cheb_apply"), (1, "cheb", "cheb_hi"),
    (1, "ffn", "load_ffn"), (1, "ffn", "tail18"),
    (3, "ffn", "ffn_res"), (3, "cheb", "cheb_lo"), (3, "gat", "gat_rstd"), (3, "gat", "gat_stats"),
    (3, "ffn", "ffn_wo"), (3, "edge", "edge_apply"), (3, "cheb", "cheb_xpT"), (3, "gat", "gat_hT"),
    (3, "ffn", "n2_rstd"),
    (4, "cheb", "cheb_res"), (4, "cheb", "cheb_prop"), (4, "gat", "gat_turn"), (4, "ffn", "ffn_y2"),
    (4, "cheb", "cheb_g"), (4, "att", "load_v"), (4, "gat", "gat_apply"), (4, "ffn", "n2_apply"),
    (4, "cheb", "stack0"), (4, "cheb", "cheb_y"), (4, "ffn", "n2_affine"), (4, "gat", "gat_wh"),
    (4, "cheb", "stack2"), (4, "gat", "gat_wh_out"),
    (5, "gat", "gat_s2"), (5, "ffn", "ffn_turn"), (5, "gat", "gat_s1_out"), (5, "ffn", "ffn_x2T"),
    (5, "ffn", "ffn_b2"),
    (6, "cheb", "stack1"), (6, "gat", "gat_scores"), (6, "ffn", "ffn_gelu"), (6, "cheb", "n1_rstd"),
    (6, "ffn", "ffn_up"), (6, "cheb", "stack3"), (6, "gat", "gat_low"), (6, "cheb", "n1_apply"),
    (7, "cheb", "n1_affine"), (7, "gat", "gat_exp"), (7, "ffn", "n3_rstd"), (7, "gat", "gat_max"),
    (7, "ffn", "ffn_y3"), (7, "gat", "gat_eT0"), (7, "ffn", "ffn_down"),
    (8, "edge", "edge_hg"), (8, "cheb", "cheb_x1"), (8, "gat", "gat_eturn0"), (8, "edge", "edge_gather"),
    (9, "cheb", "cheb_x1turn"), (9, "edge", "edge_x"), (9, "ffn", "n3_apply"), (9, "cheb", "cheb_x1T"),
    (10, "cheb", "cheb_q"), (10, "cheb", "cheb_qsplit"),
    (11, "edge", "edge_xz"), (11, "edge", "edge_store"), (11, "ffn", "store_out"), (11, "cheb", "cheb_qlow"),
    (11, "cheb", "cheb_ksplit"), (11, "gat", "gat_eturn2"), (11, "edge", "edge_z"), (11, "cheb", "cheb_klow"),
    (11, "cheb", "cheb_k"), (11, "gat", "gat_eT2"), (11, "ffn", "n3_affine"),
    (12, "edge", "edge_lb"), (12, "gat", "gat_pv"), (12, "edge", "edge_lcol"), (12, "edge", "edge_max"),
    (12, "edge", "edge_den"), (12, "edge", "edge_exp"), (12, "edge", "edge_le"), (12, "edge", "edge_u"),
    (13, "edge", "edge_scatter"), (13, "edge", "edge_yT"), (13, "ffn", "ffn_final"),
    (14, "edge", "edge_out"),
    (15, "cheb", "cheb_vout"), (15, "edge", "edge_x3"), (15, "gat", "gat_x2"), (15, "cheb", "cheb_v"),
    (15, "cheb", "store_v"),
]




def build_layers(nc, k):
    bank, sem, W, row4 = k.bank, k.sem, k.W, k.row4
    with ExitStack() as c:
        def sb(name, shape, dt=F32):
            return c.enter_context(nc.sbuf_tensor(name, shape, dt))

        def tile(name):
            return sb(name, [P, NT, D])

        ln_mem = {}
        for tag in ["gat", "edge", "cheb", "n1", "n2", "n3"]:
            ln_mem[tag] = (sb(tag + "_stat", [P, NT, 6]), sb(tag + "_mv", [P, NT, 2]), sb(tag + "_rs", [P, 4, NT]))
        xA, zA, WhA, x2 = tile("gat_xin"), tile("gat_z"), tile("gat_whs"), tile("x2")
        hTA = sb("gat_hTs", [P, N])
        gat_T, gat_V, gat_ET = (sb(n, [P, NT, N]) for n in ["gat_Ts", "gat_Vs", "gat_ETs"])
        gat_E = gat_T
        gat_small = sb("gat_small", [P, 8, NT])
        h2, x3 = tile("edge_hs"), tile("x3")
        hg = sb("edge_hgs", [P, 2 * E])
        xz = sb("edge_xzs", [P, E])
        zT = xz
        edge_junk = sb("edge_junk", [P, ET * H, E], BF16)
        edge_small = sb("edge_small", [P, 5, ET * H])
        U = sb("edge_us", [P, ET * D])
        YT = hg
        h3, y1, x1 = (tile("cheb_" + n) for n in ["hs", "y1", "x1s"])
        xpT = x1T = sb("cheb_xTs", [P, N])
        h_hi, h_lo = sb("h_hi", [P, NT, D], R32), sb("h_lo", [P, NT, D], R32)
        qk_hi = [sb(f"{n}_hi", [P, N], R32) for n in "qk"]
        qk_lo = [sb(f"{n}_lo", [P, N], R32) for n in "qk"]
        vS, vD = tile("v_out"), tile("v_in")
        Qs, Ks = sb("Q_parts", [P, H, N], R32), sb("K_parts", [P, H, N], R32)
        att_T, att_E = sb("att_Ts", [P, RING_T, N]), sb("att_Es", [P, RING_E, N])
        att_PT = sb("att_PTs", [P, H, NT, N])
        att_small = sb("att_small", [P, 3, TILES])
        oT = sb("att_oTs", [P, N])
        xrE, y2, y3, x3E = (tile("ffn_" + n) for n in ["xr", "y2s", "y3s", "x3"])
        mT = sb("ffn_mT", [P, 2, N])
        x2T = mT[:, 1, :]

        a0, a1, b0, b1, c0, c1, c2, c3 = bank

        def cols(t):
            return slice(t * P, (t + 1) * P)

        def flat(x):
            return x[:].rearrange("p t d -> p (t d)")

        def ready(eng, name, n, count=1, per=1):
            need(eng, sem(name), n * per + count)

        def freed(eng, name, n, per=1):
            need(eng, sem(name), n * per)

        def ready_alone(eng, name, n, count=1, per=1):
            wait_alone(eng, sem(name), n * per + count, sem("waits_passed"))

        def freed_alone(eng, name, n, per=1):
            wait_alone(eng, sem(name), n * per, sem("waits_passed"))

        def ln_stats(dve, tag, n, src):
            stat, mv, _ = ln_mem[tag]
            for t in range(NT):
                nc.vector.bn_stats(stat[:, t, :], src[:, t, :]).then_inc(sem(tag + "_stat"), 1)
            ready_alone(dve, tag + "_stat", n, NT, NT)
            for t in range(NT):
                nc.vector.bn_aggr(mv[:, t, :], stat[:, t, :]).then_inc(sem(tag + "_aggr"), 1)

        def ln_rstd(pool, tag, n):
            _, mv, rs = ln_mem[tag]
            ready_alone(pool, tag + "_aggr", n, NT, NT)
            nc.gpsimd.tensor_scalar(rs[:, 0, :], mv[:, :, 1], EPS, None, ALU.add).then_inc(sem(tag + "_vareps"), 1)
            ready(pool, tag + "_vareps", n)
            nc.gpsimd.tensor_tensor(rs[:, 1, :], rs[:, 0, :], k.neg_half[:], ALU.pow).then_inc(sem(tag + "_rs"), 1)

        def ln_scale_bias(pool, tag, n):
            _, mv, rs = ln_mem[tag]
            freed_alone(pool, tag + "_h", n, NT)
            ready_alone(pool, tag + "_aggr", n, NT, NT)
            nc.gpsimd.tensor_scalar(rs[:, 0, :], mv[:, :, 1], EPS, None, ALU.add).then_inc(sem(tag + "_vareps"), 1)
            nc.gpsimd.tensor_scalar(rs[:, 2, :], mv[:, :, 0], -1.0, None, ALU.mult).then_inc(sem(tag + "_vareps"), 1)
            ready(pool, tag + "_vareps", n, 2, 2)
            nc.gpsimd.tensor_tensor(rs[:, 1, :], rs[:, 0, :], k.neg_half[:], ALU.pow).then_inc(sem(tag + "_rs"), 1)
            ready(pool, tag + "_rs", n)
            nc.gpsimd.tensor_tensor(rs[:, 3, :], rs[:, 2, :], rs[:, 1, :], ALU.mult).then_inc(sem(tag + "_bias"), 1)

        def ln_relu(act, tag, n, src, dst):
            rs = ln_mem[tag][2]
            ready(act, tag + "_bias", n)
            for t in range(NT):
                nc.scalar.activation(dst[:, t, :], src[:, t, :], ACT.Relu, scale=rs[:, 1, t:t + 1],
                                     bias=rs[:, 3, t:t + 1]).then_inc(sem(tag + "_h"), 1)

        def ln_apply(dve, tag, n, src, dst):
            _, mv, rs = ln_mem[tag]
            ready(dve, tag + "_rs", n)
            for t in range(NT):
                nc.vector.tensor_scalar(dst[:, t, :], src[:, t, :], mv[:, t, 0:1], rs[:, 1, t:t + 1], ALU.subtract,
                                        ALU.mult).then_inc(sem(tag + "_normed"), 1)

        def affine(pool, tag, n, x, g, b):
            ready(pool, tag + "_normed", n, NT, NT)
            nc.gpsimd.tensor_tensor(x[:], x[:], row4(g), ALU.mult).then_inc(sem(tag + "_aff"), 1)
            ready(pool, tag + "_aff", n, 1, 2)
            nc.gpsimd.tensor_tensor(x[:], x[:], row4(b), ALU.add).then_inc(sem(tag + "_aff"), 1)

        def run(eng, fori, steps, att):
            def iteration(i):
                def n_of(stage):
                    n = i - LAG[stage]
                    return n if not isinstance(i, int) or 0 <= n < B else None

                at = 0
                for j in range(-1, TILES):
                    if j >= 0 and att and n_of("att") is not None:
                        att(n_of("att"), j)
                    while at < len(SCHEDULE) and SCHEDULE[at][0] <= j:
                        _, stage, step = SCHEDULE[at]
                        if (step in steps or att and step in TAIL) and n_of(stage) is not None:
                            steps[step](n_of(stage)) if step in steps else att(n_of(stage), TAIL[step])
                        at += 1

            fill = len(STAGES)
            for i in range(fill):
                iteration(i)
            with fori(fill, B) as i:
                iteration(i)
            for i in range(B, B + fill - 1):
                iteration(i)

        block = c.enter_context(nc.Block())

        @block.sync
        def _(sp):
            def load_x(n):
                freed_alone(sp, "gat_done", n, NT)
                sp.dma_start(xA[:], k.nodes1(k.x1_dram, n)).then_inc(sem("gat_loaded"), 16)

            def store_x3(n):
                ready_alone(sp, "edge_done", n)
                sp.dma_start(k.nodes1(k.x3_dram, n), x3[:]).then_inc(sem("x3_stored"), 16)

            def store_res(n):
                ready_alone(sp, "cheb_x1", n)
                sp.dma_start(k.nodes1(k.res_dram, n), x1[:]).then_inc(sem("res_stored"), 16)

            def store_v(n):
                ready_alone(sp, "v_out", n)
                sp.dma_start(k.nodes1(k.v_dram, n), vS[:]).then_inc(sem("v_stored"), 16)

            def load_v(n):
                ready_alone(sp, "v_stored", n, 16, 16)
                freed_alone(sp, "att_pv", n)
                sp.dma_start(vD[:], k.nodes1(k.v_dram, n)).then_inc(sem("att_v"), 16)

            def stack(n, which, h):
                ready_alone(sp, f"{'qk'[which]}_lo", n)
                wait_alone(sp, sem("att_score"), n * TILES - TILES + NT * (h + 1), sem("waits_passed"))
                dst = [Qs, Ks][which]
                order = [[0, 0, 1, 1], [0, 1, 0, 1]][which]
                for g in range(4):
                    src = [qk_hi, qk_lo][order[g]][which]
                    sp.dma_start(dst[HD * g:HD * (g + 1), h, :].bitcast(F32), src[HD * h:HD * (h + 1), :].bitcast(F32)
                                 ).then_inc(sem(f"parts{h}"), 16)

            def load_ffn(n):
                ready_alone(sp, "res_stored", n, 16, 16)
                freed_alone(sp, "ffn_y2", n)
                sp.dma_start(xrE[:], k.nodes1(k.res_dram, n)).then_inc(sem("ffn_xr"), 16)
                ready_alone(sp, "x3_stored", n, 16, 16)
                freed_alone(sp, "ffn_fin", n)
                sp.dma_start(x3E[:], k.nodes1(k.x3_dram, n)).then_inc(sem("ffn_x3"), 16)

            def store_out(n):
                ready_alone(sp, "ffn_fin", n)
                sp.dma_start(k.nodes1(k.out, n), y3[:]).then_inc(sem("out_stored"), 16)

            def stack_head(h):
                def step(n):
                    for which in range(2):
                        stack(n, which, h)
                return step

            run(sp, sp.Fori, {
                "load_x": load_x, "load_v": load_v, "load_ffn": load_ffn, "cheb_res": store_res,
                "store_v": store_v, "store_out": store_out, "edge_store": store_x3,
                "stack0": stack_head(0), "stack1": stack_head(1), "stack2": stack_head(2), "stack3": stack_head(3),
            }, None)
            for name in ["x3_stored", "res_stored", "v_stored", "out_stored"]:
                sp.wait_ge(sem(name), 16 * B)

        @block.gpsimd
        def _(pool):
            def gat_low(n):
                ready_alone(pool, "gat_small", n, 4, 4)
                wait_alone(pool, sem("gat_exp"), n * NT, sem("waits_passed"))
                for t in range(NT):
                    nc.gpsimd.tensor_scalar(gat_V[:, t, :], gat_T[:, t, :], 0.2, gat_small[:, 5, t:t + 1], ALU.mult,
                                            ALU.add).then_inc(sem("gat_low"), 1)

            def ffn_res(n):
                ready(pool, "ffn_xr", n, 16, 16)
                nc.gpsimd.tensor_tensor(xrE[:], xrE[:], row4("bo"), ALU.add).then_inc(sem("ffn_res"), 1)

            def n2_affine(n):
                affine(pool, "n2", n, y2, "g2", "be2")

            def ffn_b2(n):
                ready(pool, "ffn_turned", n)
                nc.gpsimd.tensor_tensor(y2[:], y2[:], row4("b2"), ALU.add).then_inc(sem("ffn_x2b"), 1)

            def att(n, j):
                j -= 1
                if not 0 <= j < TILES:
                    return
                ready_alone(pool, "att_rv", n, j + 1, TILES)
                e = att_E[:, j % RING_E, :]
                nc.gpsimd.tensor_scalar(e, e, att_small[:, 2, j:j + 1], 1.0, ALU.mult, ALU.mult
                                        ).then_inc(sem("att_norm"), 1)

            run(pool, pool.Fori, {
                "gat_low": gat_low, "ffn_res": ffn_res, "n2_affine": n2_affine, "ffn_b2": ffn_b2,
                "gat_rstd": lambda n: ln_rstd(pool, "gat", n), "edge_rstd": lambda n: ln_scale_bias(pool, "edge", n),
                "cheb_rstd": lambda n: ln_scale_bias(pool, "cheb", n), "n1_rstd": lambda n: ln_rstd(pool, "n1", n),
                "n2_rstd": lambda n: ln_rstd(pool, "n2", n), "n3_rstd": lambda n: ln_rstd(pool, "n3", n),
                "n1_affine": lambda n: affine(pool, "n1", n, y1, "g1", "be1"),
                "n3_affine": lambda n: affine(pool, "n3", n, y3, "g3", "be3"),
            }, att)

        @block.scalar
        def _(act):
            def copy(n, dst, src, made, done, last_reader=None, func=ACT.Copy, **kw):
                ready(act, made, n)
                if last_reader:
                    freed(act, last_reader, n)
                nc.scalar.activation(dst, src, func, **kw).then_inc(sem(done), 1)

            def gat_exp(n):
                for t in range(NT):
                    ready(act, "gat_max", n, t + 1, NT)
                    nc.scalar.activation(gat_E[:, t, :], gat_V[:, t, :], ACT.Exp, bias=gat_small[:, 4, t:t + 1],
                                         accum_out=gat_small[:, 6, t:t + 1]).then_inc(sem("gat_exp"), 1)

            def gat_eT(n, t0):
                freed(act, "gat_pv", n)
                for t in (t0, t0 + 1):
                    ready(act, "gat_eturn", n, t + 1, NT)
                    nc.scalar.copy(gat_ET[:, :, cols(t)], [a0, a1][t % 2][:].rearrange("p (s q) -> p s q", q=P)
                                   ).then_inc(sem("gat_eT"), 1)

            def cheb_hi(n):
                ready(act, "cheb_h", n, NT, NT)
                freed(act, "cheb_prop", n)
                nc.scalar.copy(h_hi[:], h3[:]).then_inc(sem("cheb_hhi"), 1)

            def ffn_gelu(n):
                freed(act, "ffn_downed", n)
                for q in range(2):
                    ready(act, "ffn_up", n, q + 1, 2)
                    nc.scalar.activation(mT[:, q, :], [b0, b1][q][:], ACT.Gelu, bias=k.b1c[:, q:q + 1]
                                         ).then_inc(sem("ffn_gelu"), 1)

            def edge_exp(n):
                ready(act, "edge_le", n, ET, ET)
                nc.scalar.activation(edge_small[:, 2, :], edge_small[:, 1, :], ACT.Exp).then_inc(sem("edge_exp"), 1)

            def att(n, j):
                if j < TILES:
                    ready(act, "att_T", n, j + 1, TILES)
                    need(act, sem("att_turn"), n * TILES + j + 1 - RING_E)
                    nc.scalar.activation(att_E[:, j % RING_E, :], att_T[:, j % RING_T, :], ACT.Exp, scale=-1.0,
                                         bias=att_small[:, 0, j:j + 1], accum_out=att_small[:, 1, j:j + 1]
                                         ).then_inc(sem("att_exp"), 1)
                i = j - 2
                if 0 <= i < TILES:
                    ready(act, "att_turn", n, i + 1, TILES)
                    if i == 0:
                        freed(act, "att_pv", n)
                    nc.scalar.copy(att_PT[:, i // NT, :, cols(i % NT)], c2[:].rearrange("p (s q) -> p s q", q=P)
                                   ).then_inc(sem("att_pt"), 1)
                if j == TILES + 2:
                    copy(n, oT[:], c2[:], "att_pv", "att_oT", "ffn_wo")

            run(act, act.Fori, {
                "gat_hT": lambda n: copy(n, hTA[:], a0[:], "gat_turned", "gat_hT", "gat_s2", ACT.Relu),
                "gat_wh_out": lambda n: copy(n, flat(WhA), a1[:], "gat_wh", "gat_whs", "gat_pv"),
                "gat_exp": gat_exp, "gat_eT0": lambda n: gat_eT(n, 0), "gat_eT2": lambda n: gat_eT(n, 2),
                "edge_hg": lambda n: copy(n, hg[:], b0[:], "edge_gathered", "edge_hg", "edge_outed"),
                "edge_xz": lambda n: copy(n, xz[:], b1[:, 0:E], "edge_x", "edge_xz", "edge_lcol"),
                "edge_exp": edge_exp,
                "edge_yT": lambda n: copy(n, YT[:], b0[:], "edge_scattered", "edge_yT", "edge_outed"),
                "edge_apply": lambda n: (freed(act, "edge_gathered", n), ln_relu(act, "edge", n, x2, h2)),
                "cheb_apply": lambda n: (freed(act, "cheb_x1", n), freed(act, "cheb_hlo", n),
                                         ln_relu(act, "cheb", n, x3, h3)),
                "cheb_hi": cheb_hi,
                "cheb_xpT": lambda n: copy(n, xpT[:], c3[:], "cheb_prop", "cheb_xpT", "cheb_v"),
                "cheb_x1T": lambda n: copy(n, x1T[:], c3[:], "x1_turned", "cheb_x1T", "cheb_v"),
                "cheb_qsplit": lambda n: (need(act, sem("parts3"), n * 128),
                                          copy(n, qk_hi[0][:], c3[:], "cheb_q", "q_hi")),
                "cheb_ksplit": lambda n: copy(n, qk_hi[1][:], c3[:], "cheb_k", "k_hi"),
                "cheb_vout": lambda n: (freed(act, "v_stored", n, 16), copy(n, flat(vS), c3[:], "cheb_v", "v_out")),
                "ffn_x2T": lambda n: copy(n, x2T, b0[:], "ffn_turned", "ffn_x2T", "ffn_downed"),
                "ffn_gelu": ffn_gelu,
            }, att)

        @block.vector
        def _(dve):
            def gat_stats(n):
                ready(dve, "gat_loaded", n, 16, 16)
                ln_stats(dve, "gat", n, xA)

            def gat_apply(n):
                freed(dve, "gat_turned", n)
                ln_apply(dve, "gat", n, xA, zA)

            def gat_wh_out(n):
                ready(dve, "gat_s1", n)
                nc.vector.tensor_copy(gat_small[:, 0, :], a0[:, 0:NT]).then_inc(sem("gat_s1s"), 1)

            def gat_scores(n):
                freed(dve, "gat_eturn", n, NT)
                ready_alone(dve, "gat_s2", n)
                for t in range(NT):
                    nc.vector.tensor_tensor_reduce(gat_T[:, t, :], a1[:], k.mask_gat[:, t, :], 1.0, -HUGE, ALU.add,
                                                   ALU.max, gat_small[:, 1, t:t + 1]).then_inc(sem("gat_T"), 1)
                s = gat_small
                ready(dve, "gat_T", n, NT, NT)
                ready(dve, "gat_s1s", n)
                nc.vector.tensor_tensor(s[:, 2, :], s[:, 0, :], s[:, 1, :], ALU.add).then_inc(sem("gat_small"), 1)
                ready(dve, "gat_small", n, 1, 4)
                nc.vector.scalar_tensor_tensor(s[:, 3, :], s[:, 2, :], 0.2, s[:, 2, :], ALU.mult, ALU.max
                                               ).then_inc(sem("gat_small"), 1)
                ready(dve, "gat_small", n, 2, 4)
                nc.vector.tensor_tensor(s[:, 4, :], s[:, 0, :], s[:, 3, :], ALU.subtract
                                        ).then_inc(sem("gat_small"), 1)
                nc.vector.tensor_scalar(s[:, 5, :], s[:, 0, :], -0.8, None, ALU.mult).then_inc(sem("gat_small"), 1)

            def gat_max(n):
                for t in range(NT):
                    ready(dve, "gat_low", n, t + 1, NT)
                    nc.vector.tensor_tensor(gat_V[:, t, :], gat_T[:, t, :], gat_V[:, t, :], ALU.max
                                            ).then_inc(sem("gat_max"), 1)

            def gat_x2(n):
                ready(dve, "gat_exp", n, NT, NT)
                nc.vector.reciprocal(gat_small[:, 7, :], gat_small[:, 6, :]).then_inc(sem("gat_rinv"), 1)
                ready(dve, "gat_rinv", n)
                ready(dve, "gat_pv", n)
                freed(dve, "edge_done", n)
                for t in range(NT):
                    nc.vector.scalar_tensor_tensor(x2[:, t, :], a0[:, cols(t)], gat_small[:, 7, t:t + 1],
                                                   xA[:, t, :], ALU.mult, ALU.add).then_inc(sem("gat_done"), 1)

            def edge_stats(n):
                ready(dve, "gat_done", n, NT, NT)
                freed(dve, "edge_bias", n)
                ln_stats(dve, "edge", n, x2)

            def edge_z(n):
                ready(dve, "edge_xz", n)
                nc.vector.scalar_tensor_tensor(zT[:], xz[:], 0.2, xz[:], ALU.mult, ALU.max
                                               ).then_inc(sem("edge_z"), 1)

            def edge_max(n):
                for h in range(H):
                    if h % 2 == 0:
                        ready_alone(dve, "edge_lb", n, h // 2 + 1, 2)
                    for e in range(ET):
                        nc.vector.tensor_tensor_reduce(
                            edge_junk[:, e * H + h, :], [b0, b1][h // 2][:, (h % 2) * E:(h % 2) * E + E],
                            k.seg_bias[:, e, :], 1.0, -HUGE, ALU.add, ALU.max,
                            edge_small[:, 0, e * H + h:e * H + h + 1]).then_inc(sem("edge_max"), 1)

            def edge_le(n):
                ready(dve, "edge_max", n, ET * H, ET * H)
                ready(dve, "edge_lcol", n)
                for e in range(ET):
                    r = slice(e * H, e * H + H)
                    nc.vector.scalar_tensor_tensor(edge_small[:, 1, r], b0[:, r], k.logA[:, e:e + 1],
                                                   edge_small[:, 0, r], ALU.add, ALU.subtract
                                                   ).then_inc(sem("edge_le"), 1)

            def edge_u(n):
                ready(dve, "edge_den", n)
                nc.vector.reciprocal(edge_small[:, 3, :], b0[:, 0:ET * H]).then_inc(sem("edge_rden"), 1)
                ready(dve, "edge_rden", n)
                nc.vector.tensor_tensor(edge_small[:, 4, :], edge_small[:, 2, :], edge_small[:, 3, :], ALU.mult
                                        ).then_inc(sem("edge_attn"), 1)
                ready(dve, "edge_attn", n)
                ready(dve, "edge_v", n)
                freed(dve, "edge_scattered", n)
                nc.vector.tensor_tensor(U[:].rearrange("p (g d) -> p g d", d=HD),
                                        b1[:, 0:ET * D].rearrange("p (g d) -> p g d", d=HD),
                                        edge_small[:, 4, :].unsqueeze(2).broadcast_to([P, ET * H, HD]), ALU.mult
                                        ).then_inc(sem("edge_u"), 1)

            def edge_x3(n):
                ready(dve, "edge_outed", n)
                freed(dve, "x3_stored", n, 16)
                freed(dve, "cheb_h", n, NT)
                nc.vector.tensor_tensor(flat(x3), b1[:], flat(x2), ALU.add).then_inc(sem("edge_done"), 1)

            def cheb_stats(n):
                ready(dve, "edge_done", n)
                freed(dve, "cheb_bias", n)
                ln_stats(dve, "cheb", n, x3)

            def cheb_lo(n):
                ready(dve, "cheb_hhi", n)
                freed(dve, "cheb_prop", n)
                nc.vector.tensor_tensor(h_lo[:], h3[:], h_hi[:].bitcast(F32), ALU.subtract
                                        ).then_inc(sem("cheb_hlo"), 1)

            def cheb_y(n):
                ready(dve, "cheb_g", n)
                nc.vector.tensor_tensor(y1[:], c3[:].rearrange("p (t d) -> p t d", d=D), row4("bc"), ALU.add
                                        ).then_inc(sem("cheb_y"), 1)
                ready(dve, "cheb_y", n)
                ln_stats(dve, "n1", n, y1)

            def n1_apply(n):
                ln_apply(dve, "n1", n, y1, y1)

            def cheb_x1(n):
                ready(dve, "n1_aff", n, 2, 2)
                freed(dve, "x1_turned", n)
                freed(dve, "res_stored", n, 16)
                nc.vector.scalar_tensor_tensor(flat(x1), flat(y1), 0.0, flat(h3), ALU.max, ALU.add
                                               ).then_inc(sem("cheb_x1"), 1)

            def split_lo(n, which):
                name = "qk"[which]
                ready(dve, name + "_hi", n)
                need(dve, sem("parts3"), n * 128)
                nc.vector.tensor_tensor(qk_lo[which][:], c3[:], qk_hi[which][:].bitcast(F32), ALU.subtract
                                        ).then_inc(sem(name + "_lo"), 1)

            def att(n, j):
                if j < TILES:
                    need(dve, sem("att_exp"), n * TILES + j + 1 - RING_T)
                    ready_alone(dve, "att_score", n, j + 1, TILES)
                    nc.vector.tensor_tensor_reduce(att_T[:, j % RING_T, :], [c0, c1][j % 2][:],
                                                   k.mask_att[:, j % NT, :], -QK_SCALE, HUGE, ALU.add, ALU.min,
                                                   att_small[:, 0, j:j + 1]).then_inc(sem("att_T"), 1)
                if 1 <= j <= TILES:
                    ready(dve, "att_exp", n, j, TILES)
                    nc.vector.reciprocal(att_small[:, 2, j - 1:j], att_small[:, 1, j - 1:j]
                                         ).then_inc(sem("att_rv"), 1)

            def ffn_y2(n):
                ready(dve, "ffn_wo", n)
                ready(dve, "ffn_res", n)
                nc.vector.tensor_tensor(flat(y2), b1[:], flat(xrE), ALU.add).then_inc(sem("ffn_y2"), 1)
                ready(dve, "ffn_y2", n)
                ln_stats(dve, "n2", n, y2)

            def n2_apply(n):
                ln_apply(dve, "n2", n, y2, y2)

            def ffn_y3(n):
                ready(dve, "ffn_downed", n)
                ready(dve, "ffn_x2b", n)
                freed(dve, "out_stored", n, 16)
                nc.vector.tensor_tensor(flat(y3), b0[:], flat(y2), ALU.add).then_inc(sem("ffn_y3"), 1)
                ready(dve, "ffn_y3", n)
                ln_stats(dve, "n3", n, y3)

            def n3_apply(n):
                ln_apply(dve, "n3", n, y3, y3)

            def ffn_final(n):
                ready(dve, "n3_aff", n, 2, 2)
                ready(dve, "ffn_x3", n, 16, 16)
                nc.vector.tensor_tensor(flat(y3), flat(y3), flat(x3E), ALU.add).then_inc(sem("ffn_fin"), 1)

            run(dve, dve.Fori, {
                "gat_stats": gat_stats, "gat_apply": gat_apply, "gat_s1_out": gat_wh_out, "gat_scores": gat_scores,
                "gat_max": gat_max, "gat_x2": gat_x2,
                "edge_stats": edge_stats, "edge_z": edge_z, "edge_max": edge_max,
                "edge_le": edge_le, "edge_u": edge_u, "edge_x3": edge_x3,
                "cheb_stats": cheb_stats, "cheb_lo": cheb_lo, "cheb_y": cheb_y,
                "n1_apply": n1_apply, "cheb_x1": cheb_x1,
                "cheb_qlow": lambda n: split_lo(n, 0), "cheb_klow": lambda n: split_lo(n, 1),
                "ffn_y2": ffn_y2, "n2_apply": n2_apply, "ffn_y3": ffn_y3, "n3_apply": n3_apply,
                "ffn_final": ffn_final,
            }, att)

        @block.tensor
        def _(pe):
            def turn(dst, src):
                for t in range(NT):
                    mm = nc.tensor.transpose(dst[:, cols(t)], src[:, t, :], k.ident[:])
                return mm

            def by_nodes(dst, left, right):
                for t in range(NT):
                    mm = nc.tensor.matmul(dst[:, cols(t)], left[:, cols(t)], right, start=True, stop=True)
                return mm

            def one(dst, left, right):
                return nc.tensor.matmul(dst, left, right, start=True, stop=True)

            def gat_turn(n):
                ready(pe, "gat_normed", n, NT, NT)
                freed(pe, "gat_done", n, NT)
                turn(a0, zA).then_inc(sem("gat_turned"), 1)

            def gat_wh(n):
                ready(pe, "gat_hT", n)
                freed(pe, "gat_eT", n, NT)
                by_nodes(a1, hTA, W["W1g"][:]).then_inc(sem("gat_wh"), 1)
                for t in range(NT):
                    mm = one(a0[:, t:t + 1], hTA[:, cols(t)], k.gat_a[:, 0:1])
                mm.then_inc(sem("gat_s1"), 1)

            def gat_s2(n):
                ready(pe, "gat_whs", n)
                one(a1[:], k.gat_a2b[:], hTA[:]).then_inc(sem("gat_s2"), 1)

            def gat_eturn(n, t0):
                for t in (t0, t0 + 1):
                    ready(pe, "gat_exp", n, t + 1, NT)
                    if t == 0:
                        ready(pe, "gat_s1s", n)
                    elif t == 1:
                        ready(pe, "gat_T", n, NT, NT)
                    else:
                        ready(pe, "gat_eT", n, t - 1, NT)
                    for s in range(NT):
                        mm = nc.tensor.transpose([a0, a1][t % 2][:, cols(s)], gat_E[:, t, cols(s)], k.ident[:])
                    mm.then_inc(sem("gat_eturn"), 1)

            def gat_pv(n):
                ready(pe, "gat_eT", n, NT, NT)
                for t in range(NT):
                    for s in range(NT):
                        mm = nc.tensor.matmul(a0[:, cols(t)], gat_ET[:, s, cols(t)], WhA[:, s, :], start=(s == 0),
                                              stop=(s == NT - 1))
                mm.then_inc(sem("gat_pv"), 1)

            def edge_gather(n):
                ready(pe, "edge_h", n, NT, NT)
                need(pe, sem("ffn_y3"), min(n - 2, B) if isinstance(n, int) else n - 2)
                freed(pe, "edge_yT", n)
                for t in range(NT):
                    mm = nc.tensor.matmul(b0[:], h2[:, t, :], k.edge_pick[:, t, :], start=(t == 0),
                                          stop=(t == NT - 1))
                mm.then_inc(sem("edge_gathered"), 1)

            def edge_x(n):
                ready(pe, "edge_hg", n)
                freed(pe, "edge_done", n)
                one(b1[:, 0:E], W["WlinT"][:], hg[:, 0:E]).then_inc(sem("edge_x"), 1)

            def edge_lb(n):
                ready(pe, "edge_z", n)
                for h in range(H):
                    mm = one([b0, b1][h // 2][:, (h % 2) * E:(h % 2) * E + E], k.head_a[:, h, :], zT[:])
                    if h % 2:
                        mm.then_inc(sem("edge_lb"), 1)

            def edge_lcol(n):
                ready(pe, "edge_max", n, ET * H, ET * H)
                for e in range(ET):
                    mm = one(b0[:, e * H:e * H + H], zT[:, cols(e)], k.head_a4[:])
                mm.then_inc(sem("edge_lcol"), 1)
                for e in range(ET):
                    mm = one(b1[:, cols(e)], hg[:, E + e * P:E + (e + 1) * P], W["WvalT"][:])
                mm.then_inc(sem("edge_v"), 1)

            def edge_den(n):
                ready(pe, "edge_exp", n)
                for e in range(ET):
                    for f in range(ET):
                        mm = nc.tensor.matmul(b0[:, e * H:e * H + H], k.same_src[:, f, cols(e)],
                                              edge_small[:, 2, f * H:f * H + H], start=(f == 0), stop=(f == ET - 1))
                mm.then_inc(sem("edge_den"), 1)

            def edge_scatter(n):
                ready(pe, "edge_u", n)
                for e in range(ET):
                    mm = nc.tensor.matmul(b0[:], U[:, cols(e)], k.src_rows[:, e, :], start=(e == 0),
                                          stop=(e == ET - 1))
                mm.then_inc(sem("edge_scattered"), 1)

            def edge_out(n):
                ready(pe, "edge_yT", n)
                by_nodes(b1, YT, W["WoutT"][:]).then_inc(sem("edge_outed"), 1)

            def cheb_prop(n):
                ready(pe, "cheb_hlo", n)
                freed(pe, "v_out", n)
                for s in range(NT):
                    for i, (left, right) in enumerate([(h_hi, k.lap_hi), (h_hi, k.lap_lo), (h_lo, k.lap_hi)]):
                        mm = nc.tensor.matmul(c3[:], left[:, s, :], right[:, s, :], start=(s == 0 and i == 0),
                                              stop=(s == NT - 1 and i == 2))
                mm.then_inc(sem("cheb_prop"), 1)

            def cheb_g(n):
                ready(pe, "cheb_xpT", n)
                by_nodes(c3, xpT, W["Wc"][:]).then_inc(sem("cheb_g"), 1)

            def cheb_x1turn(n):
                ready(pe, "cheb_x1", n)
                turn(c3, x1).then_inc(sem("x1_turned"), 1)

            def cheb_q(n):
                ready(pe, "cheb_x1T", n)
                one(c3[:], W["Wq"][:], x1T[:]).then_inc(sem("cheb_q"), 1)

            def cheb_k(n):
                ready(pe, "q_lo", n)
                one(c3[:], W["Wk"][:], x1T[:]).then_inc(sem("cheb_k"), 1)

            def cheb_v(n):
                ready(pe, "k_lo", n)
                by_nodes(c3, x1T, W["Wv"][:]).then_inc(sem("cheb_v"), 1)

            def att(n, j):
                if j < TILES:
                    h, t = j // NT, j % NT
                    if t == 0:
                        ready(pe, f"parts{h}", n, 128, 128)
                    need(pe, sem("att_T"), n * TILES + j - 1)
                    one([c0, c1][j % 2][:], Qs[:, h, cols(t)], Ks[:, h, :]).then_inc(sem("att_score"), 1)
                i = j - 2
                if 0 <= i < TILES:
                    if i == 0:
                        freed(pe, "att_oT", n)
                    ready(pe, "att_norm", n, i + 1, TILES)
                    need(pe, sem("att_pt"), n * TILES + i)
                    for s in range(NT):
                        mm = nc.tensor.transpose(c2[:, cols(s)], att_E[:, i % RING_E, cols(s)], k.ident[:])
                    mm.then_inc(sem("att_turn"), 1)
                if j == TILES + 2:
                    ready(pe, "att_pt", n, TILES, TILES)
                    ready(pe, "att_v", n, 16, 16)
                    for s in range(NT):
                        for h in range(H):
                            r = slice(HD * h, HD * (h + 1))
                            mm = nc.tensor.matmul(c2[r, :], vD[:, s, r], att_PT[:, h, s, :], start=(s == 0),
                                                  stop=(s == NT - 1))
                    mm.then_inc(sem("att_pv"), 1)

            def ffn_wo(n):
                ready(pe, "att_oT", n)
                need(pe, sem("edge_done"), min(n + 3, B) if isinstance(n, int) else n + 3)
                by_nodes(b1, oT, W["Wo"][:]).then_inc(sem("ffn_wo"), 1)

            def ffn_turn(n):
                ready(pe, "n2_aff", n, 2, 2)
                turn(b0, y2).then_inc(sem("ffn_turned"), 1)

            def ffn_up(n):
                ready(pe, "ffn_x2T", n)
                for q in range(2):
                    one([b0, b1][q][:], k.W1[:, cols(q)], x2T).then_inc(sem("ffn_up"), 1)

            def ffn_down(n):
                ready(pe, "ffn_gelu", n, 2, 2)
                for t in range(NT):
                    for q in range(2):
                        mm = nc.tensor.matmul(b0[:, cols(t)], mT[:, q, cols(t)], k.W2[:, q, :], start=(q == 0),
                                              stop=(q == 1))
                mm.then_inc(sem("ffn_downed"), 1)

            run(pe, pe.Fori, {
                "gat_turn": gat_turn, "gat_wh": gat_wh, "gat_s2": gat_s2, "gat_eturn0": lambda n: gat_eturn(n, 0),
                "gat_eturn2": lambda n: gat_eturn(n, 2), "gat_pv": gat_pv,
                "edge_gather": edge_gather, "edge_x": edge_x, "edge_lb": edge_lb, "edge_lcol": edge_lcol,
                "edge_den": edge_den, "edge_scatter": edge_scatter, "edge_out": edge_out,
                "cheb_g": cheb_g, "cheb_prop": cheb_prop, "cheb_x1turn": cheb_x1turn,
                "cheb_q": cheb_q, "cheb_k": cheb_k, "cheb_v": cheb_v,
                "ffn_wo": ffn_wo, "ffn_turn": ffn_turn, "ffn_up": ffn_up, "ffn_down": ffn_down,
            }, att)


_INS = {"x": "x", "adj": "adj", "alpha": "L0_gnn_alpha_train", "w": "L0_gnn_w", "d": "L0_gnn_d",
        "fcw": "L0_gnn_fc_in_w", "fcb": "L0_gnn_fc_in_b", "W1g": "L1_gnn_W", "ag": "L1_gnn_a",
        "Wlin": "L2_gnn_W_lin", "Wval": "L2_gnn_W_val", "aL2": "L2_gnn_a", "Wout": "L2_gnn_W_out",
        "src": "L2_gnn_src", "dst": "L2_gnn_dst"} | {n: "L3_gnn_" + n for n in NAMES[15:]}


def kernel(**inputs):
    import numpy as np
    import concourse.bacc as bacc
    from concourse.bass_utils import run_bass_kernel_spmd as run

    nc = bacc.Bacc("TRN2", target_bir_lowering=False, num_devices=1)
    arrays, t_in = {}, {}
    for name in NAMES:
        a = np.ascontiguousarray(inputs[_INS[name]])
        arrays["in_" + name] = a
        t_in[name] = nc.dram_tensor("in_" + name, a.shape, mybir.dt.from_np(a.dtype), kind="ExternalInput").ap()
    out = nc.dram_tensor("out_x", (B, N, D), F32, kind="ExternalOutput").ap()
    build(nc, t_in, out)
    r = run(nc, [arrays], core_ids=[0])
    return r.results[0]["out_x"]
```
